# Optimizing a Trainium2 kernel written in Bass

```python
import numpy as np
import jax
import jax.numpy as jnp

def _softmax(x, axis=-1):
    return jax.nn.softmax(x, axis=axis)

def _gelu(x):
    return jax.nn.gelu(x, approximate=True)

def _silu(x):
    return jax.nn.silu(x)

def _sigmoid(x):
    return jax.nn.sigmoid(x)

def _layernorm(x, axis=-1, eps=1e-05):
    m = jnp.mean(x, axis=axis, keepdims=True)
    v = jnp.var(x, axis=axis, keepdims=True)
    return (x - m) / jnp.sqrt(v + eps)

def _scatter_add(tgt, idx, src, axis=0):
    return tgt.at[idx].add(src)

def _segment_sum(src, seg, n):
    return jax.ops.segment_sum(src, seg, n)
kernel_name = 'mk_gnn_preln_d2_gnn_r64_fd795a'

def setup_inputs(seed: int=0):
    np.random.seed(seed)
    _w = jnp.asarray

    def _rec_inputs():
        import jax
        import jax.numpy as jnp
        _gk = jax.random.key(seed)
        x = -0.000202 + 1 * jax.random.normal(jax.random.fold_in(_gk, 1), (50000, 64), jnp.float32)
        src = jax.random.randint(jax.random.fold_in(_gk, 2), (25000,), 0, 50000, jnp.int32)
        dst = jnp.minimum((50000 * jax.random.uniform(jax.random.fold_in(_gk, 3), (25000,)) ** 2.0).astype(jnp.int32), 49999)
        _o = jnp.argsort(dst, stable=True)
        src = src[_o]
        dst = dst[_o]
        edge_attr_64 = -8.16379e-05 + 0.999858 * jax.random.normal(jax.random.fold_in(_gk, 12), (25000, 64), jnp.float32)
        return (x, src, dst, edge_attr_64)
    x, src, dst, edge_attr_64 = _rec_inputs()

    def _L0_gnn_setup():
        import jax, jax.numpy as jnp
        import numpy as np
        BN_EPS = 1e-05

        def _batchnorm(x, gamma, beta):
            m = jnp.mean(x, axis=0)
            v = jnp.var(x, axis=0)
            return (x - m) * jax.lax.rsqrt(v + BN_EPS) * gamma + beta
        N, E, D = (100000, 25000, 64)
        key = jax.random.key(seed)
        ks = jax.random.split(key, 6)
        return {'node_feats': jax.random.normal(ks[0], (N, D), dtype=jnp.float32), 'edge_feats': jax.random.normal(ks[1], (E, D), dtype=jnp.float32), 'src': jax.random.randint(ks[2], (E,), 0, N, dtype=jnp.int32), 'dst': jax.random.randint(ks[3], (E,), 0, N, dtype=jnp.int32), 'eps': jnp.zeros((1,), dtype=jnp.float32), 'W1': jax.random.normal(ks[4], (D, 2 * D), dtype=jnp.float32) * (1.0 / np.sqrt(D)), 'b1': jnp.zeros((2 * D,), dtype=jnp.float32), 'gamma1': jnp.ones((2 * D,), dtype=jnp.float32), 'beta1': jnp.zeros((2 * D,), dtype=jnp.float32), 'W2': jax.random.normal(ks[5], (2 * D, D), dtype=jnp.float32) * (1.0 / np.sqrt(2 * D)), 'b2': jnp.zeros((D,), dtype=jnp.float32), 'gamma2': jnp.ones((D,), dtype=jnp.float32), 'beta2': jnp.zeros((D,), dtype=jnp.float32)}
    _L0_gnn_all = _L0_gnn_setup()
    _L0_gnn_in = {k: v for k, v in _L0_gnn_all.items() if k in ('eps', 'W1', 'b1', 'gamma1', 'beta1', 'W2', 'b2', 'gamma2', 'beta2')}
    del _L0_gnn_all

    def _L1_gnn_setup():
        import jax, jax.numpy as jnp
        import numpy as np
        N_NODES = 50000
        N_EDGES = 12500
        D_IN = 64
        D_OUT = 64
        N_LAYERS = 3

        def _seg_mean(vals, idx, n):
            s = jax.ops.segment_sum(vals, idx, num_segments=n)
            c = jax.ops.segment_sum(jnp.ones((vals.shape[0], 1), vals.dtype), idx, num_segments=n)
            return s / jnp.clip(c, 1.0)
        key = jax.random.key(seed)
        ks = jax.random.split(key, 8)
        x = jax.random.normal(ks[0], (N_NODES, D_IN), dtype=jnp.float32)
        edge_index = jax.random.randint(ks[1], (2, N_EDGES), 0, N_NODES, dtype=jnp.int64)
        s = 1.0 / np.sqrt(D_IN)
        lin1_w = jax.random.uniform(ks[2], (N_LAYERS, D_OUT, D_IN), jnp.float32, -s, s)
        lin2_w = jax.random.uniform(ks[3], (N_LAYERS, D_OUT, D_IN), jnp.float32, -s, s)
        root_w = jax.random.uniform(ks[4], (N_LAYERS, D_OUT, D_IN), jnp.float32, -s, s)
        root_b = jax.random.uniform(ks[5], (N_LAYERS, D_OUT), jnp.float32, -s, s)
        d_cat = D_IN + N_LAYERS * D_OUT
        sf = 1.0 / np.sqrt(d_cat)
        final_w = jax.random.uniform(ks[6], (D_OUT, d_cat), jnp.float32, -sf, sf)
        final_b = jax.random.uniform(ks[7], (D_OUT,), jnp.float32, -sf, sf)
        return {'x': x, 'edge_index': edge_index, 'lin1_w': lin1_w, 'lin2_w': lin2_w, 'root_w': root_w, 'root_b': root_b, 'final_w': final_w, 'final_b': final_b}
    _L1_gnn_all = _L1_gnn_setup()
    _L1_gnn_in = {k: v for k, v in _L1_gnn_all.items() if k in ('lin1_w', 'lin2_w', 'root_w', 'root_b', 'final_w', 'final_b')}
    del _L1_gnn_all
    return {'x': x, 'src': src, 'dst': dst, 'edge_attr_64': edge_attr_64, 'L0_gnn_eps': _L0_gnn_in['eps'], 'L0_gnn_W1': _L0_gnn_in['W1'], 'L0_gnn_b1': _L0_gnn_in['b1'], 'L0_gnn_gamma1': _L0_gnn_in['gamma1'], 'L0_gnn_beta1': _L0_gnn_in['beta1'], 'L0_gnn_W2': _L0_gnn_in['W2'], 'L0_gnn_b2': _L0_gnn_in['b2'], 'L0_gnn_gamma2': _L0_gnn_in['gamma2'], 'L0_gnn_beta2': _L0_gnn_in['beta2'], 'L1_gnn_lin1_w': _L1_gnn_in['lin1_w'], 'L1_gnn_lin2_w': _L1_gnn_in['lin2_w'], 'L1_gnn_root_w': _L1_gnn_in['root_w'], 'L1_gnn_root_b': _L1_gnn_in['root_b'], 'L1_gnn_final_w': _L1_gnn_in['final_w'], 'L1_gnn_final_b': _L1_gnn_in['final_b']}

def reference(x, src, dst, edge_attr_64, L0_gnn_eps, L0_gnn_W1, L0_gnn_b1, L0_gnn_gamma1, L0_gnn_beta1, L0_gnn_W2, L0_gnn_b2, L0_gnn_gamma2, L0_gnn_beta2, L1_gnn_lin1_w, L1_gnn_lin2_w, L1_gnn_root_w, L1_gnn_root_b, L1_gnn_final_w, L1_gnn_final_b):
    import jax
    import jax.numpy as jnp

    def _L0_gnn_ref(node_feats, edge_feats, src, dst, eps, W1, b1, gamma1, beta1, W2, b2, gamma2, beta2):
        import jax, jax.numpy as jnp
        import numpy as np
        BN_EPS = 1e-05

        def _batchnorm(x, gamma, beta):
            m = jnp.mean(x, axis=0)
            v = jnp.var(x, axis=0)
            return (x - m) * jax.lax.rsqrt(v + BN_EPS) * gamma + beta
        N = node_feats.shape[0]
        msg = node_feats[src] + edge_feats
        agg_sum = jax.ops.segment_sum(msg, dst, num_segments=N)
        deg = jax.ops.segment_sum(jnp.ones((src.shape[0],), dtype=node_feats.dtype), dst, num_segments=N)
        agg_mean = agg_sum / jnp.maximum(deg, 1.0)[:, None]
        h = (1.0 + eps[0]) * node_feats + agg_mean
        h = jax.nn.relu(_batchnorm(h @ W1 + b1, gamma1, beta1))
        h = jax.nn.relu(_batchnorm(h @ W2 + b2, gamma2, beta2))
        return h

    def _L1_gnn_ref(x, edge_index, lin1_w, lin2_w, root_w, root_b, final_w, final_b):
        import jax, jax.numpy as jnp
        import numpy as np
        N_NODES = 50000
        N_EDGES = 12500
        D_IN = 64
        D_OUT = 64
        N_LAYERS = 3

        def _seg_mean(vals, idx, n):
            s = jax.ops.segment_sum(vals, idx, num_segments=n)
            c = jax.ops.segment_sum(jnp.ones((vals.shape[0], 1), vals.dtype), idx, num_segments=n)
            return s / jnp.clip(c, 1.0)
        src, dst = (edge_index[0], edge_index[1])
        n = x.shape[0]
        xs = [x]
        h = x
        for l in range(N_LAYERS):
            m1 = (h @ lin1_w[l].T)[src]
            out1 = _seg_mean(m1, dst, n)
            m2 = (h @ lin2_w[l].T)[dst]
            out2 = _seg_mean(m2, src, n)
            h = jax.nn.relu(h @ root_w[l].T + root_b[l] + out1 + out2)
            xs.append(h)
        cat = jnp.concatenate(xs, axis=-1)
        return cat @ final_w.T + final_b
    edge_index = jnp.stack([src, dst])
    h = jnp.maximum(_layernorm(x, axis=-1), 0.0)
    x = x + _L0_gnn_ref(h, edge_attr_64, src, dst, L0_gnn_eps, L0_gnn_W1, L0_gnn_b1, L0_gnn_gamma1, L0_gnn_beta1, L0_gnn_W2, L0_gnn_b2, L0_gnn_gamma2, L0_gnn_beta2)
    h = jnp.maximum(_layernorm(x, axis=-1), 0.0)
    x = x + _L1_gnn_ref(h, edge_index, L1_gnn_lin1_w, L1_gnn_lin2_w, L1_gnn_root_w, L1_gnn_root_b, L1_gnn_final_w, L1_gnn_final_b)
    return x

_drawn_inputs = setup_inputs


def setup_inputs(seed=0):
    import zlib

    import numpy as np

    out = dict(_drawn_inputs(seed))
    spreads = {'L0_gnn_b1': (0.0, 0.1),
     'L0_gnn_gamma1': (1.0, 0.2),
     'L0_gnn_beta1': (0.0, 0.1),
     'L0_gnn_b2': (0.0, 0.1),
     'L0_gnn_gamma2': (1.0, 0.2),
     'L0_gnn_beta2': (0.0, 0.1)}
    factors = {}
    for name, (base, spread) in spreads.items():
        noise = np.random.default_rng([zlib.crc32(name.encode()), seed]).standard_normal(out[name].shape)
        drawn = base * np.exp(spread * noise) if base else spread * noise
        out[name] = jnp.asarray(drawn.astype(out[name].dtype))
    for name, factor in factors.items():
        out[name] = (out[name] * factor).astype(out[name].dtype)
    return out
```

```python
from contextlib import ExitStack

import concourse.bass as bass
from concourse import mybir

F32 = mybir.dt.float32
BF16 = mybir.dt.bfloat16
I32 = mybir.dt.int32
ALU = mybir.AluOpType
ACT = mybir.ActivationFunctionType
AX_X = mybir.AxisListType.X

P = 128
D = 64
N = 50000
E = 25000
C = 196
U = 14
J = 8
G = 49
T = G * J
NP = T * P
LAST = (N - (G - 1) * P * J) // J
PAD = NP - 1
LAYERS = 3
EPS = 1e-5


def looped(eng, turns, body):
    body(0, True)
    if turns > 1:
        with eng.Fori(1, turns) as i:
            body(i, False)


def wait_apart(eng, sem, value, passed):
    eng.wait_ge(sem, value)
    eng.sem_inc(passed, 1)


class Chain:

    def __init__(self, eng, sem):
        self.eng, self.sem, self.n = eng, sem, 0

    def add(self, ins):
        self.n += 1
        ins.then_inc(self.sem, 1)
        return self.n

    def link(self, ins):
        self.add(ins)
        self.eng.wait_ge(self.sem, self.n)


class Scope:

    count = 0

    def __init__(self, nc, name):
        Scope.count += 1
        self.nc, self.name, self.ctx = nc, f"{name}{Scope.count}", ExitStack()
        self.sems = []

    def __enter__(self):
        self.ctx.__enter__()
        return self

    def __exit__(self, *a):
        if self.sems:
            self.nc.clear_and_free_semaphores(self.sems)
            self.nc.all_engine_barrier()
        return self.ctx.__exit__(*a)

    def sb(self, name, shape, dt=F32):
        return self.ctx.enter_context(self.nc.sbuf_tensor(f"{self.name}_{name}", shape, dt))

    def ps(self, name, shape, dt=F32):
        return self.ctx.enter_context(self.nc.psum_tensor(f"{self.name}_ps_{name}", shape, dt))

    def sem(self, name):
        self.sems.append(self.nc.alloc_semaphore(name=f"{self.name}_sem_{name}"))
        return self.sems[-1]


def sort_edges(nc, k, src, dst):
    vec, pe = nc.vector, nc.tensor
    with Scope(nc, "sort") as s:
        key = [s.sb(f"key{d}", [P, C], I32) for d in range(2)]
        t_i = s.sb("t_i", [P, 2, C], I32)
        low_i = s.sb("low_i", [P, 2, C], I32)
        lane_i = s.sb("lane_i", [P, 2, C], I32)
        tile = s.sb("tile", [P, 2, C])
        lane = s.sb("lane", [P, 2, C])
        edge_i = s.sb("edge_i", [P, C], I32)
        edge = s.sb("edge", [P, C])
        pay = s.sb("pay", [P, 2, 2, C])
        oh_lane = s.sb("oh_lane", [P, 2, 2, P], BF16)
        oh_tile = s.sb("oh_tile", [P, 2, 2, T], BF16)
        oh_row = s.sb("oh_row", [P, 2, 2, P])
        oh_col = s.sb("oh_col", [P, 2, 2, 2, C])
        zero_b = s.sb("zero_b", [P, T], BF16)
        below = s.sb("below", [P, P], BF16)
        upto = s.sb("upto", [P, P], BF16)
        ones = s.sb("ones", [P, P])
        row0 = s.sb("row0", [P, P])
        row127 = s.sb("row127", [P, P])
        eq = s.sb("eq", [P, 2])
        iota_i = s.sb("iota_i", [P, T], I32)
        iotap_i = s.sb("iotap_i", [P, 1], I32)
        deg = s.sb("deg", [P, 2, T])
        hist = s.sb("hist", [P, 2, T])
        scan = s.sb("scan", [P, 2, 2, T])
        base = s.sb("base", [P, 2, T])
        junk = s.sb("junk", [P, T])
        rank = s.sb("rank", [P, 2, C])
        rank_i = s.sb("rank_i", [P, 2, C], I32)
        row_f = s.sb("row_f", [P, 2, C])
        col_f = s.sb("col_f", [P, 2, C])
        tmp_i = s.sb("tmp_i", [P, 2, C], I32)
        out_i = s.sb("out_i", [P, 2, 2, C], I32)
        code = s.sb("code", [P, 2, C])
        tsort = s.sb("tsort", [P, 2, C])
        code_t = s.sb("code_t", [98, 2, 2, P])
        sel = s.sb("sel", [98, 2, 2, T])
        c0_i = s.sb("c0_i", [P, 2, T], I32)
        c0 = s.sb("c0", [P, 2, T])
        cl_i = s.sb("cl_i", [P, 2, T], I32)
        cl = s.sb("cl", [P, 2, T])
        more = s.sb("more", [P, 2, T])
        ends = s.sb("ends", [P, 2, 2, C])
        cont = s.sb("cont", [P, 2, C])
        ps_acc = [s.ps(f"acc{d}", [P, 512]) for d in range(2)]
        ps_x = [s.ps(f"x{d}", [P, 512]) for d in range(2)]
        ps_y = [s.ps(f"y{d}", [P, 512]) for d in range(2)]
        loaded = s.sem("loaded")
        memset_done = s.sem("memset_done")
        iota_done = s.sem("iota_done")
        v = s.sem("v")
        zeroed = s.sem("zeroed")
        hot = s.sem("hot")
        used = s.sem("used")
        counted = s.sem("counted")
        deg_ready = s.sem("deg_ready")
        hist_done = s.sem("hist_done")
        base_ready = s.sem("base_ready")
        based = s.sem("based")
        hot2 = s.sem("hot2")
        ranked = s.sem("ranked")
        prefixed = s.sem("prefixed")
        passed = s.sem("passed")
        hot3 = s.sem("hot3")
        used3 = s.sem("used3")
        placed = s.sem("placed")
        code_ready = s.sem("code_ready")
        turned = s.sem("turned")
        sel_ready = s.sem("sel_ready")
        tables_ps = s.sem("tables_ps")

        with nc.Block() as block:

            @block.sync
            def _(sp):
                sp.wait_ge(memset_done, 2)
                for ends_of, at in ((dst, key[0]), (src, key[1])):
                    sp.dma_start(at[0:127, :], ends_of[0:127 * C].rearrange("(p c) -> p c", c=C)).then_inc(loaded, 16)
                    sp.dma_start(at[127:128, 0:E - 127 * C], ends_of[127 * C:E].rearrange("(p c) -> p c", p=1)).then_inc(loaded, 16)

            @block.gpsimd
            def _(pool):
                nc.gpsimd.iota(iota_i[:, :], [[1, T]], base=0, channel_multiplier=0).then_inc(iota_done, 1)
                nc.gpsimd.iota(iotap_i[:, :], [[1, 1]], base=0, channel_multiplier=1).then_inc(iota_done, 1)
                nc.gpsimd.iota(edge_i[:, :], [[1, C]], base=0, channel_multiplier=C).then_inc(iota_done, 1)

            @block.vector
            def _(dve):
                ch = Chain(dve, v)
                for d in range(2):
                    nc.vector.memset(key[d][:, :], PAD).then_inc(memset_done, 1)
                nc.vector.memset(zero_b[:, :], 0.0)
                ch.link(nc.vector.memset(ones[:, :], 1.0))
                dve.wait_ge(iota_done, 3)
                nc.vector.tensor_copy(k.iota[:, :], iota_i[:, :])
                ch.link(nc.vector.tensor_copy(k.iotap[:, :], iotap_i[:, :]))
                ch.link(nc.vector.tensor_copy(edge[:, :], edge_i[:, :]))
                nc.vector.tensor_scalar(k.ident[:, :], k.iota[:, 0:P], k.iotap[:, 0:1], None, ALU.is_equal)
                nc.vector.tensor_scalar(below[:, :], k.iota[:, 0:P], k.iotap[:, 0:1], None, ALU.is_gt)
                nc.vector.tensor_scalar(upto[:, :], k.iota[:, 0:P], k.iotap[:, 0:1], None, ALU.is_le)
                nc.vector.tensor_scalar(eq[:, 0:1], k.iotap[:, :], 0.0, None, ALU.is_equal)
                ch.link(nc.vector.tensor_scalar(eq[:, 1:2], k.iotap[:, :], 127.0, None, ALU.is_equal))
                nc.vector.tensor_scalar(row0[:, :], ones[:, :], eq[:, 0:1], None, ALU.mult)
                ch.link(nc.vector.tensor_scalar(row127[:, :], ones[:, :], eq[:, 1:2], None, ALU.mult))
                dve.wait_ge(loaded, 64)
                for d in range(2):
                    nc.vector.tensor_scalar(t_i[:, d, :], key[d][:, :], 10, 3, ALU.logical_shift_right, ALU.logical_shift_left)
                    nc.vector.tensor_scalar(low_i[:, d, :], key[d][:, :], 7, None, ALU.bitwise_and)
                    ch.link(nc.vector.tensor_scalar(lane_i[:, d, :], key[d][:, :], 3, 127, ALU.logical_shift_right, ALU.bitwise_and))
                    ch.link(nc.vector.tensor_tensor(tmp_i[:, d, :], t_i[:, d, :], low_i[:, d, :], ALU.bitwise_or))
                nc.vector.tensor_copy(tile[:, :, :], tmp_i[:, :, :])
                ch.link(nc.vector.tensor_copy(lane[:, :, :], lane_i[:, :, :]))
                for d in range(2):
                    ch.link(nc.vector.tensor_copy(pay[:, d, 0, :], key[1 - d][:, :]))
                    ch.link(nc.vector.scalar_tensor_tensor(out=pay[:, d, 0, :], in0=pay[:, d, 0, :], scalar=128.0, in1=lane[:, d, :], op0=ALU.mult, op1=ALU.add))
                ch.link(nc.vector.tensor_scalar(edge[:, :], edge[:, :], float(E - 1), 512.0, ALU.min, ALU.mult))
                for d in range(2):
                    last = nc.vector.tensor_tensor(pay[:, d, 1, :], edge[:, :], tile[:, d, :], ALU.add)
                ch.link(last)

                def count(i, first):
                    for u in range(2):
                        for d in range(2):
                            if not (first and u < 2):
                                dve.wait_ge(used, (i * 2 + u) * 2 + d + 1 - 4)
                            c = i * 2 + u
                            nc.vector.tensor_scalar(oh_lane[:, u, d, :], k.iota[:, 0:P], lane[:, d, bass.ds(c, 1)], None, ALU.is_equal)
                            nc.vector.tensor_scalar(oh_tile[:, u, d, :], k.iota[:, :], tile[:, d, bass.ds(c, 1)], None, ALU.is_equal).then_inc(hot, 1)
                looped(dve, C // 2, count)
                dve.wait_ge(counted, 1)
                for d in range(2):
                    last = nc.vector.tensor_copy(deg[:, d, :], ps_acc[d][:, 0:T])
                last.then_inc(deg_ready, 1)
                dve.wait_ge(deg_ready, 1)
                ch.link(nc.vector.tensor_scalar(k.inv[:, :, :], deg[:, :, :], 1.0, None, ALU.max))
                ch.link(nc.vector.reciprocal(k.inv[:, :, :], k.inv[:, :, :]))
                dve.wait_ge(hist_done, 1)
                for d in range(2):
                    nc.vector.tensor_copy(hist[:, d, :], ps_x[d][:, 0:T])
                    last = nc.vector.tensor_copy(scan[:, 0, d, :], ps_x[d][:, 0:T])
                ch.link(last)
                step, at = 1, 0
                while step < T:
                    nc.vector.tensor_copy(scan[:, 1 - at, :, 0:step], scan[:, at, :, 0:step])
                    ch.link(nc.vector.tensor_tensor(scan[:, 1 - at, :, step:T], scan[:, at, :, step:T], scan[:, at, :, 0:T - step], ALU.add))
                    step, at = 2 * step, 1 - at
                nc.vector.tensor_tensor(base[:, :, :], scan[:, at, :, :], hist[:, :, :], ALU.subtract).then_inc(base_ready, 1)
                dve.wait_ge(base_ready, 1)

                def order(i, first):
                    for u in range(2):
                        for d in range(2):
                            c = i * 2 + u
                            n = (i * 2 + u) * 2 + d
                            if not (first and u < 2):
                                dve.wait_ge(passed, n + 1 - 4)
                            nc.vector.tensor_scalar(oh_tile[:, u, d, :], k.iota[:, :], tile[:, d, bass.ds(c, 1)], None, ALU.is_equal).then_inc(hot2, 1)
                    for u in range(2):
                        for d in range(2):
                            c = i * 2 + u
                            n = (i * 2 + u) * 2 + d
                            dve.wait_ge(prefixed, n + 1)
                            if not (first and u == 0 and d == 0):
                                dve.wait_ge(ranked, n)
                            nc.vector.scalar_tensor_tensor(out=junk[:, :], in0=k.iota[:, :], scalar=tile[:, d, bass.ds(c, 1)], in1=ps_acc[d][:, 0:T], op0=ALU.is_equal, op1=ALU.mult, accum_out=rank[:, d, bass.ds(c, 1)]).then_inc(ranked, 1)
                looped(dve, C // 2, order)
                dve.wait_ge(ranked, 2 * C)
                ch.link(nc.vector.tensor_copy(rank_i[:, :, :], rank[:, :, :]))
                ch.link(nc.vector.tensor_scalar(tmp_i[:, :, :], rank_i[:, :, :], 127, None, ALU.bitwise_and))
                ch.link(nc.vector.tensor_copy(row_f[:, :, :], tmp_i[:, :, :]))
                ch.link(nc.vector.tensor_scalar(tmp_i[:, :, :], rank_i[:, :, :], 7, None, ALU.logical_shift_right))
                ch.link(nc.vector.tensor_copy(col_f[:, :, :], tmp_i[:, :, :]))

                def place(i, first):
                    for u in range(2):
                        for d in range(2):
                            c = i * 2 + u
                            if not (first and u < 2):
                                dve.wait_ge(used3, (i * 2 + u) * 2 + d + 1 - 4)
                            nc.vector.tensor_scalar(oh_row[:, u, d, :], k.iota[:, 0:P], row_f[:, d, bass.ds(c, 1)], None, ALU.is_equal)
                            for w in range(2):
                                last = nc.vector.tensor_scalar(oh_col[:, u, d, w, :], k.iota[:, 0:C], col_f[:, d, bass.ds(c, 1)], pay[:, d, w, bass.ds(c, 1)], ALU.is_equal, ALU.mult)
                            last.then_inc(hot3, 1)
                looped(dve, C // 2, place)
                dve.wait_ge(placed, 1)
                for d in range(2):
                    last = nc.vector.tensor_copy(out_i[:, d, :, :], ps_x[d][:, 0:2 * C].rearrange("p (w c) -> p w c", w=2))
                ch.link(last)
                for d in range(2):
                    nc.vector.tensor_scalar(k.other[:, d, :], out_i[:, d, 0, :], 7, None, ALU.logical_shift_right)
                    nc.vector.tensor_scalar(low_i[:, d, :], out_i[:, d, 0, :], 127, None, ALU.bitwise_and)
                    last = nc.vector.tensor_scalar(t_i[:, d, :], out_i[:, d, 1, :], 511, None, ALU.bitwise_and)
                nc.vector.tensor_scalar(k.number[:, :], out_i[:, 0, 1, :], 9, None, ALU.logical_shift_right)
                ch.link(last)
                nc.vector.tensor_copy(lane[:, :, :], low_i[:, :, :])
                ch.link(nc.vector.tensor_copy(tsort[:, :, :], t_i[:, :, :]))
                nc.vector.scalar_tensor_tensor(out=code[:, :, :], in0=tsort[:, :, :], scalar=128.0, in1=lane[:, :, :], op0=ALU.mult, op1=ALU.add).then_inc(code_ready, 1)
                dve.wait_ge(code_ready, 1)
                ch.link(nc.vector.tensor_copy(c0_i[:, :, :], base[:, :, :]))
                ch.link(nc.vector.tensor_scalar(c0_i[:, :, :], c0_i[:, :, :], 7, None, ALU.logical_shift_right))
                ch.link(nc.vector.tensor_copy(c0[:, :, :], c0_i[:, :, :]))
                ch.link(nc.vector.tensor_scalar(c0[:, :, :], c0[:, :, :], float(C - 1), None, ALU.min))
                ch.link(nc.vector.tensor_tensor(cl[:, :, :], base[:, :, :], hist[:, :, :], ALU.add))
                ch.link(nc.vector.tensor_scalar(cl[:, :, :], cl[:, :, :], 1.0, 0.0, ALU.subtract, ALU.max))
                ch.link(nc.vector.tensor_copy(cl_i[:, :, :], cl[:, :, :]))
                ch.link(nc.vector.tensor_scalar(cl_i[:, :, :], cl_i[:, :, :], 7, None, ALU.logical_shift_right))
                ch.link(nc.vector.tensor_copy(cl[:, :, :], cl_i[:, :, :]))
                ch.link(nc.vector.tensor_tensor(more[:, :, :], cl[:, :, :], c0[:, :, :], ALU.is_gt))
                ch.link(nc.vector.scalar_tensor_tensor(out=cl[:, :, :], in0=cl[:, :, :], scalar=1.0, in1=more[:, :, :], op0=ALU.add, op1=ALU.mult))
                for d in range(2):
                    nc.vector.tensor_scalar(k.offs[:, d, :, 0], c0[0:1, d, :], float(D), None, ALU.mult)
                    nc.vector.tensor_scalar(k.offs[:, d, :, 1], cl[0:1, d, :], float(D), None, ALU.mult)
                for d in range(2):
                    for h in range(2):
                        last = nc.vector.tensor_scalar(sel[:, d, h, :], c0[0:98, d, :], k.iotap[0:98, 0:1], float(98 * h), ALU.subtract, ALU.is_equal)
                dve.wait_ge(turned, 1)
                for d in range(2):
                    for h in range(2):
                        last = nc.vector.tensor_copy(code_t[:, d, h, :], ps_y[d][0:98, h * P:(h + 1) * P])
                    nc.vector.tensor_copy(ends[:, d, :, :], ps_acc[d][:, 0:2 * C].rearrange("p (w c) -> p w c", w=2))
                last.then_inc(sel_ready, 1)
                ch.link(nc.vector.memset(cont[:, :, 0:1], 0.0))
                ch.link(nc.vector.tensor_tensor(cont[:, :, 1:C], ends[:, :, 1, 0:C - 1], ends[:, :, 0, 1:C], ALU.is_equal))
                ch.link(nc.vector.scalar_tensor_tensor(out=k.pb[:, :, :], in0=ends[:, :, 0, :], scalar=-128.0, in1=code[:, :, :], op0=ALU.mult, op1=ALU.add))
                ch.link(nc.vector.scalar_tensor_tensor(out=k.pb[:, :, :], in0=k.pb[:, :, :], scalar=1.0, in1=cont[:, :, :], op0=ALU.add, op1=ALU.mult))
                ch.link(nc.vector.tensor_scalar(k.pb[:, :, :], k.pb[:, :, :], -1.0, None, ALU.add))
                ch.link(nc.vector.memset(k.keep[:, :, 0:1], 0.0))
                ch.link(nc.vector.tensor_tensor(k.keep[:, :, 1:C], ends[:, :, 0, 0:C - 1], ends[:, :, 0, 1:C], ALU.is_equal))
                ch.link(nc.vector.tensor_tensor(k.keep[:, :, 1:C], k.keep[:, :, 1:C], cont[:, :, 1:C], ALU.mult))
                dve.wait_ge(tables_ps, 1)
                for d in range(2):
                    nc.vector.scalar_tensor_tensor(out=k.pa[:, d, :], in0=k.iota[:, :], scalar=-128.0, in1=ps_x[d][:, 0:T], op0=ALU.mult, op1=ALU.add)

            @block.tensor
            def _(t):
                t.wait_ge(hot, 1)
                for d in range(2):
                    nc.tensor.matmul(ps_acc[d][:, 0:T], zero_b[:, 0:P], zero_b[:, :], start=True, stop=False)

                def count(i, first):
                    for u in range(2):
                        for d in range(2):
                            t.wait_ge(hot, (i * 2 + u) * 2 + d + 1)
                            nc.tensor.matmul(ps_acc[d][:, 0:T], oh_lane[:, u, d, :], oh_tile[:, u, d, :], start=False, stop=False).then_inc(used, 1)
                looped(t, C // 2, count)
                for d in range(2):
                    last = nc.tensor.matmul(ps_acc[d][:, 0:T], zero_b[:, 0:P], zero_b[:, :], start=False, stop=True)
                last.then_inc(counted, 1)
                t.wait_ge(deg_ready, 1)
                for d in range(2):
                    last = nc.tensor.matmul(ps_x[d][:, 0:T], ones[:, :], deg[:, d, :], start=True, stop=True)
                last.then_inc(hist_done, 1)
                t.wait_ge(base_ready, 1)
                for d in range(2):
                    nc.tensor.matmul(ps_acc[d][:, 0:T], k.ident[:, :], base[:, d, :], start=True, stop=True)

                def order(i, first):
                    for u in range(2):
                        for d in range(2):
                            n = (i * 2 + u) * 2 + d
                            t.wait_ge(hot2, n + 1)
                            nc.tensor.matmul(ps_acc[d][:, 0:T], below[:, :], oh_tile[:, u, d, :], start=False, stop=True, skip_group_check=True).then_inc(prefixed, 1)
                            if not (first and u == 0 and d == 0):
                                after(n - 1, u if d else 1 - u, 1 - d)
                    
                def after(n, u, d):
                    t.wait_ge(ranked, n + 1)
                    nc.tensor.matmul(ps_acc[d][:, 0:T], upto[:, :], oh_tile[:, u, d, :], start=False, stop=True, skip_group_check=True).then_inc(passed, 1)
                looped(t, C // 2, order)
                after(2 * C - 1, 1, 1)
                for d in range(2):
                    nc.tensor.matmul(ps_x[d][:, 0:2 * C], zero_b[:, 0:P], zero_b[:, 0:2 * C], start=True, stop=False)

                def place(i, first):
                    for u in range(2):
                        for d in range(2):
                            t.wait_ge(hot3, (i * 2 + u) * 2 + d + 1)
                            nc.tensor.matmul(ps_x[d][:, 0:2 * C], oh_row[:, u, d, :], oh_col[:, u, d, :, :].rearrange("p w c -> p (w c)"), start=False, stop=False).then_inc(used3, 1)
                looped(t, C // 2, place)
                for d in range(2):
                    last = nc.tensor.matmul(ps_x[d][:, 0:2 * C], zero_b[:, 0:P], zero_b[:, 0:2 * C], start=False, stop=True)
                last.then_inc(placed, 1)
                t.wait_ge(code_ready, 1)
                for d in range(2):
                    for h in range(2):
                        nc.tensor.transpose(ps_y[d][0:98, h * P:(h + 1) * P], code[:, d, 98 * h:98 * h + 98], k.ident[:, :])
                    nc.tensor.matmul(ps_acc[d][:, 0:C], row0[:, :], tsort[:, d, :], start=True, stop=True)
                    last = nc.tensor.matmul(ps_acc[d][:, C:2 * C], row127[:, :], tsort[:, d, :], start=True, stop=True)
                last.then_inc(turned, 1)
                t.wait_ge(sel_ready, 1)
                for d in range(2):
                    for h in range(2):
                        last = nc.tensor.matmul(ps_x[d][:, 0:T], code_t[:, d, h, :], sel[:, d, h, :], start=h == 0, stop=h == 1)
                last.then_inc(tables_ps, 1)



def by_group(eng, body):
    body(0, 0, True)
    body(1, 1, True)
    with eng.Fori(1, G // 2) as i:
        body(2 * i, 0, False)
        body(2 * i + 1, 1, False)
    body(G - 1, 0, False)


def uses(g, s):
    return ((g - s) * 8) + 16 if not isinstance(g, int) else ((g - s) // 2 + 1) * 16


def rows(table, g):
    v = table.rearrange("(g p f) d -> g p (f d)", p=P, f=J)
    return v[bass.ds(g, 1), :, :].rearrange("a p f -> (a p) f")


def outer_rows(nc, x, g):
    if isinstance(g, int) and g == G - 1:
        return x[(G - 1) * P * J:N, :].rearrange("(p f) d -> p (f d)", f=J)
    return rows(x[0:(G - 1) * P * J, :], g)


def lanes(g):
    return LAST if isinstance(g, int) and g == G - 1 else P


class Norm:

    def __init__(self, nc, k, s):
        self.nc = nc
        self.cent = s.sb("cent", [P, 2, J, D])
        self.sq = s.sb("sq", [P, 2, J, D])
        self.h = s.sb("h", [P, 2, J, D])
        self.small = s.sb("small", [P, 2, 4, J])
        self.k = k
        self.std_done = s.sem("std_done")
        self.sum_done = s.sem("sum_done")
        self.mean_done = s.sem("mean_done")
        self.cent_done = s.sem("cent_done")
        self.sq_done = s.sem("sq_done")
        self.var_done = s.sem("var_done")
        self.rstd_done = s.sem("rstd_done")
        self.h_done = s.sem("h_done")

    def center(self, dve, g, s, first, x):
        vec, m = self.nc.vector, self.small
        vec.tensor_reduce(m[:, s, 0, :], x, mybir.AxisListType.X, ALU.add).then_inc(self.sum_done, 1)
        dve.wait_ge(self.sum_done, g + 1)
        vec.tensor_scalar(m[:, s, 1, :], m[:, s, 0, :], 1.0 / D, None, ALU.mult).then_inc(self.mean_done, 1)
        dve.wait_ge(self.mean_done, g + 1)
        vec.tensor_tensor(self.cent[:, s], x, m[:, s, 1, :].unsqueeze(2).to_broadcast([P, J, D]), ALU.subtract).then_inc(self.cent_done, 1)

    def square(self, act, g, s, first):
        act.wait_ge(self.cent_done, g + 1)
        if not first:
            act.wait_ge(self.var_done, g - 1)
        self.nc.scalar.activation(self.sq[:, s], self.cent[:, s], ACT.Square).then_inc(self.sq_done, 1)

    def variance(self, dve, g, s, first):
        dve.wait_ge(self.sq_done, g + 1)
        self.nc.vector.tensor_reduce(self.small[:, s, 2, :], self.sq[:, s], mybir.AxisListType.X, ALU.add).then_inc(self.var_done, 1)

    def deviation(self, act, g, s, first):
        act.wait_ge(self.var_done, g + 1)
        self.nc.scalar.activation(self.small[:, s, 1, :], self.small[:, s, 2, :], ACT.Sqrt, bias=self.k.eps[:, 0:1], scale=1.0 / D).then_inc(self.std_done, 1)

    def scale(self, dve, g, s, first, stored):
        vec, m = self.nc.vector, self.small
        dve.wait_ge(self.sq_done, g + 1)
        dve.wait_ge(self.std_done, g + 1)
        vec.reciprocal(m[:, s, 3, :], m[:, s, 1, :]).then_inc(self.rstd_done, 1)
        dve.wait_ge(self.rstd_done, g + 1)
        if not first:
            stored()
        vec.scalar_tensor_tensor(out=self.h[:, s], in0=self.cent[:, s], scalar=0.0, in1=m[:, s, 3, :].unsqueeze(2).to_broadcast([P, J, D]), op0=ALU.max, op1=ALU.mult).then_inc(self.h_done, 1)


def staged(eng, early, late):
    early(0, 0, True)
    early(1, 1, True)
    late(0, 0, True)
    early(2, 0, False)
    late(1, 1, True)
    with eng.Fori(1, G // 2) as i:
        early(2 * i + 1, 1, False)
        late(2 * i, 0, False)
        early(2 * i + 2, 0, False)
        late(2 * i + 1, 1, False)
    late(G - 1, 0, False)


def three_stages(eng, early, middle, late):
    early(0, 0, True)
    middle(0, 0, True)
    early(1, 1, True)
    late(0, 0, True)
    middle(1, 1, True)
    early(2, 0, False)
    late(1, 1, True)
    middle(2, 0, False)
    early(3, 1, False)
    with eng.Fori(2, G // 2) as i:
        late(2 * i - 2, 0, False)
        middle(2 * i - 1, 1, False)
        early(2 * i, 0, False)
        late(2 * i - 1, 1, False)
        middle(2 * i, 0, False)
        early(2 * i + 1, 1, False)
    late(G - 3, 0, False)
    middle(G - 2, 1, False)
    early(G - 1, 0, False)
    late(G - 2, 1, False)
    middle(G - 1, 0, False)
    late(G - 1, 0, False)


def normalise_input(nc, k, x, table):
    with Scope(nc, "ln") as s:
        xin = s.sb("xin", [P, 2, J * D])
        nm = Norm(nc, k, s)
        loaded = [s.sem(f"loaded{i}") for i in range(2)]
        stored = [s.sem(f"stored{i}") for i in range(2)]
        with nc.Block() as block:

            @block.sync
            def _(sp):
                def load(g, s, first):
                    if not first:
                        sp.wait_ge(nm.cent_done, g - 1)
                    sp.dma_start(xin[0:lanes(g), s, :], outer_rows(nc, x, g)).then_inc(loaded[s], 16)
                by_group(sp, load)

            @block.vector
            def _(dve):
                def early(g, s, first):
                    dve.wait_ge(loaded[s], uses(g, s))
                    nm.center(dve, g, s, first, xin[:, s, :].rearrange("p (j d) -> p j d", j=J))

                def late(g, s, first):
                    nm.scale(dve, g, s, first, lambda: dve.wait_ge(stored[s], uses(g, s) - 16))
                three_stages(dve, early, lambda g, s, first: nm.variance(dve, g, s, first), late)

            @block.scalar
            def _(act):
                staged(act, lambda g, s, first: nm.square(act, g, s, first), lambda g, s, first: nm.deviation(act, g, s, first))

            @block.gpsimd
            def _(pool):
                def store(g, s, first):
                    pool.wait_ge(nm.h_done, g + 1)
                    pool.dma_start(rows(table, g), nm.h[:, s].rearrange("p j d -> p (j d)")).then_inc(stored[s], 16)
                by_group(pool, store)
                pool.wait_ge(stored[0], 25 * 16)
                pool.wait_ge(stored[1], 24 * 16)


def gather_edges(nc, k, d, table, weights=None, edge_attr=None):
    H = U // 2
    with Scope(nc, f"edges") as s:
        land = s.sb("land", [P, U, D])
        eland = s.sb("eland", [P, U, D]) if edge_attr is not None else None
        idx = s.sb("idx", [P, 2, H], I32)
        eidx = s.sb("eidx", [P, 2, H], I32)
        rows_t = s.sb("rows_t", [D, 2, P])
        ohb = s.sb("ohb", [P, 2, P])
        ps_t = [s.ps(f"t{i}", [P, 512]) for i in range(2)]
        ps_m = [s.ps(f"m{i}", [P, 512]) for i in range(2)]
        ps_r = [s.ps(f"r{i}", [P, 512]) for i in range(2)]
        indexed = s.sem("indexed")
        indices_seen = s.sem("indices_seen")
        passed = s.sem("passed")
        landed = [s.sem(f"landed{u}") for u in range(U)]
        taken = s.sem("taken")
        turned_sb = s.sem("turned_sb")
        made = s.sem("made")
        kept = s.sem("kept")
        hot = s.sem("hot")
        summed = s.sem("summed")
        carried = s.sem("carried")
        parts = 1 if edge_attr is None else 2
        with nc.Block() as block:

            @block.gpsimd
            def _(pool):
                def turn(i, first):
                    for h in range(2):
                        if not first:
                            pool.wait_ge(taken if edge_attr is None else kept, U * (i - 1) + H * (h + 1))
                        if edge_attr is not None:
                            nc.gpsimd.tensor_copy(eidx[:, h, :], k.number[:, bass.ds(U * i + H * h, H)])
                        nc.gpsimd.tensor_copy(idx[:, h, :], k.other[:, d, bass.ds(U * i + H * h, H)]).then_inc(indexed, 1)
                        wait_apart(pool, indexed, 2 * i + h + 1, indices_seen)
                        for q in range(H):
                            u = H * h + q
                            nc.gpsimd.indirect_dma_start(out=land[:, u, :], out_offset=None, in_=table, in_offset=bass.IndirectOffsetOnAxis(ap=idx[:, h, q:q + 1], axis=0)).then_inc(landed[u], 16)
                            if edge_attr is not None:
                                nc.gpsimd.indirect_dma_start(out=eland[:, u, :], out_offset=None, in_=edge_attr, in_offset=bass.IndirectOffsetOnAxis(ap=eidx[:, h, q:q + 1], axis=0)).then_inc(landed[u], 16)
                looped(pool, C // U, turn)

            def steps(eng, stages):
                most = max(lag for lag, _ in stages)

                def turn(i, first):
                    for u in range(U):
                        for lag, what in stages:
                            if not (first and u < lag):
                                n = i * U + u - lag
                                what(n, (u - lag) % U, i if u >= lag else i - 1, first and u - lag < 2)
                looped(eng, C // U, turn)
                for u in range(most):
                    for lag, what in stages:
                        if u < lag:
                            n = C + u - lag
                            what(n, (u - lag) % U, C // U - 1, False)

            @block.tensor
            def _(t):
                def turn_rows(n, u, i, first):
                    if not first:
                        t.wait_ge(turned_sb, n - 1)
                    wait_apart(t, landed[u], 16 * (i + 1), passed)
                    nc.tensor.transpose(ps_t[u % 2][0:D, 0:P], land[:, u, :], k.ident[:, :]).then_inc(taken, 1)

                def transform(n, u, i, first):
                    t.wait_ge(turned_sb, n + 1)
                    if not first:
                        t.wait_ge(kept, n - 1)
                    nc.tensor.matmul(ps_m[u % 2][:, 0:D], rows_t[:, u % 2, :], weights, start=True, stop=True).then_inc(made, 1)

                def sum_up(n, u, i, first):
                    t.wait_ge(kept, n + 1)
                    t.wait_ge(hot, n + 1)
                    if not first:
                        t.wait_ge(carried, n)
                    nc.tensor.matmul(ps_r[u % 2][:, 0:D], ohb[:, u % 2, :], k.msg[:, bass.ds(n * D, D)], start=True, stop=True).then_inc(summed, 1)
                steps(t, [(0, turn_rows), (1, transform), (3, sum_up)] if edge_attr is None else [(0, sum_up)])

            @block.scalar
            def _(act):
                def keep_turned(n, u, i, first):
                    act.wait_ge(taken, n + 1)
                    if not first:
                        act.wait_ge(made, n - 1)
                    nc.scalar.copy(rows_t[:, u % 2, :], ps_t[u % 2][0:D, 0:P]).then_inc(turned_sb, 1)

                def keep(n, u, i, first):
                    act.wait_ge(made, n + 1)
                    nc.scalar.copy(k.msg[:, bass.ds(n * D, D)], ps_m[u % 2][:, 0:D]).then_inc(kept, 1)
                if edge_attr is None:
                    steps(act, [(0, keep_turned), (1, keep)])

            @block.vector
            def _(dve):
                dve_zero = nc.vector.memset(k.carry[:, 0:D], 0.0)
                dve_zero.then_inc(carried, 1)

                def add_attr(n, u, i, first):
                    dve.wait_ge(landed[u], 32 * (i + 1))
                    nc.vector.tensor_tensor(k.msg[:, bass.ds(n * D, D)], land[:, u, :], eland[:, u, :], ALU.add).then_inc(kept, 1)

                def one_hot(n, u, i, first):
                    if not first:
                        dve.wait_ge(summed, n - 1)
                    nc.vector.tensor_scalar(ohb[:, u % 2, :], k.iota[:, 0:P], k.pb[:, d, bass.ds(n, 1)], None, ALU.is_equal).then_inc(hot, 1)

                def carry(n, u, i, first):
                    dve.wait_ge(summed, n + 1)
                    dve.wait_ge(carried, n + 1)
                    nc.vector.scalar_tensor_tensor(out=k.carry[:, bass.ds(n * D + D, D)], in0=k.carry[:, bass.ds(n * D, D)], scalar=k.keep[:, d, bass.ds(n, 1)], in1=ps_r[u % 2][:, 0:D], op0=ALU.mult, op1=ALU.add).then_inc(carried, 1)
                steps(dve, [(0, one_hot), (1, carry)] if edge_attr is None else [(0, add_attr), (0, one_hot), (1, carry)])


class Tiles:

    def __init__(self, nc, k, s, d):
        self.nc, self.k, self.d = nc, k, d
        self.oh = s.sb("oh", [P, J, P])
        self.ps = [s.ps(f"agg{i}", [P, 512]) for i in range(2)]
        self.hot = s.sem("hot")
        self.tile_done = s.sem("tile_done")
        self.agg_free = s.sem("agg_free")
        self.agg = s.sb("agg", [P, 2, J, D])
        self.scaled = s.sem("scaled")

    def one_hots(self, dve, g, s, first):
        for j in range(J):
            if not (first and s == 0):
                dve.wait_ge(self.tile_done, g * J + j + 1 - J)
            self.nc.vector.tensor_scalar(self.oh[:, j, :], self.k.iota[:, 0:P], self.k.pa[:, self.d, bass.ds(g * J + j, 1)], None, ALU.is_equal).then_inc(self.hot, 1)

    def sum_tiles(self, t, g, s, first):
        k, nc = self.k, self.nc
        _, offs = nc.values_load_multi_w_load_instructions(
            k.offs[0:1, self.d, bass.ds(g * J, J), :].rearrange("p t w -> p (t w)"), engines=[mybir.EngineType.PE], min_val=0, max_val=C * D,
            skip_runtime_bounds_check_because="offsets come from ranks clamped to the tables")
        if not first:
            t.wait_ge(self.agg_free, g - 1)
        for j in range(J):
            t.wait_ge(self.hot, g * J + j + 1)
            o = self.ps[s][:, j * D:(j + 1) * D]
            nc.tensor.matmul(o, self.oh[:, j, :], k.msg[:, bass.ds(offs[2 * j], D)], start=True, stop=False)
            nc.tensor.matmul(o, k.ident[:, :], k.carry[:, bass.ds(offs[2 * j + 1], D)], start=False, stop=True).then_inc(self.tile_done, 1)

    def mean(self, dve, g, s, first):
        dve.wait_ge(self.tile_done, g * J + J)
        self.nc.vector.tensor_tensor(self.agg[:, s], self.ps[s][:, :].rearrange("p (j d) -> p j d", j=J),
                                     self.k.inv[:, self.d, bass.ds(g * J, J)].unsqueeze(2).to_broadcast([P, J, D]), ALU.mult).then_inc(self.agg_free, 1)
        dve.wait_ge(self.agg_free, g + 1)


def combine(nc, k, d, z, target, relu):
    with Scope(nc, "comb") as s:
        tl = Tiles(nc, k, s, d)
        zin = s.sb("zin", [P, 2, J * D])
        res = s.sb("res", [P, 2, J * D])
        loaded = [s.sem(f"loaded{i}") for i in range(2)]
        stored = [s.sem(f"stored{i}") for i in range(2)]
        added = s.sem("added")
        relued = s.sem("relued")
        with nc.Block() as block:

            @block.sync
            def _(sp):
                def load(g, s, first):
                    if not first:
                        sp.wait_ge(added, g - 1)
                    sp.dma_start(zin[:, s, :], rows(z, g)).then_inc(loaded[s], 16)
                by_group(sp, load)

            @block.tensor
            def _(t):
                by_group(t, lambda g, s, first: tl.sum_tiles(t, g, s, first))

            @block.vector
            def _(dve):
                def early(g, s, first):
                    tl.one_hots(dve, g, s, first)

                def late(g, s, first):
                    tl.mean(dve, g, s, first)
                    dve.wait_ge(loaded[s], uses(g, s))
                    if not first:
                        dve.wait_ge(stored[s], uses(g, s) - 16)
                    nc.vector.tensor_tensor(res[:, s, :], tl.agg[:, s].rearrange("p j d -> p (j d)"), zin[:, s, :], ALU.add).then_inc(added, 1)
                by_group(dve, lambda g, s, first: (early(g, s, first), late(g, s, first)))

            @block.scalar
            def _(act):
                def store(g, s, first):
                    act.wait_ge(added, g + 1)
                    if relu:
                        nc.scalar.activation(res[:, s, :], res[:, s, :], ACT.Relu).then_inc(relued, 1)
                        act.wait_ge(relued, g + 1)
                    act.dma_start(rows(target, g), res[:, s, :]).then_inc(stored[s], 16)
                by_group(act, store)
                act.wait_ge(stored[0], 25 * 16)
                act.wait_ge(stored[1], 24 * 16)


class Turn:

    def __init__(self, nc, k, s, name="turn"):
        self.nc, self.k = nc, k
        self.ps = [s.ps(f"{name}{i}", [P, 512]) for i in range(2)]
        self.sb = s.sb(f"{name}_sb", [D, 2, J * P])
        self.turned = s.sem(f"{name}_turned")
        self.kept = s.sem(f"{name}_kept")
        self.passed = s.sem(f"{name}_passed")

    def turn(self, t, g, s, x):
        if not (isinstance(g, int) and g == 0):
            wait_apart(t, self.kept, 2 * g, self.passed)
        for j in range(J):
            last = self.nc.tensor.transpose(self.ps[j // 4][0:D, (j % 4) * P:(j % 4 + 1) * P], x[:, j * D:(j + 1) * D], self.k.ident[:, :])
            if j % 4 == 3:
                last.then_inc(self.turned, 1)

    def keep(self, act, g, s):
        for h in range(2):
            act.wait_ge(self.turned, 2 * g + h + 1)
            self.nc.scalar.copy(self.sb[:, s, h * 512:(h + 1) * 512], self.ps[h][0:D, :]).then_inc(self.kept, 1)


def mix_nodes(nc, k, z_t, w):
    with Scope(nc, "mix") as s:
        tl = Tiles(nc, k, s, 0)
        tn = Turn(nc, k, s)
        hin = s.sb("hin", [P, 2, J * D])
        hp = s.sb("hp", [P, 2, J * D])
        ps_z = [s.ps(f"z{i}", [P, 512]) for i in range(2)]
        loaded = [s.sem(f"loaded{i}") for i in range(2)]
        stored = [s.sem(f"stored{i}") for i in range(2)]
        mixed = s.sem("mixed")
        made = s.sem("made")
        counted = s.sem("counted")
        stats_done = s.sem("stats_done")
        rooted = s.sem("rooted")
        with nc.Block() as block:

            @block.sync
            def _(sp):
                def load(g, s, first):
                    if not first:
                        sp.wait_ge(mixed, g - 1)
                    sp.dma_start(hin[:, s, :], rows(k.tab[0], g)).then_inc(loaded[s], 16)
                by_group(sp, load)

            @block.tensor
            def _(t):
                def group(g, s, first):
                    tl.sum_tiles(t, g, s, first)
                    t.wait_ge(mixed, g + 1)
                    tn.turn(t, g, s, hp[:, s, :])
                    for h in range(2):
                        t.wait_ge(tn.kept, 2 * g + h + 1)
                        if not (isinstance(g, int) and g == 0):
                            t.wait_ge(counted, 2 * g + h - 1)
                        nc.tensor.matmul(ps_z[h][:, :], k.w1[:, :], tn.sb[:, s, h * 512:(h + 1) * 512], start=True, stop=True).then_inc(made, 1)
                by_group(t, group)

            @block.scalar
            def _(act):
                def store(g, s, first):
                    if not first:
                        act.wait_ge(stored[s], uses(g, s) - 16)
                    tn.keep(act, g, s)
                    act.wait_ge(tn.kept, 2 * g + 2)
                    act.dma_start(z_t[bass.ds(g, 1), :, :].rearrange("a f n -> (a f) n"), tn.sb[:, s, :]).then_inc(stored[s], 16)
                by_group(act, store)
                root_of_variance(nc, act, k, stats_done, rooted, P)
                act.wait_ge(stored[0], 25 * 16)
                act.wait_ge(stored[1], 24 * 16)

            @block.vector
            def _(dve):
                def group(g, s, first):
                    tl.one_hots(dve, g, s, first)
                    tl.mean(dve, g, s, first)
                    dve.wait_ge(loaded[s], uses(g, s))
                    nc.vector.scalar_tensor_tensor(out=hp[:, s, :], in0=hin[:, s, :], scalar=k.one_eps[:, 0:1], in1=tl.agg[:, s].rearrange("p j d -> p (j d)"), op0=ALU.mult, op1=ALU.add).then_inc(mixed, 1)
                    statistics(nc, dve, g, ps_z, made, counted, k.stats, P)
                by_group(dve, group)
                aggregate(nc, dve, k, counted, stats_done, rooted, P, k.b1, k.gamma1, k.beta1, k.scale1, k.shift1)


def statistics(nc, dve, g, ps, made, counted, stats, parts):
    last_group = isinstance(g, int) and g == G - 1
    for h in range(2):
        dve.wait_ge(made, 2 * g + h + 1)
        if last_group:
            for j in range(4):
                last = nc.vector.bn_stats(stats[0:parts, 2 * (G - 1) + h * 4 + j, :], ps[h][0:parts, j * P:j * P + LAST])
        else:
            last = nc.vector.bn_stats(stats[0:parts, bass.ds(2 * g + h, 1), :].rearrange("p a b -> p (a b)"), ps[h][0:parts, :])
        last.then_inc(counted, 1)


def aggregate(nc, dve, k, counted, done, rooted, parts, bias, gamma, beta, scale, shift):
    m = k.moments[0:parts, :]
    ch = Chain(dve, done)
    dve.wait_ge(counted, 2 * G)
    ch.link(nc.vector.bn_aggr(m[:, 0:2], k.stats[0:parts, :, :].rearrange("p a b -> p (a b)")))
    dve.wait_ge(rooted, 1)
    ch.link(nc.vector.reciprocal(m[:, 2:3], m[:, 2:3]))
    ch.link(nc.vector.tensor_tensor(scale[:, :], m[:, 2:3], gamma[:, :], ALU.mult))
    ch.link(nc.vector.tensor_tensor(m[:, 3:4], m[:, 0:1], bias[:, :], ALU.add))
    ch.link(nc.vector.tensor_tensor(m[:, 3:4], bias[:, :], m[:, 3:4], ALU.subtract))
    nc.vector.scalar_tensor_tensor(out=shift[:, :], in0=m[:, 3:4], scalar=scale[:, 0:1], in1=beta[:, :], op0=ALU.mult, op1=ALU.add).then_inc(done, 1)


def root_of_variance(nc, act, k, done, rooted, parts):
    act.wait_ge(done, 1)
    nc.scalar.activation(k.moments[0:parts, 2:3], k.moments[0:parts, 1:2], ACT.Sqrt, bias=k.eps[0:parts, 0:1]).then_inc(rooted, 1)


def second_product(nc, k, z_t):
    with Scope(nc, "prod") as s:
        hp = s.sb("hp", [D, 2, J * P])
        a1 = s.sb("a1", [P, 2, J * P])
        z2 = s.sb("z2", [D, 2, J * P])
        ps_a = [s.ps(f"a{i}", [P, 512]) for i in range(2)]
        ps_z = [s.ps(f"z{i}", [P, 512]) for i in range(2)]
        loaded = [s.sem(f"loaded{i}") for i in range(2)]
        stored = [s.sem(f"stored{i}") for i in range(2)]
        first_done = s.sem("first_done")
        relued = s.sem("relued")
        made = s.sem("made")
        copied = s.sem("copied")
        counted = s.sem("counted")
        done = s.sem("done")
        rooted = s.sem("rooted")

        def at(g):
            return z_t[bass.ds(g, 1), :, :].rearrange("a f n -> (a f) n")
        with nc.Block() as block:

            @block.sync
            def _(sp):
                def load(g, s, first):
                    if not first:
                        sp.wait_ge(first_done, 2 * g - 2)
                    sp.dma_start(hp[:, s, :], at(g)).then_inc(loaded[s], 16)
                by_group(sp, load)

            @block.tensor
            def _(t):
                def early(g, s, first):
                    t.wait_ge(loaded[s], uses(g, s))
                    for h in range(2):
                        if not (isinstance(g, int) and g == 0):
                            t.wait_ge(relued, 2 * g + h - 1)
                        nc.tensor.matmul(ps_a[h][:, :], k.w1[:, :], hp[:, s, h * 512:(h + 1) * 512], start=True, stop=True).then_inc(first_done, 1)

                def late(g, s, first):
                    for h in range(2):
                        t.wait_ge(relued, 2 * g + h + 1)
                        if not (isinstance(g, int) and g == 0):
                            t.wait_ge(copied, 2 * g + h - 1)
                            t.wait_ge(counted, 2 * g + h - 1)
                        nc.tensor.matmul(ps_z[h][0:D, :], k.w2[:, :], a1[:, s, h * 512:(h + 1) * 512], start=True, stop=True).then_inc(made, 1)
                staged(t, early, late)

            @block.scalar
            def _(act):
                def group(g, s, first):
                    for h in range(2):
                        act.wait_ge(first_done, 2 * g + h + 1)
                        if not first:
                            act.wait_ge(made, 2 * g + h - 3)
                        nc.scalar.activation(a1[:, s, h * 512:(h + 1) * 512], ps_a[h][:, :], ACT.Relu, bias=k.shift1[:, 0:1], scale=k.scale1[:, 0:1]).then_inc(relued, 1)
                by_group(act, group)
                root_of_variance(nc, act, k, done, rooted, D)

            @block.vector
            def _(dve):
                def group(g, s, first):
                    if not first:
                        dve.wait_ge(stored[s], uses(g, s) - 16)
                    statistics(nc, dve, g, [p for p in ps_z], made, counted, k.stats, D)
                    for h in range(2):
                        nc.vector.tensor_copy(z2[:, s, h * 512:(h + 1) * 512], ps_z[h][0:D, :]).then_inc(copied, 1)
                by_group(dve, group)
                aggregate(nc, dve, k, counted, done, rooted, D, k.b2, k.gamma2, k.beta2, k.scale2, k.shift2)

            @block.gpsimd
            def _(pool):
                def store(g, s, first):
                    pool.wait_ge(copied, 2 * g + 2)
                    pool.dma_start(at(g), z2[:, s, :]).then_inc(stored[s], 16)
                by_group(pool, store)
                pool.wait_ge(stored[0], 25 * 16)
                pool.wait_ge(stored[1], 24 * 16)


def finish_first(nc, k, x, z_t, y_tab, h_tab):
    with Scope(nc, "fin") as s:
        z = s.sb("z", [D, 2, J * P])
        r = s.sb("r", [D, 2, J * P])
        xin = s.sb("xin", [P, 2, J * D])
        x1 = s.sb("x1", [P, 2, J * D])
        y = s.sb("y", [P, 2, J * D])
        nm = Norm(nc, k, s)
        ps_b = [s.ps(f"b{i}", [P, 512]) for i in range(2)]
        z_loaded = [s.sem(f"z_loaded{i}") for i in range(2)]
        x_loaded = [s.sem(f"x_loaded{i}") for i in range(2)]
        h_stored = [s.sem(f"h_stored{i}") for i in range(2)]
        y_stored = [s.sem(f"y_stored{i}") for i in range(2)]
        relued = s.sem("relued")
        back = s.sem("back")
        passed = s.sem("passed")
        added = s.sem("added")
        y_done = s.sem("y_done")
        with nc.Block() as block:

            @block.sync
            def _(sp):
                def load(g, s, first):
                    if not first:
                        sp.wait_ge(relued, g - 1)
                    sp.dma_start(z[:, s, :], z_t[bass.ds(g, 1), :, :].rearrange("a f n -> (a f) n")).then_inc(z_loaded[s], 16)
                    if not first:
                        sp.wait_ge(added, g - 1)
                    sp.dma_start(xin[0:lanes(g), s, :], outer_rows(nc, x, g)).then_inc(x_loaded[s], 16)
                by_group(sp, load)

            @block.scalar
            def _(act):
                def relu(g, s, first):
                    act.wait_ge(z_loaded[s], uses(g, s))
                    if not first:
                        act.wait_ge(back, g - 1)
                    nc.scalar.activation(r[:, s, :], z[:, s, :], ACT.Relu, bias=k.shift2[:, 0:1], scale=k.scale2[:, 0:1]).then_inc(relued, 1)

                def rest(g, s, first):
                    nm.square(act, g, s, first)
                    act.wait_ge(y_done, g + 1)
                    act.dma_start(rows(y_tab, g), y[:, s, :]).then_inc(y_stored[s], 16)
                three_stages(act, relu, rest, lambda g, s, first: nm.deviation(act, g, s, first))
                act.wait_ge(y_stored[0], 25 * 16)
                act.wait_ge(y_stored[1], 24 * 16)

            @block.tensor
            def _(t):
                def group(g, s, first):
                    if not first:
                        t.wait_ge(added, g - 1)
                    wait_apart(t, relued, g + 1, passed)
                    for j in range(J):
                        last = nc.tensor.transpose(ps_b[s][:, j * D:(j + 1) * D], r[:, s, j * P:(j + 1) * P], k.ident[0:D, 0:D])
                    last.then_inc(back, 1)
                by_group(t, group)

            @block.vector
            def _(dve):
                def early(g, s, first):
                    dve.wait_ge(back, g + 1)
                    dve.wait_ge(x_loaded[s], uses(g, s))
                    nc.vector.tensor_tensor(x1[:, s, :], xin[:, s, :], ps_b[s][:, :], ALU.add).then_inc(added, 1)
                    dve.wait_ge(added, g + 1)
                    nm.center(dve, g, s, first, x1[:, s, :].rearrange("p (j d) -> p j d", j=J))
                    if not first:
                        dve.wait_ge(y_stored[s], uses(g, s) - 16)
                    nc.vector.tensor_tensor(y[:, s, :].rearrange("p (j d) -> p j d", j=J), x1[:, s, :].rearrange("p (j d) -> p j d", j=J), k.final_b[:, :].unsqueeze(1).to_broadcast([P, J, D]), ALU.add).then_inc(y_done, 1)

                def late(g, s, first):
                    nm.scale(dve, g, s, first, lambda: dve.wait_ge(h_stored[s], uses(g, s) - 16))
                three_stages(dve, early, lambda g, s, first: nm.variance(dve, g, s, first), late)

            @block.gpsimd
            def _(pool):
                def store(g, s, first):
                    pool.wait_ge(nm.h_done, g + 1)
                    pool.dma_start(rows(h_tab, g), nm.h[:, s].rearrange("p j d -> p (j d)")).then_inc(h_stored[s], 16)
                by_group(pool, store)
                pool.wait_ge(h_stored[0], 25 * 16)
                pool.wait_ge(h_stored[1], 24 * 16)


def root_product(nc, k, layer, h_tab, z_tab, y_tab, out=None):
    last_layer = layer == LAYERS
    W = D if last_layer else 2 * D
    with Scope(nc, "root") as s:
        tn = Turn(nc, k, s)
        hin = s.sb("hin", [P, 2, J * D])
        yin = s.sb("yin", [P, 2, J * D])
        yo = s.sb("yo", [P, 2, J * D])
        zo = s.sb("zo", [P, 2, J * D])
        ps_w = [s.ps(f"w{i}", [P, 512]) for i in range(2)]
        h_loaded = [s.sem(f"h_loaded{i}") for i in range(2)]
        y_loaded = [s.sem(f"y_loaded{i}") for i in range(2)]
        y_stored = [s.sem(f"y_stored{i}") for i in range(2)]
        z_stored = [s.sem(f"z_stored{i}") for i in range(2)]
        made = s.sem("made")
        half_free = s.sem("half_free")
        with nc.Block() as block:

            @block.sync
            def _(sp):
                def load(g, s, first):
                    if not first:
                        sp.wait_ge(tn.turned, 2 * g - 2)
                    sp.dma_start(hin[:, s, :], rows(h_tab, g)).then_inc(h_loaded[s], 16)
                    if not first:
                        sp.wait_ge(half_free, 2 * g - 2)
                    sp.dma_start(yin[:, s, :], rows(y_tab, g)).then_inc(y_loaded[s], 16)
                by_group(sp, load)

            @block.tensor
            def _(t):
                def group(g, s, first):
                    t.wait_ge(h_loaded[s], uses(g, s))
                    tn.turn(t, g, s, hin[:, s, :])
                    for h in range(2):
                        t.wait_ge(tn.kept, 2 * g + h + 1)
                        if not (isinstance(g, int) and g == 0):
                            t.wait_ge(half_free, 2 * g + h - 1)
                        for j in range(4):
                            last = nc.tensor.matmul(ps_w[h][:, j * W:(j + 1) * W], tn.sb[:, s, (4 * h + j) * P:(4 * h + j + 1) * P], k.wt_pair(layer), start=True, stop=True)
                        last.then_inc(made, 1)
                by_group(t, group)

            @block.scalar
            def _(act):
                by_group(act, lambda g, s, first: tn.keep(act, g, s))

            @block.vector
            def _(dve):
                def group(g, s, first):
                    dve.wait_ge(y_loaded[s], uses(g, s))
                    if not first:
                        dve.wait_ge(y_stored[s], uses(g, s) - 16)
                        if not last_layer:
                            dve.wait_ge(z_stored[s], uses(g, s) - 16)
                    for h in range(2):
                        dve.wait_ge(made, 2 * g + h + 1)
                        v = ps_w[h][:, 0:4 * W].rearrange("p (j w) -> p j w", j=4)
                        c = slice(h * 4 * D, (h + 1) * 4 * D)
                        as_tiles = lambda b: b[:, s, c].rearrange("p (j d) -> p j d", j=4)
                        if not last_layer:
                            nc.vector.tensor_tensor(as_tiles(zo), v[:, :, D:2 * D], k.root_b[:, layer, :].unsqueeze(1).to_broadcast([P, 4, D]), ALU.add)
                        last = nc.vector.tensor_tensor(as_tiles(yo), v[:, :, 0:D], as_tiles(yin), ALU.add).then_inc(half_free, 1)
                by_group(dve, group)

            @block.gpsimd
            def _(pool):
                def store(g, s, first):
                    pool.wait_ge(half_free, 2 * g + 2)
                    target = outer_rows(nc, out, g) if last_layer else rows(y_tab, g)
                    part = lanes(g) if last_layer else P
                    pool.dma_start(target, yo[0:part, s, :]).then_inc(y_stored[s], 16)
                    if not last_layer:
                        pool.dma_start(rows(z_tab, g), zo[:, s, :]).then_inc(z_stored[s], 16)
                by_group(pool, store)
                pool.wait_ge(y_stored[0], 25 * 16)
                pool.wait_ge(y_stored[1], 24 * 16)
                if not last_layer:
                    pool.wait_ge(z_stored[0], 25 * 16)
                    pool.wait_ge(z_stored[1], 24 * 16)


def load_parameters(nc, k, a):
    with Scope(nc, "par") as s:
        wn = s.sb("wn", [D, 13, D])
        ps = [s.ps(f"w{i}", [P, 512]) for i in range(2)]
        loaded = s.sem("loaded")
        turned = s.sem("turned")
        eps_done = s.sem("eps_done")
        n = [0]
        col = lambda v: v.rearrange("(p o) -> p o", o=1)
        row = lambda v, cnt: v.rearrange("(o n) -> o n", o=1).to_broadcast([P, cnt])
        with nc.Block() as block:

            @block.sync
            def _(sp):
                def load(to, of):
                    n[0] += 1
                    sp.dma_start(to, of).then_inc(loaded, 16)
                for i, w in enumerate(("root_w", "lin1_w", "lin2_w")):
                    load(wn[:, 3 * i:3 * i + 3, :], a["L1_gnn_" + w].rearrange("l o i -> o l i"))
                load(wn[:, 9:13, :], a["L1_gnn_final_w"].rearrange("o (l i) -> o l i", l=4))
                load(k.w1[:, :], a["L0_gnn_W1"])
                load(k.w2[:, :], a["L0_gnn_W2"])
                for to, of in ((k.b1, "b1"), (k.gamma1, "gamma1"), (k.beta1, "beta1"), (k.b2, "b2"), (k.gamma2, "gamma2"), (k.beta2, "beta2")):
                    load(to[:, :], col(a["L0_gnn_" + of]))
                load(k.one_eps[:, :], row(a["L0_gnn_eps"], 1))
                load(k.final_b[:, :], row(a["L1_gnn_final_b"], D))
                for l in range(LAYERS):
                    load(k.root_b[:, l, :], a["L1_gnn_root_b"][l:l + 1, :].to_broadcast([P, D]))
                sp.wait_ge(loaded, 16 * n[0])

            @block.tensor
            def _(t):
                t.wait_ge(loaded, 16 * 17)
                for i in range(13):
                    last = nc.tensor.transpose(ps[i // 8][0:D, (i % 8) * D:(i % 8 + 1) * D], wn[:, i, :], k.ident[0:D, 0:D])
                last.then_inc(turned, 1)

            @block.vector
            def _(dve):
                dve.wait_ge(turned, 1)
                f = lambda i: ps[i // 8][0:D, (i % 8) * D:(i % 8 + 1) * D]
                for l in range(4):
                    nc.vector.tensor_copy(k.wt[:, 2 * l, :], f(9 + l))
                    if l < 3:
                        nc.vector.tensor_copy(k.wt[:, 2 * l + 1, :], f(l))
                for i in range(6):
                    nc.vector.tensor_copy(k.wt[:, 7 + i, :], f(3 + i))
                nc.vector.memset(k.eps[:, :], EPS)
                nc.vector.tensor_scalar(k.one_eps[:, :], k.one_eps[:, :], 1.0, None, ALU.add)


class Kept:

    def __init__(self, s):
        self.iota = s.sb("iota", [P, T])
        self.iotap = s.sb("iotap", [P, 1])
        self.ident = s.sb("ident", [P, P])
        self.inv = s.sb("inv", [P, 2, T])
        self.other = s.sb("other", [P, 2, C], I32)
        self.number = s.sb("number", [P, C], I32)
        self.pa = s.sb("pa", [P, 2, T])
        self.pb = s.sb("pb", [P, 2, C])
        self.keep = s.sb("keep", [P, 2, C])
        self.offs = s.sb("offs", [1, 2, T, 2], I32)
        self.w1 = s.sb("w1", [D, 2 * D])
        self.w2 = s.sb("w2", [2 * D, D])
        self.wt = s.sb("wt", [D, 13, D])
        self.b1, self.gamma1, self.beta1, self.scale1, self.shift1 = (
            s.sb(name, [2 * D, 1]) for name in ("b1", "gamma1", "beta1", "scale1", "shift1"))
        self.b2, self.gamma2, self.beta2, self.scale2, self.shift2 = (
            s.sb(name, [D, 1]) for name in ("b2", "gamma2", "beta2", "scale2", "shift2"))
        self.one_eps = s.sb("one_eps", [P, 1])
        self.final_b = s.sb("final_b", [P, D])
        self.root_b = s.sb("root_b", [P, LAYERS, D])
        self.stats = s.sb("stats", [P, 2 * (G - 1) + 8, 6])
        self.moments = s.sb("moments", [P, 4])
        self.eps = s.sb("eps", [P, 1])

    def wt_pair(self, layer):
        if layer == LAYERS:
            return self.wt[:, 6, :]
        return self.wt[:, 2 * layer:2 * layer + 2, :].rearrange("p a d -> p (a d)")


def build(nc, a, out):
    with Scope(nc, "kept") as s:
        k = Kept(s)
        k.tab = [nc.dram_tensor(f"tab{i}", (NP, D), F32, kind="Internal").ap() for i in range(2)]
        z_tab = nc.dram_tensor("z_tab", (NP, D), F32, kind="Internal").ap()
        y_tab = nc.dram_tensor("y_tab", (NP, D), F32, kind="Internal").ap()
        z_t = nc.dram_tensor("z_t", (G, D, J * P), F32, kind="Internal").ap()
        k.dbg = (z_tab, y_tab, z_t)
        sort_edges(nc, k, a["src"], a["dst"])
        load_parameters(nc, k, a)
        normalise_input(nc, k, a["x"], k.tab[0])
        with Scope(nc, "msgs") as m:
            k.msg = m.sb("msg", [P, (C + 1) * D])
            k.carry = m.sb("carry", [P, (C + 1) * D])
            gather_edges(nc, k, 0, k.tab[0], edge_attr=a["edge_attr_64"])
            mix_nodes(nc, k, z_t, None)
            second_product(nc, k, z_t)
            finish_first(nc, k, a["x"], z_t, y_tab, k.tab[1])
            for l in range(LAYERS):
                h_in, h_out = k.tab[(l + 1) % 2], k.tab[l % 2]
                root_product(nc, k, l, h_in, z_tab, y_tab)
                for d in range(2):
                    gather_edges(nc, k, d, h_in, weights=k.wt[:, 7 + 3 * d + l, :])
                    combine(nc, k, d, z_tab, z_tab if d == 0 else h_out, relu=d == 1)
            root_product(nc, k, LAYERS, k.tab[(LAYERS + 1) % 2], z_tab, y_tab, out)


_INS = ["x", "src", "dst", "edge_attr_64", "L0_gnn_eps", "L0_gnn_W1", "L0_gnn_b1", "L0_gnn_gamma1", "L0_gnn_beta1",
        "L0_gnn_W2", "L0_gnn_b2", "L0_gnn_gamma2", "L0_gnn_beta2", "L1_gnn_lin1_w", "L1_gnn_lin2_w", "L1_gnn_root_w",
        "L1_gnn_root_b", "L1_gnn_final_w", "L1_gnn_final_b"]


def kernel(**inputs):
    import numpy as np
    import concourse.bacc as bacc
    from concourse.bass_utils import run_bass_kernel_spmd

    nc = bacc.Bacc("TRN2", target_bir_lowering=False, num_devices=1)
    arrays, args = {}, {}
    for name in _INS:
        v = np.ascontiguousarray(inputs[name])
        arrays[f"in_{name}"] = v
        args[name] = nc.dram_tensor(f"in_{name}", v.shape, mybir.dt.from_np(v.dtype), kind="ExternalInput").ap()
    out = nc.dram_tensor("out", (N, D), F32, kind="ExternalOutput").ap()
    build(nc, args, out)
    return run_bass_kernel_spmd(nc, [arrays], core_ids=[0]).results[0]["out"]
```

```python
from contextlib import ExitStack

import concourse.bass as bass
from concourse import mybir

F32 = mybir.dt.float32
BF16 = mybir.dt.bfloat16
I32 = mybir.dt.int32
ALU = mybir.AluOpType
ACT = mybir.ActivationFunctionType
AX_X = mybir.AxisListType.X

P = 128
D = 64
N = 50000
E = 25000
C = 196
U = 14
J = 8
G = 49
T = G * J
NP = T * P
LAST = (N - (G - 1) * P * J) // J
PAD = NP - 1
LAYERS = 3
EPS = 1e-5


def looped(eng, turns, body):
    body(0, True)
    if turns > 1:
        with eng.Fori(1, turns) as i:
            body(i, False)


def wait_apart(eng, sem, value, passed):
    eng.wait_ge(sem, value)
    eng.sem_inc(passed, 1)


class Chain:

    def __init__(self, eng, sem):
        self.eng, self.sem, self.n = eng, sem, 0

    def add(self, ins):
        self.n += 1
        ins.then_inc(self.sem, 1)
        return self.n

    def link(self, ins):
        self.add(ins)
        self.eng.wait_ge(self.sem, self.n)


class Scope:

    count = 0

    def __init__(self, nc, name):
        Scope.count += 1
        self.nc, self.name, self.ctx = nc, f"{name}{Scope.count}", ExitStack()
        self.sems = []

    def __enter__(self):
        self.ctx.__enter__()
        return self

    def __exit__(self, *a):
        if self.sems:
            self.nc.clear_and_free_semaphores(self.sems)
            self.nc.all_engine_barrier()
        return self.ctx.__exit__(*a)

    def sb(self, name, shape, dt=F32):
        return self.ctx.enter_context(self.nc.sbuf_tensor(f"{self.name}_{name}", shape, dt))

    def ps(self, name, shape, dt=F32):
        return self.ctx.enter_context(self.nc.psum_tensor(f"{self.name}_ps_{name}", shape, dt))

    def sem(self, name):
        self.sems.append(self.nc.alloc_semaphore(name=f"{self.name}_sem_{name}"))
        return self.sems[-1]


def sort_edges(nc, k, src, dst):
    vec, pe = nc.vector, nc.tensor
    with Scope(nc, "sort") as s:
        key = [s.sb(f"key{d}", [P, C], I32) for d in range(2)]
        t_i = s.sb("t_i", [P, 2, C], I32)
        low_i = s.sb("low_i", [P, 2, C], I32)
        lane_i = s.sb("lane_i", [P, 2, C], I32)
        tile = s.sb("tile", [P, 2, C])
        lane = s.sb("lane", [P, 2, C])
        edge_i = s.sb("edge_i", [P, C], I32)
        edge = s.sb("edge", [P, C])
        pay = s.sb("pay", [P, 2, 2, C])
        oh_lane = s.sb("oh_lane", [P, 2, 2, P], BF16)
        oh_tile = s.sb("oh_tile", [P, 2, 2, T], BF16)
        oh_row = s.sb("oh_row", [P, 2, 2, P])
        oh_col = s.sb("oh_col", [P, 2, 2, 2, C])
        zero_b = s.sb("zero_b", [P, T], BF16)
        below = s.sb("below", [P, P], BF16)
        upto = s.sb("upto", [P, P], BF16)
        ones = s.sb("ones", [P, P])
        row0 = s.sb("row0", [P, P])
        row127 = s.sb("row127", [P, P])
        eq = s.sb("eq", [P, 2])
        iota_i = s.sb("iota_i", [P, T], I32)
        iotap_i = s.sb("iotap_i", [P, 1], I32)
        deg = s.sb("deg", [P, 2, T])
        hist = s.sb("hist", [P, 2, T])
        scan = s.sb("scan", [P, 2, 2, T])
        base = s.sb("base", [P, 2, T])
        junk = s.sb("junk", [P, T])
        rank = s.sb("rank", [P, 2, C])
        rank_i = s.sb("rank_i", [P, 2, C], I32)
        row_f = s.sb("row_f", [P, 2, C])
        col_f = s.sb("col_f", [P, 2, C])
        tmp_i = s.sb("tmp_i", [P, 2, C], I32)
        out_i = s.sb("out_i", [P, 2, 2, C], I32)
        code = s.sb("code", [P, 2, C])
        tsort = s.sb("tsort", [P, 2, C])
        code_t = s.sb("code_t", [98, 2, 2, P])
        sel = s.sb("sel", [98, 2, 2, T])
        c0_i = s.sb("c0_i", [P, 2, T], I32)
        c0 = s.sb("c0", [P, 2, T])
        cl_i = s.sb("cl_i", [P, 2, T], I32)
        cl = s.sb("cl", [P, 2, T])
        more = s.sb("more", [P, 2, T])
        ends = s.sb("ends", [P, 2, 2, C])
        cont = s.sb("cont", [P, 2, C])
        ps_acc = [s.ps(f"acc{d}", [P, 512]) for d in range(2)]
        ps_x = [s.ps(f"x{d}", [P, 512]) for d in range(2)]
        ps_y = [s.ps(f"y{d}", [P, 512]) for d in range(2)]
        loaded = s.sem("loaded")
        memset_done = s.sem("memset_done")
        iota_done = s.sem("iota_done")
        v = s.sem("v")
        zeroed = s.sem("zeroed")
        hot = s.sem("hot")
        used = s.sem("used")
        counted = s.sem("counted")
        deg_ready = s.sem("deg_ready")
        hist_done = s.sem("hist_done")
        base_ready = s.sem("base_ready")
        based = s.sem("based")
        hot2 = s.sem("hot2")
        ranked = s.sem("ranked")
        prefixed = s.sem("prefixed")
        passed = s.sem("passed")
        hot3 = s.sem("hot3")
        used3 = s.sem("used3")
        placed = s.sem("placed")
        code_ready = s.sem("code_ready")
        turned = s.sem("turned")
        sel_ready = s.sem("sel_ready")
        tables_ps = s.sem("tables_ps")

        with nc.Block() as block:

            @block.sync
            def _(sp):
                sp.wait_ge(memset_done, 2)
                for ends_of, at in ((dst, key[0]), (src, key[1])):
                    sp.dma_start(at[0:127, :], ends_of[0:127 * C].rearrange("(p c) -> p c", c=C)).then_inc(loaded, 16)
                    sp.dma_start(at[127:128, 0:E - 127 * C], ends_of[127 * C:E].rearrange("(p c) -> p c", p=1)).then_inc(loaded, 16)

            @block.gpsimd
            def _(pool):
                nc.gpsimd.iota(iota_i[:, :], [[1, T]], base=0, channel_multiplier=0).then_inc(iota_done, 1)
                nc.gpsimd.iota(iotap_i[:, :], [[1, 1]], base=0, channel_multiplier=1).then_inc(iota_done, 1)
                nc.gpsimd.iota(edge_i[:, :], [[1, C]], base=0, channel_multiplier=C).then_inc(iota_done, 1)

            @block.vector
            def _(dve):
                ch = Chain(dve, v)
                for d in range(2):
                    nc.vector.memset(key[d][:, :], PAD).then_inc(memset_done, 1)
                nc.vector.memset(zero_b[:, :], 0.0)
                ch.link(nc.vector.memset(ones[:, :], 1.0))
                dve.wait_ge(iota_done, 3)
                nc.vector.tensor_copy(k.iota[:, :], iota_i[:, :])
                ch.link(nc.vector.tensor_copy(k.iotap[:, :], iotap_i[:, :]))
                ch.link(nc.vector.tensor_copy(edge[:, :], edge_i[:, :]))
                nc.vector.tensor_scalar(k.ident[:, :], k.iota[:, 0:P], k.iotap[:, 0:1], None, ALU.is_equal)
                nc.vector.tensor_scalar(below[:, :], k.iota[:, 0:P], k.iotap[:, 0:1], None, ALU.is_gt)
                nc.vector.tensor_scalar(upto[:, :], k.iota[:, 0:P], k.iotap[:, 0:1], None, ALU.is_le)
                nc.vector.tensor_scalar(eq[:, 0:1], k.iotap[:, :], 0.0, None, ALU.is_equal)
                ch.link(nc.vector.tensor_scalar(eq[:, 1:2], k.iotap[:, :], 127.0, None, ALU.is_equal))
                nc.vector.tensor_scalar(row0[:, :], ones[:, :], eq[:, 0:1], None, ALU.mult)
                ch.link(nc.vector.tensor_scalar(row127[:, :], ones[:, :], eq[:, 1:2], None, ALU.mult))
                dve.wait_ge(loaded, 64)
                for d in range(2):
                    nc.vector.tensor_scalar(t_i[:, d, :], key[d][:, :], 10, 3, ALU.logical_shift_right, ALU.logical_shift_left)
                    nc.vector.tensor_scalar(low_i[:, d, :], key[d][:, :], 7, None, ALU.bitwise_and)
                    ch.link(nc.vector.tensor_scalar(lane_i[:, d, :], key[d][:, :], 3, 127, ALU.logical_shift_right, ALU.bitwise_and))
                    ch.link(nc.vector.tensor_tensor(tmp_i[:, d, :], t_i[:, d, :], low_i[:, d, :], ALU.bitwise_or))
                nc.vector.tensor_copy(tile[:, :, :], tmp_i[:, :, :])
                ch.link(nc.vector.tensor_copy(lane[:, :, :], lane_i[:, :, :]))
                for d in range(2):
                    ch.link(nc.vector.tensor_copy(pay[:, d, 0, :], key[1 - d][:, :]))
                    ch.link(nc.vector.scalar_tensor_tensor(out=pay[:, d, 0, :], in0=pay[:, d, 0, :], scalar=128.0, in1=lane[:, d, :], op0=ALU.mult, op1=ALU.add))
                ch.link(nc.vector.tensor_scalar(edge[:, :], edge[:, :], float(E - 1), 512.0, ALU.min, ALU.mult))
                for d in range(2):
                    last = nc.vector.tensor_tensor(pay[:, d, 1, :], edge[:, :], tile[:, d, :], ALU.add)
                ch.link(last)

                def count(i, first):
                    for u in range(2):
                        for d in range(2):
                            if not (first and u < 2):
                                dve.wait_ge(used, (i * 2 + u) * 2 + d + 1 - 4)
                            c = i * 2 + u
                            nc.vector.tensor_scalar(oh_lane[:, u, d, :], k.iota[:, 0:P], lane[:, d, bass.ds(c, 1)], None, ALU.is_equal)
                            nc.vector.tensor_scalar(oh_tile[:, u, d, :], k.iota[:, :], tile[:, d, bass.ds(c, 1)], None, ALU.is_equal).then_inc(hot, 1)
                looped(dve, C // 2, count)
                dve.wait_ge(counted, 1)
                for d in range(2):
                    last = nc.vector.tensor_copy(deg[:, d, :], ps_acc[d][:, 0:T])
                last.then_inc(deg_ready, 1)
                dve.wait_ge(deg_ready, 1)
                ch.link(nc.vector.tensor_scalar(k.inv[:, :, :], deg[:, :, :], 1.0, None, ALU.max))
                ch.link(nc.vector.reciprocal(k.inv[:, :, :], k.inv[:, :, :]))
                dve.wait_ge(hist_done, 1)
                for d in range(2):
                    nc.vector.tensor_copy(hist[:, d, :], ps_x[d][:, 0:T])
                    last = nc.vector.tensor_copy(scan[:, 0, d, :], ps_x[d][:, 0:T])
                ch.link(last)
                step, at = 1, 0
                while step < T:
                    nc.vector.tensor_copy(scan[:, 1 - at, :, 0:step], scan[:, at, :, 0:step])
                    ch.link(nc.vector.tensor_tensor(scan[:, 1 - at, :, step:T], scan[:, at, :, step:T], scan[:, at, :, 0:T - step], ALU.add))
                    step, at = 2 * step, 1 - at
                nc.vector.tensor_tensor(base[:, :, :], scan[:, at, :, :], hist[:, :, :], ALU.subtract).then_inc(base_ready, 1)
                dve.wait_ge(base_ready, 1)

                def order(i, first):
                    for u in range(2):
                        for d in range(2):
                            c = i * 2 + u
                            n = (i * 2 + u) * 2 + d
                            if not (first and u < 2):
                                dve.wait_ge(passed, n + 1 - 4)
                            nc.vector.tensor_scalar(oh_tile[:, u, d, :], k.iota[:, :], tile[:, d, bass.ds(c, 1)], None, ALU.is_equal).then_inc(hot2, 1)
                    for u in range(2):
                        for d in range(2):
                            c = i * 2 + u
                            n = (i * 2 + u) * 2 + d
                            dve.wait_ge(prefixed, n + 1)
                            if not (first and u == 0 and d == 0):
                                dve.wait_ge(ranked, n)
                            nc.vector.scalar_tensor_tensor(out=junk[:, :], in0=k.iota[:, :], scalar=tile[:, d, bass.ds(c, 1)], in1=ps_acc[d][:, 0:T], op0=ALU.is_equal, op1=ALU.mult, accum_out=rank[:, d, bass.ds(c, 1)]).then_inc(ranked, 1)
                looped(dve, C // 2, order)
                dve.wait_ge(ranked, 2 * C)
                ch.link(nc.vector.tensor_copy(rank_i[:, :, :], rank[:, :, :]))
                ch.link(nc.vector.tensor_scalar(tmp_i[:, :, :], rank_i[:, :, :], 127, None, ALU.bitwise_and))
                ch.link(nc.vector.tensor_copy(row_f[:, :, :], tmp_i[:, :, :]))
                ch.link(nc.vector.tensor_scalar(tmp_i[:, :, :], rank_i[:, :, :], 7, None, ALU.logical_shift_right))
                ch.link(nc.vector.tensor_copy(col_f[:, :, :], tmp_i[:, :, :]))

                def place(i, first):
                    for u in range(2):
                        for d in range(2):
                            c = i * 2 + u
                            if not (first and u < 2):
                                dve.wait_ge(used3, (i * 2 + u) * 2 + d + 1 - 4)
                            nc.vector.tensor_scalar(oh_row[:, u, d, :], k.iota[:, 0:P], row_f[:, d, bass.ds(c, 1)], None, ALU.is_equal)
                            for w in range(2):
                                last = nc.vector.tensor_scalar(oh_col[:, u, d, w, :], k.iota[:, 0:C], col_f[:, d, bass.ds(c, 1)], pay[:, d, w, bass.ds(c, 1)], ALU.is_equal, ALU.mult)
                            last.then_inc(hot3, 1)
                looped(dve, C // 2, place)
                dve.wait_ge(placed, 1)
                for d in range(2):
                    last = nc.vector.tensor_copy(out_i[:, d, :, :], ps_x[d][:, 0:2 * C].rearrange("p (w c) -> p w c", w=2))
                ch.link(last)
                for d in range(2):
                    nc.vector.tensor_scalar(k.other[:, d, :], out_i[:, d, 0, :], 7, None, ALU.logical_shift_right)
                    nc.vector.tensor_scalar(low_i[:, d, :], out_i[:, d, 0, :], 127, None, ALU.bitwise_and)
                    last = nc.vector.tensor_scalar(t_i[:, d, :], out_i[:, d, 1, :], 511, None, ALU.bitwise_and)
                nc.vector.tensor_scalar(k.number[:, :], out_i[:, 0, 1, :], 9, None, ALU.logical_shift_right)
                ch.link(last)
                nc.vector.tensor_copy(lane[:, :, :], low_i[:, :, :])
                ch.link(nc.vector.tensor_copy(tsort[:, :, :], t_i[:, :, :]))
                nc.vector.scalar_tensor_tensor(out=code[:, :, :], in0=tsort[:, :, :], scalar=128.0, in1=lane[:, :, :], op0=ALU.mult, op1=ALU.add).then_inc(code_ready, 1)
                dve.wait_ge(code_ready, 1)
                ch.link(nc.vector.tensor_copy(c0_i[:, :, :], base[:, :, :]))
                ch.link(nc.vector.tensor_scalar(c0_i[:, :, :], c0_i[:, :, :], 7, None, ALU.logical_shift_right))
                ch.link(nc.vector.tensor_copy(c0[:, :, :], c0_i[:, :, :]))
                ch.link(nc.vector.tensor_scalar(c0[:, :, :], c0[:, :, :], float(C - 1), None, ALU.min))
                ch.link(nc.vector.tensor_tensor(cl[:, :, :], base[:, :, :], hist[:, :, :], ALU.add))
                ch.link(nc.vector.tensor_scalar(cl[:, :, :], cl[:, :, :], 1.0, 0.0, ALU.subtract, ALU.max))
                ch.link(nc.vector.tensor_copy(cl_i[:, :, :], cl[:, :, :]))
                ch.link(nc.vector.tensor_scalar(cl_i[:, :, :], cl_i[:, :, :], 7, None, ALU.logical_shift_right))
                ch.link(nc.vector.tensor_copy(cl[:, :, :], cl_i[:, :, :]))
                ch.link(nc.vector.tensor_tensor(more[:, :, :], cl[:, :, :], c0[:, :, :], ALU.is_gt))
                ch.link(nc.vector.scalar_tensor_tensor(out=cl[:, :, :], in0=cl[:, :, :], scalar=1.0, in1=more[:, :, :], op0=ALU.add, op1=ALU.mult))
                for d in range(2):
                    nc.vector.tensor_scalar(k.offs[:, d, 0, :], c0[0:1, d, :], float(D), None, ALU.mult)
                    nc.vector.tensor_scalar(k.offs[:, d, 1, :], cl[0:1, d, :], float(D), None, ALU.mult)
                for d in range(2):
                    for h in range(2):
                        last = nc.vector.tensor_scalar(sel[:, d, h, :], c0[0:98, d, :], k.iotap[0:98, 0:1], float(98 * h), ALU.subtract, ALU.is_equal)
                dve.wait_ge(turned, 1)
                for d in range(2):
                    for h in range(2):
                        last = nc.vector.tensor_copy(code_t[:, d, h, :], ps_y[d][0:98, h * P:(h + 1) * P])
                    nc.vector.tensor_copy(ends[:, d, :, :], ps_acc[d][:, 0:2 * C].rearrange("p (w c) -> p w c", w=2))
                last.then_inc(sel_ready, 1)
                ch.link(nc.vector.memset(cont[:, :, 0:1], 0.0))
                ch.link(nc.vector.tensor_tensor(cont[:, :, 1:C], ends[:, :, 1, 0:C - 1], ends[:, :, 0, 1:C], ALU.is_equal))
                ch.link(nc.vector.scalar_tensor_tensor(out=k.pb[:, :, :], in0=ends[:, :, 0, :], scalar=-128.0, in1=code[:, :, :], op0=ALU.mult, op1=ALU.add))
                ch.link(nc.vector.scalar_tensor_tensor(out=k.pb[:, :, :], in0=k.pb[:, :, :], scalar=1.0, in1=cont[:, :, :], op0=ALU.add, op1=ALU.mult))
                ch.link(nc.vector.tensor_scalar(k.pb[:, :, :], k.pb[:, :, :], -1.0, None, ALU.add))
                ch.link(nc.vector.memset(k.keep[:, :, 0:1], 0.0))
                ch.link(nc.vector.tensor_tensor(k.keep[:, :, 1:C], ends[:, :, 0, 0:C - 1], ends[:, :, 0, 1:C], ALU.is_equal))
                ch.link(nc.vector.tensor_tensor(k.keep[:, :, 1:C], k.keep[:, :, 1:C], cont[:, :, 1:C], ALU.mult))
                dve.wait_ge(tables_ps, 1)
                for d in range(2):
                    nc.vector.scalar_tensor_tensor(out=k.pa[:, d, :], in0=k.iota[:, :], scalar=-128.0, in1=ps_x[d][:, 0:T], op0=ALU.mult, op1=ALU.add)

            @block.tensor
            def _(t):
                t.wait_ge(hot, 1)
                for d in range(2):
                    nc.tensor.matmul(ps_acc[d][:, 0:T], zero_b[:, 0:P], zero_b[:, :], start=True, stop=False)

                def count(i, first):
                    for u in range(2):
                        for d in range(2):
                            t.wait_ge(hot, (i * 2 + u) * 2 + d + 1)
                            nc.tensor.matmul(ps_acc[d][:, 0:T], oh_lane[:, u, d, :], oh_tile[:, u, d, :], start=False, stop=False).then_inc(used, 1)
                looped(t, C // 2, count)
                for d in range(2):
                    last = nc.tensor.matmul(ps_acc[d][:, 0:T], zero_b[:, 0:P], zero_b[:, :], start=False, stop=True)
                last.then_inc(counted, 1)
                t.wait_ge(deg_ready, 1)
                for d in range(2):
                    last = nc.tensor.matmul(ps_x[d][:, 0:T], ones[:, :], deg[:, d, :], start=True, stop=True)
                last.then_inc(hist_done, 1)
                t.wait_ge(base_ready, 1)
                for d in range(2):
                    nc.tensor.matmul(ps_acc[d][:, 0:T], k.ident[:, :], base[:, d, :], start=True, stop=True)

                def order(i, first):
                    for u in range(2):
                        for d in range(2):
                            n = (i * 2 + u) * 2 + d
                            t.wait_ge(hot2, n + 1)
                            nc.tensor.matmul(ps_acc[d][:, 0:T], below[:, :], oh_tile[:, u, d, :], start=False, stop=True, skip_group_check=True).then_inc(prefixed, 1)
                            if not (first and u == 0 and d == 0):
                                after(n - 1, u if d else 1 - u, 1 - d)
                    
                def after(n, u, d):
                    t.wait_ge(ranked, n + 1)
                    nc.tensor.matmul(ps_acc[d][:, 0:T], upto[:, :], oh_tile[:, u, d, :], start=False, stop=True, skip_group_check=True).then_inc(passed, 1)
                looped(t, C // 2, order)
                after(2 * C - 1, 1, 1)
                for d in range(2):
                    nc.tensor.matmul(ps_x[d][:, 0:2 * C], zero_b[:, 0:P], zero_b[:, 0:2 * C], start=True, stop=False)

                def place(i, first):
                    for u in range(2):
                        for d in range(2):
                            t.wait_ge(hot3, (i * 2 + u) * 2 + d + 1)
                            nc.tensor.matmul(ps_x[d][:, 0:2 * C], oh_row[:, u, d, :], oh_col[:, u, d, :, :].rearrange("p w c -> p (w c)"), start=False, stop=False).then_inc(used3, 1)
                looped(t, C // 2, place)
                for d in range(2):
                    last = nc.tensor.matmul(ps_x[d][:, 0:2 * C], zero_b[:, 0:P], zero_b[:, 0:2 * C], start=False, stop=True)
                last.then_inc(placed, 1)
                t.wait_ge(code_ready, 1)
                for d in range(2):
                    for h in range(2):
                        nc.tensor.transpose(ps_y[d][0:98, h * P:(h + 1) * P], code[:, d, 98 * h:98 * h + 98], k.ident[:, :])
                    nc.tensor.matmul(ps_acc[d][:, 0:C], row0[:, :], tsort[:, d, :], start=True, stop=True)
                    last = nc.tensor.matmul(ps_acc[d][:, C:2 * C], row127[:, :], tsort[:, d, :], start=True, stop=True)
                last.then_inc(turned, 1)
                t.wait_ge(sel_ready, 1)
                for d in range(2):
                    for h in range(2):
                        last = nc.tensor.matmul(ps_x[d][:, 0:T], code_t[:, d, h, :], sel[:, d, h, :], start=h == 0, stop=h == 1)
                last.then_inc(tables_ps, 1)



def by_group(eng, body, late=0):
    for g in range(8):
        body(g, g % 4)
    with eng.Fori(2, G // 4) as i:
        for s in range(4):
            body(4 * i + s, s)
    for g in range(G - 1, G + late):
        body(g, g % 4)


def past(g, n):
    return not isinstance(g, int) or g >= n


def back(stage, eng, g, s, lag):
    if not isinstance(g, int) or 0 <= g - lag < G:
        stage(eng, g - lag, (s - lag) % 4)


def uses(g, s):
    return (g - s % 2) * 8 + 16


def rows(table, g):
    v = table.rearrange("(g p f) d -> g p (f d)", p=P, f=J)
    return v[bass.ds(g, 1), :, :].rearrange("a p f -> (a p) f")


def outer_rows(nc, x, g):
    if isinstance(g, int) and g == G - 1:
        return x[(G - 1) * P * J:N, :].rearrange("(p f) d -> p (f d)", f=J)
    return rows(x[0:(G - 1) * P * J, :], g)


def lanes(g):
    return LAST if isinstance(g, int) and g == G - 1 else P


class Norm:

    def __init__(self, nc, k, s, stored):
        self.nc, self.k, self.stored = nc, k, stored
        self.cent = s.sb("cent", [P, 4, J, D])
        self.sq = s.sb("sq", [P, 2, J, D])
        self.h = s.sb("h", [P, 2, J, D])
        self.sum = s.sb("sum", [P, 2, J])
        self.mean = s.sb("mean", [P, 2, J])
        self.var = s.sb("var", [P, 2, J])
        self.std = s.sb("std", [P, 2, J])
        self.rstd = s.sb("rstd", [P, 2, J])
        self.sum_done = s.sem("sum_done")
        self.mean_done = s.sem("mean_done")
        self.cent_done = s.sem("cent_done")
        self.sq_done = s.sem("sq_done")
        self.var_done = s.sem("var_done")
        self.std_done = s.sem("std_done")
        self.rstd_done = s.sem("rstd_done")
        self.h_done = s.sem("h_done")

    def add_up(self, dve, g, s, x):
        self.nc.vector.tensor_reduce(self.sum[:, s % 2, :], x, mybir.AxisListType.X, ALU.add).then_inc(self.sum_done, 1)
        dve.wait_ge(self.sum_done, g + 1)
        self.nc.vector.tensor_scalar(self.mean[:, s % 2, :], self.sum[:, s % 2, :], 1.0 / D, None, ALU.mult).then_inc(self.mean_done, 1)

    def center(self, dve, g, s, x):
        dve.wait_ge(self.mean_done, g + 1)
        self.nc.vector.tensor_tensor(self.cent[:, s], x, self.mean[:, s % 2, :].unsqueeze(2).to_broadcast([P, J, D]), ALU.subtract).then_inc(self.cent_done, 1)

    def square(self, act, g, s):
        act.wait_ge(self.cent_done, g + 1)
        if past(g, 2):
            act.wait_ge(self.var_done, g - 1)
        self.nc.scalar.activation(self.sq[:, s % 2], self.cent[:, s], ACT.Square).then_inc(self.sq_done, 1)

    def variance(self, dve, g, s):
        dve.wait_ge(self.sq_done, g + 1)
        self.nc.vector.tensor_reduce(self.var[:, s % 2, :], self.sq[:, s % 2], mybir.AxisListType.X, ALU.add).then_inc(self.var_done, 1)

    def deviation(self, act, g, s):
        act.wait_ge(self.var_done, g + 1)
        self.nc.scalar.activation(self.std[:, s % 2, :], self.var[:, s % 2, :], ACT.Sqrt, bias=self.k.eps[:, 0:1], scale=1.0 / D).then_inc(self.std_done, 1)

    def scale(self, dve, g, s):
        dve.wait_ge(self.std_done, g + 1)
        self.nc.vector.reciprocal(self.rstd[:, s % 2, :], self.std[:, s % 2, :]).then_inc(self.rstd_done, 1)
        if past(g, 2):
            dve.wait_ge(self.stored[s % 2], uses(g, s) - 16)
        dve.wait_ge(self.rstd_done, g + 1)
        self.nc.vector.scalar_tensor_tensor(out=self.h[:, s % 2], in0=self.cent[:, s], scalar=0.0, in1=self.rstd[:, s % 2, :].unsqueeze(2).to_broadcast([P, J, D]), op0=ALU.max, op1=ALU.mult).then_inc(self.h_done, 1)


def tiles(ap):
    return ap.rearrange("p (j d) -> p j d", d=D)


def all_stored(eng, stored):
    eng.wait_ge(stored[0], (G + 1) // 2 * 16)
    eng.wait_ge(stored[1], G // 2 * 16)


def normalise_input(nc, k, x, table):
    with Scope(nc, "ln") as s:
        xin = s.sb("xin", [P, 2, J * D])
        loaded = [s.sem(f"loaded{i}") for i in range(2)]
        stored = [s.sem(f"stored{i}") for i in range(2)]
        store_seen = s.sem("store_seen")
        nm = Norm(nc, k, s, stored)
        with nc.Block() as block:

            @block.sync
            def _(sp):
                def load(g, s):
                    if past(g, 2):
                        sp.wait_ge(nm.cent_done, g - 1)
                    sp.dma_start(xin[0:lanes(g), s % 2, :], outer_rows(nc, x, g)).then_inc(loaded[s % 2], 16)
                by_group(sp, load)

            @block.vector
            def _(dve):
                def add_up(dve, g, s):
                    dve.wait_ge(loaded[s % 2], uses(g, s))
                    nm.add_up(dve, g, s, tiles(xin[:, s % 2, :]))

                def group(g, s):
                    back(nm.scale, dve, g, s, 2)
                    back(add_up, dve, g, s, 0)
                    back(nm.variance, dve, g, s, 1)
                    back(lambda dve, g, s: nm.center(dve, g, s, tiles(xin[:, s % 2, :])), dve, g, s, 0)
                by_group(dve, group, 2)

            @block.scalar
            def _(act):
                def group(g, s):
                    back(nm.deviation, act, g, s, 1)
                    back(nm.square, act, g, s, 0)
                by_group(act, group, 1)

            @block.gpsimd
            def _(pool):
                def store(g, s):
                    wait_apart(pool, nm.h_done, g + 1, store_seen)
                    pool.dma_start(rows(table, g), nm.h[:, s % 2].rearrange("p j d -> p (j d)")).then_inc(stored[s % 2], 16)
                by_group(pool, store)
                all_stored(pool, stored)


B = C // G


class Chunks:

    def __init__(self, nc, k, s, d, table, weights=None, edge_attr=None, spill=None):
        self.spill = spill
        self.nc, self.k, self.d, self.table, self.weights, self.edge_attr = nc, k, d, table, weights, edge_attr
        self.land = s.sb("land", [P, 4, B * D])
        self.idx = s.sb("idx", [P, 4, B], I32)
        self.msg = s.sb("msg", [P, 2, B * D])
        self.oh = s.sb("oh_b", [P, 2, B, P])
        self.ps_r = s.ps("r", [P, 512])
        self.indexed = s.sem("indexed")
        self.indices_seen = s.sem("indices_seen")
        self.landed = [s.sem(f"landed{u}") for u in range(4)]
        self.taken = s.sem("taken")
        self.made = s.sem("made")
        self.staged = s.sem("staged")
        self.kept = s.sem("kept")
        self.hot = s.sem("chunk_hot")
        self.summed = s.sem("summed")
        self.sums_kept = s.sem("sums_kept")
        if spill is not None:
            self.sums = s.sb("sums", [P, 2, B * D])
            self.spilled = [s.sem(f"spilled{i}") for i in range(2)]
        if edge_attr is None:
            self.rows_t = s.sb("rows_t", [D, 2, B * P])
            self.ps_t = s.ps("t", [P, 512])
            self.ps_m = s.ps("m", [P, 512])
            self.rows_kept = s.sem("rows_kept")
            self.rows_seen = s.sem("rows_seen")
        else:
            self.attr = s.sb("attr", [P, 4, B * D])
            self.numbers = s.sb("numbers", [P, 4, B], I32)

    def gather(self, pool, g, s):
        nc, k = self.nc, self.k
        if past(g, 4):
            pool.wait_ge(self.taken, g - 3)
        if self.edge_attr is not None:
            nc.gpsimd.tensor_copy(self.numbers[:, s, :], k.number[:, bass.ds(B * g, B)])
        nc.gpsimd.tensor_copy(self.idx[:, s, :], k.other[:, self.d, bass.ds(B * g, B)]).then_inc(self.indexed, 1)
        wait_apart(pool, self.indexed, g + 1, self.indices_seen)
        for q in range(B):
            nc.gpsimd.indirect_dma_start(out=self.land[:, s, q * D:(q + 1) * D], out_offset=None, in_=self.table, in_offset=bass.IndirectOffsetOnAxis(ap=self.idx[:, s, q:q + 1], axis=0)).then_inc(self.landed[s], 16)
            if self.edge_attr is not None:
                nc.gpsimd.indirect_dma_start(out=self.attr[:, s, q * D:(q + 1) * D], out_offset=None, in_=self.edge_attr, in_offset=bass.IndirectOffsetOnAxis(ap=self.numbers[:, s, q:q + 1], axis=0)).then_inc(self.landed[s], 16)

    def turn(self, t, g, s):
        if past(g, 1):
            t.wait_ge(self.rows_kept, g)
        wait_apart(t, self.landed[s], (g - s) * 4 * B + 16 * B, self.rows_seen)
        for q in range(B):
            last = self.nc.tensor.transpose(self.ps_t[0:D, q * P:(q + 1) * P], self.land[:, s, q * D:(q + 1) * D], self.k.ident[:, :])
        last.then_inc(self.taken, 1)

    def keep_rows(self, act, g, s):
        act.wait_ge(self.taken, g + 1)
        if past(g, 2):
            act.wait_ge(self.made, g - 1)
        self.nc.scalar.copy(self.rows_t[:, s % 2, :], self.ps_t[0:D, :]).then_inc(self.rows_kept, 1)

    def transform(self, t, g, s):
        t.wait_ge(self.rows_kept, g + 1)
        if past(g, 1):
            t.wait_ge(self.kept, g)
        for q in range(B):
            last = self.nc.tensor.matmul(self.ps_m[:, q * D:(q + 1) * D], self.rows_t[:, s % 2, q * P:(q + 1) * P], self.weights, start=True, stop=True)
        last.then_inc(self.made, 1)

    def keep(self, act, g, s):
        act.wait_ge(self.made, g + 1)
        if past(g, 2):
            act.wait_ge(self.summed, g - 1)
        self.nc.scalar.copy(self.msg[:, s % 2, :], self.ps_m[:, 0:B * D]).then_inc(self.staged, 1)
        self.nc.scalar.copy(self.k.msg[self.d][:, bass.ds(g * (B * D), B * D)], self.ps_m[:, 0:B * D]).then_inc(self.kept, 1)

    def add_attr(self, dve, g, s):
        dve.wait_ge(self.landed[s], (g - s) * 8 * B + 32 * B)
        if past(g, 2):
            dve.wait_ge(self.kept, g - 1)
            dve.wait_ge(self.summed, g - 1)
        self.nc.vector.tensor_tensor(self.msg[:, s % 2, :], self.land[:, s, :], self.attr[:, s, :], ALU.add).then_inc(self.taken, 1)

    def keep_added(self, act, g, s):
        act.wait_ge(self.taken, g + 1)
        self.nc.scalar.copy(self.k.msg[self.d][:, bass.ds(g * (B * D), B * D)], self.msg[:, s % 2, :]).then_inc(self.kept, 1)

    def one_hot(self, dve, g, s):
        if past(g, 2):
            dve.wait_ge(self.summed, g - 1)
        self.nc.vector.tensor_tensor(self.oh[:, s % 2], self.k.iota[:, 0:P].unsqueeze(1).to_broadcast([P, B, P]),
                                     self.k.pb[:, self.d, bass.ds(g * B, B)].unsqueeze(2).to_broadcast([P, B, P]), ALU.is_equal).then_inc(self.hot, 1)

    def sum_up(self, t, g, s):
        t.wait_ge(self.staged if self.edge_attr is None else self.taken, g + 1)
        t.wait_ge(self.hot, g + 1)
        if past(g, 1):
            t.wait_ge(self.sums_kept, g)
        for q in range(B):
            last = self.nc.tensor.matmul(self.ps_r[:, q * D:(q + 1) * D], self.oh[:, s % 2, q, :], self.msg[:, s % 2, q * D:(q + 1) * D], start=True, stop=True)
        last.then_inc(self.summed, 1)

    def keep_sums(self, act, g, s):
        act.wait_ge(self.summed, g + 1)
        if self.spill is not None:
            if past(g, 2):
                act.wait_ge(self.spilled[s % 2], uses(g, s) - 16)
            to = self.sums[:, s % 2, :]
        else:
            to = self.k.carry[:, bass.ds(g * (B * D) + D, B * D)]
        self.nc.scalar.copy(to, self.ps_r[:, 0:B * D]).then_inc(self.sums_kept, 1)

    def spill_sums(self, sp, g, s):
        sp.wait_ge(self.sums_kept, g + 1)
        sp.dma_start(self.spill[:, bass.ds(g * (B * D), B * D)], self.sums[:, s % 2, :]).then_inc(self.spilled[s % 2], 16)


def carry_over(nc, k, d):
    nc.vector.memset(k.carry[:, 0:D], 0.0)
    sums = k.carry[:, D:(C + 1) * D].rearrange("p (c f) -> p f c", f=D)
    for f in range(D):
        last = nc.vector.tensor_tensor_scan(sums[:, f, :], k.keep[:, d, :], sums[:, f, :], 0.0, ALU.mult, ALU.add)
    return last


class Tiles:

    def __init__(self, nc, k, s, d, used):
        self.nc, self.k, self.d, self.used = nc, k, d, used
        self.oh = s.sb("oh", [P, 2, J // 2, P])
        self.first = s.sb("first", [P, 2, J // 2 * D])
        self.mean = s.sb("mean", [P, 2, J * D])
        self.ps = [s.ps(f"agg{i}", [P, 512]) for i in range(2)]
        self.first_here = s.sem("first_here")
        self.hot = s.sem("hot")
        self.tiles_done = s.sem("tiles_done")
        self.carried_here = s.sem("carried_here")
        self.summed = s.sem("tile_summed")
        self.mean_done = s.sem("tile_mean_done")

    def offsets(self, engine, g, which):
        _, offs = self.nc.values_load_multi_w_load_instructions(
            self.k.offs[0:1, self.d, which, bass.ds(g * J, J)], engines=[engine], min_val=0, max_val=C * D,
            skip_runtime_bounds_check_because="offsets come from ranks clamped to the tables")
        return offs

    def fetch_first(self, eng, copy, g, s):
        offs = self.offsets(eng.engine, g, 0)
        for h in range(2):
            if past(g, 1):
                eng.wait_ge(self.tiles_done, 2 * g + h - 1)
            for q in range(J // 2):
                last = copy(self.first[:, h, q * D:(q + 1) * D], self.k.msg[self.d][:, bass.ds(offs[h * (J // 2) + q], D)])
            last.then_inc(self.first_here, 1)

    def fetch_carried(self, act, g, s):
        offs = self.offsets(act.engine, g, 1)
        if past(g, 2):
            act.wait_ge(self.used, g - 1)
        for j in range(J):
            last = self.nc.scalar.copy(self.mean[:, s % 2, j * D:(j + 1) * D], self.k.carry[:, bass.ds(offs[j], D)])
        last.then_inc(self.carried_here, 1)

    def one_hot(self, dve, g, s):
        for h in range(2):
            if past(g, 1):
                dve.wait_ge(self.tiles_done, 2 * g + h - 1)
            self.nc.vector.tensor_tensor(self.oh[:, h], self.k.iota[:, 0:P].unsqueeze(1).to_broadcast([P, J // 2, P]),
                                         self.k.pa[:, self.d, bass.ds(g * J + h * (J // 2), J // 2)].unsqueeze(2).to_broadcast([P, J // 2, P]), ALU.is_equal).then_inc(self.hot, 1)

    def sum_tiles(self, t, g, s):
        if past(g, 2):
            t.wait_ge(self.summed, g - 1)
        for h in range(2):
            t.wait_ge(self.hot, 2 * g + h + 1)
            t.wait_ge(self.first_here, 2 * g + h + 1)
            for q in range(J // 2):
                j = h * (J // 2) + q
                last = self.nc.tensor.matmul(self.ps[s % 2][:, j * D:(j + 1) * D], self.oh[:, h, q, :], self.first[:, h, q * D:(q + 1) * D], start=True, stop=True)
            last.then_inc(self.tiles_done, 1)

    def take_mean(self, dve, g, s):
        dve.wait_ge(self.tiles_done, 2 * g + 2)
        dve.wait_ge(self.carried_here, g + 1)
        m = self.mean[:, s % 2, :]
        self.nc.vector.tensor_tensor(m, self.ps[s % 2][:, :], m, ALU.add).then_inc(self.summed, 1)
        dve.wait_ge(self.summed, g + 1)
        self.nc.vector.tensor_tensor(tiles(m), tiles(m), self.k.inv[:, self.d, bass.ds(g * J, J)].unsqueeze(2).to_broadcast([P, J, D]), ALU.mult).then_inc(self.mean_done, 1)


class Combine:

    def __init__(self, nc, k, s, d, z, target, relu):
        self.nc, self.z, self.target, self.relu = nc, z, target, relu
        self.added = s.sem("added")
        self.tl = Tiles(nc, k, s, d, used=self.added)
        self.zin = s.sb("zin", [P, 4, J * D])
        self.loaded = [s.sem(f"z_loaded{i}") for i in range(4)]
        self.stored = [s.sem(f"res_stored{i}") for i in range(4)]
        self.relued = s.sem("relued")

    def load(self, sp, g, s):
        if past(g, 4):
            sp.wait_ge(self.stored[s], (g - s) * 4)
        sp.dma_start(self.zin[:, s, :], rows(self.z, g)).then_inc(self.loaded[s], 16)

    def add(self, dve, g, s):
        dve.wait_ge(self.loaded[s], (g - s) * 4 + 16)
        dve.wait_ge(self.tl.mean_done, g + 1)
        self.nc.vector.tensor_tensor(self.zin[:, s, :], self.tl.mean[:, s % 2, :], self.zin[:, s, :], ALU.add).then_inc(self.added, 1)

    def store(self, act, g, s):
        act.wait_ge(self.added, g + 1)
        if self.relu:
            self.nc.scalar.activation(self.zin[:, s, :], self.zin[:, s, :], ACT.Relu).then_inc(self.relued, 1)
            act.wait_ge(self.relued, g + 1)
        act.dma_start(rows(self.target, g), self.zin[:, s, :]).then_inc(self.stored[s], 16)

    def end(self, act):
        for s in range(4):
            act.wait_ge(self.stored[s], ((G - 1 - s) // 4 + 1) * 16)


def gather_edges_and_attributes(nc, k, table, edge_attr):
    with Scope(nc, "edges") as s:
        ck = Chunks(nc, k, s, 0, table, edge_attr=edge_attr)
        with nc.Block() as block:

            @block.gpsimd
            def _(pool):
                by_group(pool, lambda g, s: ck.gather(pool, g, s))

            @block.tensor
            def _(t):
                by_group(t, lambda g, s: ck.sum_up(t, g, s))

            @block.scalar
            def _(act):
                def group(g, s):
                    ck.keep_added(act, g, s)
                    ck.keep_sums(act, g, s)
                by_group(act, group)

            @block.vector
            def _(dve):
                def group(g, s):
                    ck.one_hot(dve, g, s)
                    ck.add_attr(dve, g, s)
                by_group(dve, group)
                dve.wait_ge(ck.sums_kept, G)
                carry_over(nc, k, ck.d)


def gather_first(nc, k, layer, h_tab, z_tab, y_tab):
    with Scope(nc, "edges") as s:
        ck = Chunks(nc, k, s, 0, h_tab, weights=k.wt[:, 7 + layer, :])
        rt = Root(nc, k, s, layer, h_tab, z_tab, y_tab)
        with nc.Block() as block:

            @block.gpsimd
            def _(pool):
                by_group(pool, lambda g, s: ck.gather(pool, g, s))

            @block.tensor
            def _(t):
                def group(g, s):
                    back(ck.turn, t, g, s, 0)
                    back(rt.turn, t, g, s, 0)
                    back(ck.transform, t, g, s, 1)
                    back(rt.product, t, g, s, 0)
                    back(ck.sum_up, t, g, s, 2)
                by_group(t, group, 2)

            @block.scalar
            def _(act):
                def group(g, s):
                    back(ck.keep_rows, act, g, s, 0)
                    back(rt.keep, act, g, s, 0)
                    back(ck.keep, act, g, s, 1)
                    back(ck.keep_sums, act, g, s, 2)
                by_group(act, group, 2)

            @block.vector
            def _(dve):
                def group(g, s):
                    back(ck.one_hot, dve, g, s, 0)
                    back(rt.add, dve, g, s, 0)
                by_group(dve, group)
                dve.wait_ge(ck.sums_kept, G)
                carry_over(nc, k, 0)

            @block.sync
            def _(sp):
                def group(g, s):
                    back(rt.load, sp, g, s, 0)
                    back(rt.store, sp, g, s, 2)
                by_group(sp, group, 2)
                rt.end(sp)


def gather_second(nc, k, layer, h_tab, z_tab, spill):
    with Scope(nc, "both") as s:
        ck = Chunks(nc, k, s, 1, h_tab, weights=k.wt[:, 10 + layer, :], spill=spill)
        cb = Combine(nc, k, s, 0, z_tab, z_tab, relu=False)
        with nc.Block() as block:

            @block.gpsimd
            def _(pool):
                by_group(pool, lambda g, s: ck.gather(pool, g, s))

            @block.tensor
            def _(t):
                def group(g, s):
                    back(ck.sum_up, t, g, s, 2)
                    back(ck.transform, t, g, s, 1)
                    back(ck.turn, t, g, s, 0)
                    back(cb.tl.sum_tiles, t, g, s, 0)
                by_group(t, group, 2)

            @block.scalar
            def _(act):
                def group(g, s):
                    back(ck.keep_sums, act, g, s, 2)
                    back(ck.keep, act, g, s, 1)
                    back(ck.keep_rows, act, g, s, 0)
                    back(cb.tl.fetch_carried, act, g, s, 0)
                by_group(act, group, 2)

            @block.vector
            def _(dve):
                def group(g, s):
                    back(ck.one_hot, dve, g, s, 0)
                    back(cb.tl.one_hot, dve, g, s, 0)
                    back(lambda dve, g, s: cb.tl.fetch_first(dve, nc.vector.tensor_copy, g, s), dve, g, s, 0)
                    back(cb.tl.take_mean, dve, g, s, 1)
                    back(cb.add, dve, g, s, 1)
                by_group(dve, group, 1)

            @block.sync
            def _(sp):
                def group(g, s):
                    back(cb.load, sp, g, s, 0)
                    back(cb.store, sp, g, s, 2)
                    back(ck.spill_sums, sp, g, s, 3)
                by_group(sp, group, 3)
                cb.end(sp)
                all_stored(sp, ck.spilled)


def finish_layer(nc, k, z_tab, target, spill):
    with Scope(nc, "comb") as s:
        cb = Combine(nc, k, s, 1, z_tab, target, relu=True)
        fetched = s.sem("fetched")
        carried = s.sem("carried")
        with nc.Block() as block:

            @block.sync
            def _(sp):
                sp.dma_start(k.carry[:, D:(C + 1) * D], spill[:, :]).then_inc(fetched, 16)
                by_group(sp, lambda g, s: cb.load(sp, g, s))

            @block.tensor
            def _(t):
                by_group(t, lambda g, s: cb.tl.sum_tiles(t, g, s))

            @block.vector
            def _(dve):
                def group(g, s):
                    back(cb.tl.one_hot, dve, g, s, 0)
                    back(cb.tl.take_mean, dve, g, s, 1)
                    back(cb.add, dve, g, s, 1)
                dve.wait_ge(fetched, 16)
                carry_over(nc, k, 1).then_inc(carried, 1)
                by_group(dve, group, 1)

            @block.scalar
            def _(act):
                def group(g, s):
                    back(cb.tl.fetch_carried, act, g, s, 0)
                    back(cb.store, act, g, s, 2)
                act.wait_ge(carried, 1)
                by_group(act, group, 2)
                cb.end(act)

            @block.gpsimd
            def _(pool):
                by_group(pool, lambda g, s: cb.tl.fetch_first(pool, nc.gpsimd.tensor_copy, g, s))


class Turn:

    def __init__(self, nc, k, s, slots=2, name="turn"):
        self.nc, self.k, self.slots = nc, k, slots
        self.ps = [s.ps(f"{name}{i}", [P, 512]) for i in range(2)]
        self.sb = s.sb(f"{name}_sb", [D, slots, J * P])
        self.turned = s.sem(f"{name}_turned")
        self.kept = s.sem(f"{name}_kept")
        self.passed = s.sem(f"{name}_passed")

    def turn(self, t, g, s, x):
        if past(g, 1):
            wait_apart(t, self.kept, 2 * g, self.passed)
        for j in range(J):
            last = self.nc.tensor.transpose(self.ps[j // 4][0:D, (j % 4) * P:(j % 4 + 1) * P], x[:, j * D:(j + 1) * D], self.k.ident[:, :])
            if j % 4 == 3:
                last.then_inc(self.turned, 1)

    def keep(self, act, g, s):
        for h in range(2):
            act.wait_ge(self.turned, 2 * g + h + 1)
            self.nc.scalar.copy(self.sb[:, s % self.slots, h * 512:(h + 1) * 512], self.ps[h][0:D, :]).then_inc(self.kept, 1)


class Root:

    def __init__(self, nc, k, s, layer, h_tab, z_tab, y_tab, out=None):
        self.nc, self.k, self.layer, self.h_tab, self.z_tab, self.y_tab, self.out = nc, k, layer, h_tab, z_tab, y_tab, out
        self.ends = layer == LAYERS
        self.W = D if self.ends else 2 * D
        self.tn = Turn(nc, k, s, slots=2 if self.ends else 1)
        self.hin = s.sb("hin", [P, 2, J * D])
        self.y = s.sb("y", [P, 4, J * D])
        self.z = s.sb("z", [P, 2, J * D])
        self.ps = [s.ps(f"w{i}", [P, 512]) for i in range(2)]
        self.h_loaded = [s.sem(f"h_loaded{i}") for i in range(2)]
        self.y_loaded = [s.sem(f"y_loaded{i}") for i in range(4)]
        self.y_stored = [s.sem(f"y_stored{i}") for i in range(4)]
        self.z_stored = [s.sem(f"z_stored{i}") for i in range(2)]
        self.product_done = s.sem("product_done")
        self.half_added = s.sem("half_added")
        self.seen = s.sem("root_seen")

    def load(self, sp, g, s):
        if past(g, 2):
            sp.wait_ge(self.tn.turned, 2 * g - 2)
        sp.dma_start(self.hin[:, s % 2, :], rows(self.h_tab, g)).then_inc(self.h_loaded[s % 2], 16)
        if past(g, 4):
            sp.wait_ge(self.y_stored[s], (g - s) * 4)
        sp.dma_start(self.y[:, s, :], rows(self.y_tab, g)).then_inc(self.y_loaded[s], 16)

    def turn(self, t, g, s):
        wait_apart(t, self.h_loaded[s % 2], uses(g, s), self.seen)
        self.tn.turn(t, g, s, self.hin[:, s % 2, :])

    def keep(self, act, g, s):
        if past(g, self.tn.slots):
            act.wait_ge(self.product_done, 2 * (g - self.tn.slots) + 2)
        self.tn.keep(act, g, s)

    def product(self, t, g, s):
        for h in range(2):
            t.wait_ge(self.tn.kept, 2 * g + h + 1)
            if past(g, 1):
                t.wait_ge(self.half_added, 2 * g + h - 1)
            for j in range(4):
                last = self.nc.tensor.matmul(self.ps[h][:, j * self.W:(j + 1) * self.W], self.tn.sb[:, s % self.tn.slots, (4 * h + j) * P:(4 * h + j + 1) * P], self.k.wt_pair(self.layer), start=True, stop=True)
            last.then_inc(self.product_done, 1)

    def add(self, dve, g, s):
        dve.wait_ge(self.y_loaded[s], (g - s) * 4 + 16)
        if past(g, 2) and not self.ends:
            dve.wait_ge(self.z_stored[s % 2], uses(g, s) - 16)
        for h in range(2):
            dve.wait_ge(self.product_done, 2 * g + h + 1)
            v = self.ps[h][:, 0:4 * self.W].rearrange("p (j w) -> p j w", j=4)
            c = slice(h * 4 * D, (h + 1) * 4 * D)
            if not self.ends:
                self.nc.vector.tensor_tensor(tiles(self.z[:, s % 2, c]), v[:, :, D:2 * D], self.k.root_b[:, self.layer, :].unsqueeze(1).to_broadcast([P, 4, D]), ALU.add)
            self.nc.vector.tensor_tensor(tiles(self.y[:, s, c]), v[:, :, 0:D], tiles(self.y[:, s, c]), ALU.add).then_inc(self.half_added, 1)

    def store(self, sp, g, s):
        sp.wait_ge(self.half_added, 2 * g + 2)
        if self.ends:
            sp.dma_start(outer_rows(self.nc, self.out, g), self.y[0:lanes(g), s, :]).then_inc(self.y_stored[s], 16)
        else:
            sp.dma_start(rows(self.y_tab, g), self.y[:, s, :]).then_inc(self.y_stored[s], 16)
            sp.dma_start(rows(self.z_tab, g), self.z[:, s % 2, :]).then_inc(self.z_stored[s % 2], 16)

    def end(self, sp):
        for s in range(4):
            sp.wait_ge(self.y_stored[s], ((G - 1 - s) // 4 + 1) * 16)
        if not self.ends:
            all_stored(sp, self.z_stored)


def last_product(nc, k, h_tab, y_tab, out):
    with Scope(nc, "last") as s:
        rt = Root(nc, k, s, LAYERS, h_tab, None, y_tab, out)
        with nc.Block() as block:

            @block.sync
            def _(sp):
                def group(g, s):
                    back(rt.load, sp, g, s, 0)
                    back(rt.store, sp, g, s, 2)
                by_group(sp, group, 2)
                rt.end(sp)

            @block.tensor
            def _(t):
                def group(g, s):
                    back(rt.turn, t, g, s, 0)
                    back(rt.product, t, g, s, 1)
                by_group(t, group, 1)

            @block.scalar
            def _(act):
                by_group(act, lambda g, s: rt.keep(act, g, s))

            @block.vector
            def _(dve):
                by_group(dve, lambda g, s: rt.add(dve, g, s))


def mix_nodes(nc, k, z_t):
    with Scope(nc, "mix") as s:
        mixed = s.sem("mixed")
        tl = Tiles(nc, k, s, 0, used=mixed)
        tn = Turn(nc, k, s)
        hin = s.sb("hin", [P, 2, J * D])
        hp = s.sb("hp", [P, 2, J * D])
        stats = s.sb("stats", [P, 2 * (G - 1) + 8, 6])
        moments = s.sb("moments", [P, 4])
        ps_z = [s.ps(f"z{i}", [P, 512]) for i in range(2)]
        loaded = [s.sem(f"loaded{i}") for i in range(2)]
        stored = [s.sem(f"stored{i}") for i in range(2)]
        made = s.sem("made")
        counted = s.sem("counted")
        stats_done = s.sem("stats_done")
        rooted = s.sem("rooted")
        with nc.Block() as block:

            @block.sync
            def _(sp):
                def load(g, s):
                    if past(g, 2):
                        sp.wait_ge(mixed, g - 1)
                    sp.dma_start(hin[:, s % 2, :], rows(k.tab[0], g)).then_inc(loaded[s % 2], 16)
                by_group(sp, load)

            @block.tensor
            def _(t):
                def turn(t, g, s):
                    t.wait_ge(mixed, g + 1)
                    tn.turn(t, g, s, hp[:, s % 2, :])

                def product(t, g, s):
                    for h in range(2):
                        t.wait_ge(tn.kept, 2 * g + h + 1)
                        if past(g, 1):
                            t.wait_ge(counted, 2 * g + h - 1)
                        nc.tensor.matmul(ps_z[h][:, :], k.w1[:, :], tn.sb[:, s % 2, h * 512:(h + 1) * 512], start=True, stop=True).then_inc(made, 1)

                def group(g, s):
                    back(tl.sum_tiles, t, g, s, 0)
                    back(product, t, g, s, 2)
                    back(turn, t, g, s, 1)
                by_group(t, group, 2)

            @block.scalar
            def _(act):
                def store(act, g, s):
                    if past(g, 2):
                        act.wait_ge(stored[s % 2], uses(g, s) - 16)
                        act.wait_ge(made, 2 * g - 2)
                    tn.keep(act, g, s)
                    act.wait_ge(tn.kept, 2 * g + 2)
                    act.dma_start(z_t[bass.ds(g, 1), :, :].rearrange("a f n -> (a f) n"), tn.sb[:, s % 2, :]).then_inc(stored[s % 2], 16)

                def group(g, s):
                    back(tl.fetch_carried, act, g, s, 0)
                    back(store, act, g, s, 2)
                by_group(act, group, 2)
                root_of_variance(nc, act, k, moments, stats_done, rooted, P)
                all_stored(act, stored)

            @block.gpsimd
            def _(pool):
                by_group(pool, lambda g, s: tl.fetch_first(pool, nc.gpsimd.tensor_copy, g, s))

            @block.vector
            def _(dve):
                def mix(dve, g, s):
                    dve.wait_ge(loaded[s % 2], uses(g, s))
                    dve.wait_ge(tl.mean_done, g + 1)
                    if past(g, 2):
                        dve.wait_ge(tn.turned, 2 * g - 2)
                    nc.vector.scalar_tensor_tensor(out=hp[:, s % 2, :], in0=hin[:, s % 2, :], scalar=k.one_eps[:, 0:1], in1=tl.mean[:, s % 2, :], op0=ALU.mult, op1=ALU.add).then_inc(mixed, 1)

                def group(g, s):
                    back(tl.one_hot, dve, g, s, 0)
                    back(tl.take_mean, dve, g, s, 1)
                    back(lambda dve, g, s: statistics(nc, dve, g, ps_z, made, counted, stats, P), dve, g, s, 3)
                    back(mix, dve, g, s, 1)
                by_group(dve, group, 3)
                aggregate(nc, dve, k, stats, moments, counted, stats_done, rooted, P, k.b1, k.gamma1, k.beta1, k.scale1, k.shift1)


def statistics(nc, dve, g, ps, made, counted, stats, parts):
    last_group = isinstance(g, int) and g == G - 1
    for h in range(2):
        dve.wait_ge(made, 2 * g + h + 1)
        if last_group:
            for j in range(4):
                last = nc.vector.bn_stats(stats[0:parts, 2 * (G - 1) + h * 4 + j, :], ps[h][0:parts, j * P:j * P + LAST])
        else:
            last = nc.vector.bn_stats(stats[0:parts, bass.ds(2 * g + h, 1), :].rearrange("p a b -> p (a b)"), ps[h][0:parts, :])
        last.then_inc(counted, 1)


def aggregate(nc, dve, k, stats, moments, counted, done, rooted, parts, bias, gamma, beta, scale, shift):
    m = moments[0:parts, :]
    ch = Chain(dve, done)
    dve.wait_ge(counted, 2 * G)
    ch.link(nc.vector.bn_aggr(m[:, 0:2], stats[0:parts, :, :].rearrange("p a b -> p (a b)")))
    dve.wait_ge(rooted, 1)
    ch.link(nc.vector.reciprocal(m[:, 2:3], m[:, 2:3]))
    ch.link(nc.vector.tensor_tensor(scale[:, :], m[:, 2:3], gamma[:, :], ALU.mult))
    ch.link(nc.vector.tensor_tensor(m[:, 3:4], m[:, 0:1], bias[:, :], ALU.add))
    ch.link(nc.vector.tensor_tensor(m[:, 3:4], bias[:, :], m[:, 3:4], ALU.subtract))
    nc.vector.scalar_tensor_tensor(out=shift[:, :], in0=m[:, 3:4], scalar=scale[:, 0:1], in1=beta[:, :], op0=ALU.mult, op1=ALU.add).then_inc(done, 1)


def root_of_variance(nc, act, k, moments, done, rooted, parts):
    act.wait_ge(done, 1)
    nc.scalar.activation(moments[0:parts, 2:3], moments[0:parts, 1:2], ACT.Sqrt, bias=k.eps[0:parts, 0:1]).then_inc(rooted, 1)


def second_product(nc, k, z_t):
    with Scope(nc, "prod") as s:
        hp = s.sb("hp", [D, 2, J * P])
        a1 = s.sb("a1", [P, 2, J * P])
        z2 = s.sb("z2", [D, 2, J * P])
        ps_a = [s.ps(f"a{i}", [P, 512]) for i in range(2)]
        stats = s.sb("stats", [P, 2 * (G - 1) + 8, 6])
        moments = s.sb("moments", [P, 4])
        ps_z = [s.ps(f"z{i}", [P, 512]) for i in range(2)]
        loaded = [s.sem(f"loaded{i}") for i in range(2)]
        stored = [s.sem(f"stored{i}") for i in range(2)]
        first_done = s.sem("first_done")
        relued = s.sem("relued")
        made = s.sem("made")
        copied = s.sem("copied")
        store_seen = s.sem("store_seen")
        counted = s.sem("counted")
        done = s.sem("done")
        rooted = s.sem("rooted")

        def at(g):
            return z_t[bass.ds(g, 1), :, :].rearrange("a f n -> (a f) n")
        with nc.Block() as block:

            @block.sync
            def _(sp):
                def load(g, s):
                    if past(g, 2):
                        sp.wait_ge(first_done, 2 * g - 2)
                    sp.dma_start(hp[:, s % 2, :], at(g)).then_inc(loaded[s % 2], 16)
                by_group(sp, load)

            @block.tensor
            def _(t):
                def early(t, g, s):
                    t.wait_ge(loaded[s % 2], uses(g, s))
                    for h in range(2):
                        if past(g, 1):
                            t.wait_ge(relued, 2 * g + h - 1)
                        nc.tensor.matmul(ps_a[h][:, :], k.w1[:, :], hp[:, s % 2, h * 512:(h + 1) * 512], start=True, stop=True).then_inc(first_done, 1)

                def late(t, g, s):
                    for h in range(2):
                        t.wait_ge(relued, 2 * g + h + 1)
                        if past(g, 1):
                            t.wait_ge(copied, 2 * g + h - 1)
                        nc.tensor.matmul(ps_z[h][0:D, :], k.w2[:, :], a1[:, s % 2, h * 512:(h + 1) * 512], start=True, stop=True).then_inc(made, 1)

                def group(g, s):
                    back(early, t, g, s, 0)
                    back(late, t, g, s, 1)
                by_group(t, group, 1)

            @block.scalar
            def _(act):
                def group(g, s):
                    for h in range(2):
                        act.wait_ge(first_done, 2 * g + h + 1)
                        if past(g, 2):
                            act.wait_ge(made, 2 * g + h - 3)
                        nc.scalar.activation(a1[:, s % 2, h * 512:(h + 1) * 512], ps_a[h][:, :], ACT.Relu, bias=k.shift1[:, 0:1], scale=k.scale1[:, 0:1]).then_inc(relued, 1)
                by_group(act, group)
                root_of_variance(nc, act, k, moments, done, rooted, D)

            @block.vector
            def _(dve):
                def group(g, s):
                    if past(g, 2):
                        dve.wait_ge(stored[s % 2], uses(g, s) - 16)
                    statistics(nc, dve, g, ps_z, made, counted, stats, D)
                    for h in range(2):
                        nc.vector.tensor_copy(z2[:, s % 2, h * 512:(h + 1) * 512], ps_z[h][0:D, :]).then_inc(copied, 1)
                by_group(dve, group)
                aggregate(nc, dve, k, stats, moments, counted, done, rooted, D, k.b2, k.gamma2, k.beta2, k.scale2, k.shift2)

            @block.gpsimd
            def _(pool):
                def store(g, s):
                    wait_apart(pool, copied, 2 * g + 2, store_seen)
                    pool.dma_start(at(g), z2[:, s % 2, :]).then_inc(stored[s % 2], 16)
                by_group(pool, store)
                all_stored(pool, stored)


def finish_first(nc, k, x, z_t, y_tab, h_tab):
    with Scope(nc, "fin") as s:
        z = s.sb("z", [D, 2, J * P])
        r = s.sb("r", [D, 2, J * P])
        xin = s.sb("xin", [P, 2, J * D])
        x1 = s.sb("x1", [P, 2, J * D])
        y = s.sb("y", [P, 2, J * D])
        ps_b = [s.ps(f"b{i}", [P, 512]) for i in range(2)]
        z_loaded = [s.sem(f"z_loaded{i}") for i in range(2)]
        x_loaded = [s.sem(f"x_loaded{i}") for i in range(2)]
        h_stored = [s.sem(f"h_stored{i}") for i in range(2)]
        y_stored = [s.sem(f"y_stored{i}") for i in range(2)]
        relued = s.sem("relued")
        back_done = s.sem("back_done")
        passed = s.sem("passed")
        added = s.sem("added")
        y_done = s.sem("y_done")
        store_seen = s.sem("store_seen")
        nm = Norm(nc, k, s, h_stored)
        with nc.Block() as block:

            @block.sync
            def _(sp):
                def load(g, s):
                    if past(g, 2):
                        sp.wait_ge(relued, g - 1)
                    sp.dma_start(z[:, s % 2, :], z_t[bass.ds(g, 1), :, :].rearrange("a f n -> (a f) n")).then_inc(z_loaded[s % 2], 16)
                    if past(g, 2):
                        sp.wait_ge(added, g - 1)
                    sp.dma_start(xin[0:lanes(g), s % 2, :], outer_rows(nc, x, g)).then_inc(x_loaded[s % 2], 16)
                by_group(sp, load)

            @block.scalar
            def _(act):
                def relu(act, g, s):
                    act.wait_ge(z_loaded[s % 2], uses(g, s))
                    if past(g, 2):
                        act.wait_ge(back_done, g - 1)
                    nc.scalar.activation(r[:, s % 2, :], z[:, s % 2, :], ACT.Relu, bias=k.shift2[:, 0:1], scale=k.scale2[:, 0:1]).then_inc(relued, 1)

                def group(g, s):
                    back(relu, act, g, s, 0)
                    back(nm.square, act, g, s, 1)
                    back(nm.deviation, act, g, s, 2)
                by_group(act, group, 2)

            @block.tensor
            def _(t):
                def group(g, s):
                    if past(g, 2):
                        t.wait_ge(added, g - 1)
                    wait_apart(t, relued, g + 1, passed)
                    for j in range(J):
                        last = nc.tensor.transpose(ps_b[s % 2][:, j * D:(j + 1) * D], r[:, s % 2, j * P:(j + 1) * P], k.ident[0:D, 0:D])
                    last.then_inc(back_done, 1)
                by_group(t, group)

            @block.vector
            def _(dve):
                def add(dve, g, s):
                    dve.wait_ge(back_done, g + 1)
                    dve.wait_ge(x_loaded[s % 2], uses(g, s))
                    nc.vector.tensor_tensor(x1[:, s % 2, :], xin[:, s % 2, :], ps_b[s % 2][:, :], ALU.add).then_inc(added, 1)

                def normal(dve, g, s):
                    dve.wait_ge(added, g + 1)
                    nm.add_up(dve, g, s, tiles(x1[:, s % 2, :]))
                    if past(g, 2):
                        dve.wait_ge(y_stored[s % 2], uses(g, s) - 16)
                    nc.vector.tensor_tensor(tiles(y[:, s % 2, :]), tiles(x1[:, s % 2, :]), k.final_b[:, :].unsqueeze(1).to_broadcast([P, J, D]), ALU.add).then_inc(y_done, 1)
                    nm.center(dve, g, s, tiles(x1[:, s % 2, :]))

                def group(g, s):
                    back(add, dve, g, s, 0)
                    back(nm.variance, dve, g, s, 2)
                    back(normal, dve, g, s, 1)
                    back(nm.scale, dve, g, s, 3)
                by_group(dve, group, 3)

            @block.gpsimd
            def _(pool):
                def store(g, s):
                    wait_apart(pool, y_done, g + 1, store_seen)
                    pool.dma_start(rows(y_tab, g), y[:, s % 2, :]).then_inc(y_stored[s % 2], 16)
                    back(store_h, pool, g, s, 2)

                def store_h(pool, g, s):
                    wait_apart(pool, nm.h_done, g + 1, store_seen)
                    pool.dma_start(rows(h_tab, g), nm.h[:, s % 2].rearrange("p j d -> p (j d)")).then_inc(h_stored[s % 2], 16)

                def group(g, s):
                    if not isinstance(g, int) or g < G:
                        store(g, s)
                    else:
                        back(store_h, pool, g, s, 2)
                by_group(pool, group, 2)
                all_stored(pool, h_stored)
                all_stored(pool, y_stored)


def load_parameters(nc, k, a):
    with Scope(nc, "par") as s:
        wn = s.sb("wn", [D, 13, D])
        ps = [s.ps(f"w{i}", [P, 512]) for i in range(2)]
        loaded = s.sem("loaded")
        turned = s.sem("turned")
        eps_done = s.sem("eps_done")
        n = [0]
        col = lambda v: v.rearrange("(p o) -> p o", o=1)
        row = lambda v, cnt: v.rearrange("(o n) -> o n", o=1).to_broadcast([P, cnt])
        with nc.Block() as block:

            @block.sync
            def _(sp):
                def load(to, of):
                    n[0] += 1
                    sp.dma_start(to, of).then_inc(loaded, 16)
                for i, w in enumerate(("root_w", "lin1_w", "lin2_w")):
                    load(wn[:, 3 * i:3 * i + 3, :], a["L1_gnn_" + w].rearrange("l o i -> o l i"))
                load(wn[:, 9:13, :], a["L1_gnn_final_w"].rearrange("o (l i) -> o l i", l=4))
                load(k.w1[:, :], a["L0_gnn_W1"])
                load(k.w2[:, :], a["L0_gnn_W2"])
                for to, of in ((k.b1, "b1"), (k.gamma1, "gamma1"), (k.beta1, "beta1"), (k.b2, "b2"), (k.gamma2, "gamma2"), (k.beta2, "beta2")):
                    load(to[:, :], col(a["L0_gnn_" + of]))
                load(k.one_eps[:, :], row(a["L0_gnn_eps"], 1))
                load(k.final_b[:, :], row(a["L1_gnn_final_b"], D))
                for l in range(LAYERS):
                    load(k.root_b[:, l, :], a["L1_gnn_root_b"][l:l + 1, :].to_broadcast([P, D]))
                sp.wait_ge(loaded, 16 * n[0])

            @block.tensor
            def _(t):
                t.wait_ge(loaded, 16 * 17)
                for i in range(13):
                    last = nc.tensor.transpose(ps[i // 8][0:D, (i % 8) * D:(i % 8 + 1) * D], wn[:, i, :], k.ident[0:D, 0:D])
                last.then_inc(turned, 1)

            @block.vector
            def _(dve):
                dve.wait_ge(turned, 1)
                f = lambda i: ps[i // 8][0:D, (i % 8) * D:(i % 8 + 1) * D]
                for l in range(4):
                    nc.vector.tensor_copy(k.wt[:, 2 * l, :], f(9 + l))
                    if l < 3:
                        nc.vector.tensor_copy(k.wt[:, 2 * l + 1, :], f(l))
                for i in range(6):
                    nc.vector.tensor_copy(k.wt[:, 7 + i, :], f(3 + i))
                nc.vector.memset(k.eps[:, :], EPS)
                nc.vector.tensor_scalar(k.one_eps[:, :], k.one_eps[:, :], 1.0, None, ALU.add)


class Kept:

    def __init__(self, s):
        self.iota = s.sb("iota", [P, T])
        self.iotap = s.sb("iotap", [P, 1])
        self.ident = s.sb("ident", [P, P])
        self.inv = s.sb("inv", [P, 2, T])
        self.other = s.sb("other", [P, 2, C], I32)
        self.number = s.sb("number", [P, C], I32)
        self.pa = s.sb("pa", [P, 2, T])
        self.pb = s.sb("pb", [P, 2, C])
        self.keep = s.sb("keep", [P, 2, C])
        self.offs = s.sb("offs", [1, 2, 2, T], I32)
        self.w1 = s.sb("w1", [D, 2 * D])
        self.w2 = s.sb("w2", [2 * D, D])
        self.wt = s.sb("wt", [D, 13, D])
        self.b1, self.gamma1, self.beta1, self.scale1, self.shift1 = (
            s.sb(name, [2 * D, 1]) for name in ("b1", "gamma1", "beta1", "scale1", "shift1"))
        self.b2, self.gamma2, self.beta2, self.scale2, self.shift2 = (
            s.sb(name, [D, 1]) for name in ("b2", "gamma2", "beta2", "scale2", "shift2"))
        self.one_eps = s.sb("one_eps", [P, 1])
        self.final_b = s.sb("final_b", [P, D])
        self.root_b = s.sb("root_b", [P, LAYERS, D])
        self.eps = s.sb("eps", [P, 1])

    def wt_pair(self, layer):
        if layer == LAYERS:
            return self.wt[:, 6, :]
        return self.wt[:, 2 * layer:2 * layer + 2, :].rearrange("p a d -> p (a d)")


def build(nc, a, out):
    with Scope(nc, "kept") as s:
        k = Kept(s)
        k.tab = [nc.dram_tensor(f"tab{i}", (NP, D), F32, kind="Internal").ap() for i in range(2)]
        z_tab = nc.dram_tensor("z_tab", (NP, D), F32, kind="Internal").ap()
        y_tab = nc.dram_tensor("y_tab", (NP, D), F32, kind="Internal").ap()
        spill = nc.dram_tensor("spill", (P, C * D), F32, kind="Internal").ap()
        z_t = nc.dram_tensor("z_t", (G, D, J * P), F32, kind="Internal").ap()
        k.dbg = (z_tab, y_tab, z_t)
        sort_edges(nc, k, a["src"], a["dst"])
        load_parameters(nc, k, a)
        normalise_input(nc, k, a["x"], k.tab[0])
        with Scope(nc, "msg") as m:
            k.msg = [m.sb("first", [P, (C + 1) * D])]
            k.carry = m.sb("carry", [P, (C + 1) * D])
            gather_edges_and_attributes(nc, k, k.tab[0], a["edge_attr_64"])
            mix_nodes(nc, k, z_t)
        second_product(nc, k, z_t)
        finish_first(nc, k, a["x"], z_t, y_tab, k.tab[1])
        with Scope(nc, "msgs") as m:
            k.msg = [m.sb(f"of{d}", [P, (C + 1) * D]) for d in range(2)]
            k.carry = m.sb("carry", [P, (C + 1) * D])
            for l in range(LAYERS):
                h_in, h_out = k.tab[(l + 1) % 2], k.tab[l % 2]
                gather_first(nc, k, l, h_in, z_tab, y_tab)
                gather_second(nc, k, l, h_in, z_tab, spill)
                finish_layer(nc, k, z_tab, h_out, spill)
        last_product(nc, k, k.tab[(LAYERS + 1) % 2], y_tab, out)


_INS = ["x", "src", "dst", "edge_attr_64", "L0_gnn_eps", "L0_gnn_W1", "L0_gnn_b1", "L0_gnn_gamma1", "L0_gnn_beta1",
        "L0_gnn_W2", "L0_gnn_b2", "L0_gnn_gamma2", "L0_gnn_beta2", "L1_gnn_lin1_w", "L1_gnn_lin2_w", "L1_gnn_root_w",
        "L1_gnn_root_b", "L1_gnn_final_w", "L1_gnn_final_b"]


def kernel(**inputs):
    import numpy as np
    import concourse.bacc as bacc
    from concourse.bass_utils import run_bass_kernel_spmd

    nc = bacc.Bacc("TRN2", target_bir_lowering=False, num_devices=1)
    arrays, args = {}, {}
    for name in _INS:
        v = np.ascontiguousarray(inputs[name])
        arrays[f"in_{name}"] = v
        args[name] = nc.dram_tensor(f"in_{name}", v.shape, mybir.dt.from_np(v.dtype), kind="ExternalInput").ap()
    out = nc.dram_tensor("out", (N, D), F32, kind="ExternalOutput").ap()
    build(nc, args, out)
    return run_bass_kernel_spmd(nc, [arrays], core_ids=[0]).results[0]["out"]
```

```python
from contextlib import ExitStack

import concourse.bass as bass
from concourse import mybir

F32 = mybir.dt.float32
F16 = mybir.dt.float16
I32 = mybir.dt.int32
ALU = mybir.AluOpType
ACT = mybir.ActivationFunctionType
AX_X = mybir.AxisListType.X

P = 128
D = 64
N = 50000
E = 25000
C = 196
J = 8
H = J // 2
G = 49
T = G * J
B = C // G
NP = T * P
LAST = (N - (G - 1) * P * J) // J
PAD = NP - 1
LAYERS = 3
W_ROW = D + 4
EPS = 1e-5
PARAMETER_LOADS = 21
WARM_UP = 24
KEEP_WARM = 6


def wait_apart(eng, sem, value, passed):
    eng.wait_ge(sem, value)
    eng.sem_inc(passed, 1)


class Chain:

    def __init__(self, eng, sem):
        self.eng, self.sem, self.n = eng, sem, 0

    def add(self, ins):
        self.n += 1
        ins.then_inc(self.sem, 1)
        return self.n

    def link(self, ins):
        self.add(ins)
        self.eng.wait_ge(self.sem, self.n)


class Scope:

    count = 0

    def __init__(self, nc, name):
        Scope.count += 1
        self.nc, self.name, self.ctx = nc, f"{name}{Scope.count}", ExitStack()
        self.sems = []

    def __enter__(self):
        self.ctx.__enter__()
        return self

    def __exit__(self, *a):
        if self.sems:
            self.nc.clear_and_free_semaphores(self.sems)
            self.nc.all_engine_barrier()
        return self.ctx.__exit__(*a)

    def sb(self, name, shape, dt=F32):
        return self.ctx.enter_context(self.nc.sbuf_tensor(f"{self.name}_{name}", shape, dt))

    def ps(self, name, shape, dt=F32):
        return self.ctx.enter_context(self.nc.psum_tensor(f"{self.name}_ps_{name}", shape, dt))

    def sem(self, name):
        self.sems.append(self.nc.alloc_semaphore(name=f"{self.name}_sem_{name}"))
        return self.sems[-1]


def by_group(eng, body, late=0):
    for g in range(8):
        body(g, g % 4)
    with eng.Fori(2, G // 4) as i:
        for s in range(4):
            body(4 * i + s, s)
    for g in range(G - 1, G + late):
        body(g, g % 4)


def past(g, n):
    return not isinstance(g, int) or g >= n


def back(stage, eng, g, s, lag):
    if not isinstance(g, int) or 0 <= g - lag < G:
        stage(eng, g - lag, (s - lag) % 4)


def uses(g, s):
    return (g - s % 2) * 8 + 16


def rows(table, g):
    v = table.rearrange("(g p f) d -> g p (f d)", p=P, f=J)
    return v[bass.ds(g, 1), :, :].rearrange("a p f -> (a p) f")


def outer_rows(nc, x, g):
    if isinstance(g, int) and g == G - 1:
        return x[(G - 1) * P * J:N, :].rearrange("(p f) d -> p (f d)", f=J)
    return rows(x[0:(G - 1) * P * J, :], g)


def lanes(g):
    return LAST if isinstance(g, int) and g == G - 1 else P


class Sorting:

    def __init__(self, nc, s):
        self.key = s.sb("key", [P, 2, C], I32)
        self.tile = s.sb("tile", [P, 2, C])
        self.lane = s.sb("lane", [P, 2, C])
        self.base = s.sb("base", [P, 2, T])
        self.total = s.sb("total", [P, 2, T])
        self.front = s.sb("front", [P, T])
        self.rank = s.sb("rank", [P, C])
        self.spot = s.sb("spot", [P, C], I32)
        self.pay = s.sb("pay", [P, C, 4])
        self.tables = [nc.dram_tensor(f"sorted{d}", (P * C, w), F32, kind="Internal").ap() for d, w in enumerate((W_ROW, 4))]
        self.iota = s.sb("iota", [P, T])
        self.iota16 = s.sb("iota16", [P, T], F16)
        self.offs = s.sb("offs", [1, 1, T], I32)
        self.below = s.sb("below", [P, P], F16)
        self.upto = s.sb("upto", [P, P], F16)
        self.ones = s.sb("ones", [P, T])
        self.row0 = s.sb("row0", [P, P])
        self.row127 = s.sb("row127", [P, P])


def chunk(g, i):
    return 2 * g + i // 2 + (C // 2) * (i % 2)


class Count:

    def __init__(self, nc, k, so, s, d):
        self.nc, self.k, self.so, self.d = nc, k, so, d
        self.oh_lane = s.sb("oh_lane", [P, 4, P], F16)
        self.oh_tile = s.sb("oh_tile", [P, 4, T], F16)
        self.half = s.sb("half", [P, 2, T])
        self.deg = s.sb("deg", [P, T])
        self.scan = s.sb("scan", [P, T])
        self.ps = [s.ps(f"count{h}", [P, 512]) for h in range(2)]
        self.hot = s.sem("count_hot")
        self.used = s.sem("count_used")
        self.deg_ready = s.sem("deg_ready")
        self.added = s.sem("count_added")
        self.order = s.sem("count_order")

    def one_hot(self, dve, g, s):
        so, d = self.so, self.d
        for i in range(4):
            if past(g, 1):
                dve.wait_ge(self.used, 4 * g + i - 3)
            c = bass.ds(chunk(g, i), 1)
            self.nc.vector.tensor_scalar(self.oh_lane[:, i, :], so.iota16[:, 0:P], so.lane[:, d, c], None, ALU.is_equal)
            self.nc.vector.tensor_scalar(self.oh_tile[:, i, :], so.iota16[:, :], so.tile[:, d, c], None, ALU.is_equal).then_inc(self.hot, 1)

    def add(self, t, g, s):
        for i in range(4):
            t.wait_ge(self.hot, 4 * g + i + 1)
            self.nc.tensor.matmul(self.ps[i % 2][:, 0:T], self.oh_lane[:, i, :], self.oh_tile[:, i, :], start=not past(g, 1) and i < 2,
                                  stop=isinstance(g, int) and g == G - 1 and i >= 2).then_inc(self.used, 1)

    def read(self, dve):
        nc, k, d = self.nc, self.k, self.d
        ch = Chain(dve, self.order)
        dve.wait_ge(self.used, C)
        nc.vector.tensor_copy(self.half[:, 0, :], self.ps[0][:, 0:T])
        ch.link(nc.vector.tensor_copy(self.half[:, 1, :], self.ps[1][:, 0:T]))
        nc.vector.tensor_tensor(self.deg[:, :], self.half[:, 0, :], self.half[:, 1, :], ALU.add).then_inc(self.deg_ready, 1)
        dve.wait_ge(self.deg_ready, 1)
        ch.link(nc.vector.tensor_scalar(k.inv[:, d, :], self.deg[:, :], 1.0, None, ALU.max))
        nc.vector.reciprocal(k.inv[:, d, :], k.inv[:, d, :])

    def add_lanes(self, t):
        t.wait_ge(self.deg_ready, 1)
        self.nc.tensor.matmul(self.ps[0][:, 0:T], self.so.ones[:, 0:P], self.half[:, 0, :], start=True, stop=True)
        self.nc.tensor.matmul(self.ps[1][:, 0:T], self.so.ones[:, 0:P], self.deg[:, :], start=True, stop=True).then_inc(self.added, 1)

    def bases(self, dve, done):
        nc, so, d = self.nc, self.so, self.d
        dve.wait_ge(self.added, 1)
        nc.vector.tensor_copy(so.front[:, :], self.ps[0][:, 0:T])
        nc.vector.tensor_copy(so.total[:, d, :], self.ps[1][:, 0:T])
        nc.vector.tensor_tensor_scan(self.scan[:, :], so.ones[:, :], self.ps[1][:, 0:T], 0.0, ALU.mult, ALU.add).then_inc(self.order, 1)
        dve.wait_ge(self.order, 3)
        nc.vector.tensor_tensor(so.base[:, d, :], self.scan[:, :], so.total[:, d, :], ALU.subtract).then_inc(done, 1)


class Rank:

    def __init__(self, nc, k, so, s, d):
        self.nc, self.k, self.so, self.d = nc, k, so, d
        self.oh = s.sb("rank_oh", [P, 16, T], F16)
        self.start = s.sb("start", [P, T])
        self.junk = s.sb("junk", [P, 4, T])
        self.whole = s.sb("whole", [P, C], I32)
        self.part = s.sb("part", [P, 2, C], I32)
        self.part_f = s.sb("part_f", [P, 2, C])
        self.ps = [s.ps(f"rank{h}", [P, 512]) for h in range(2)]
        self.based = s.sem("based")
        self.hot = s.sem("rank_hot")
        self.prefixed = s.sem("prefixed")
        self.ranked = s.sem("ranked")
        self.passed = s.sem("chunk_passed")
        self.order = s.sem("rank_order")

    def second_start(self, dve):
        self.nc.vector.tensor_tensor(self.start[:, :], self.so.base[:, self.d, :], self.so.front[:, :], ALU.add).then_inc(self.based, 1)

    def begin(self, t):
        t.wait_ge(self.based, 1)
        self.nc.tensor.matmul(self.ps[0][:, 0:T], self.k.ident[:, :], self.so.base[:, self.d, :], start=True, stop=True)
        self.nc.tensor.matmul(self.ps[1][:, 0:T], self.k.ident[:, :], self.start[:, :], start=True, stop=True)

    def one_hot(self, dve, g, s):
        for i in range(4):
            if past(g, 4):
                dve.wait_ge(self.passed, 4 * g + i - 15)
            self.nc.vector.tensor_scalar(self.oh[:, 4 * s + i, :], self.so.iota16[:, :], self.so.tile[:, self.d, bass.ds(chunk(g, i), 1)], None, ALU.is_equal).then_inc(self.hot, 1)

    def prefix(self, t, g, s):
        for i in range(4):
            n = 4 * g + i
            slot = 4 * s + i
            t.wait_ge(self.hot, n + 1)
            self.nc.tensor.matmul(self.ps[i % 2][:, 0:T], self.so.below[:, :], self.oh[:, slot, :], start=False, stop=True, skip_group_check=True).then_inc(self.prefixed, 1)
            if past(g, 1) or i > 0:
                t.wait_ge(self.ranked, n)
                self.nc.tensor.matmul(self.ps[1 - i % 2][:, 0:T], self.so.upto[:, :], self.oh[:, (slot - 1) % 16, :], start=False, stop=True, skip_group_check=True).then_inc(self.passed, 1)

    def read(self, dve, g, s):
        for i in range(4):
            n = 4 * g + i
            dve.wait_ge(self.prefixed, n + 1)
            if past(g, 1):
                dve.wait_ge(self.ranked, n - 3)
            c = bass.ds(chunk(g, i), 1)
            self.nc.vector.scalar_tensor_tensor(out=self.junk[:, i, :], in0=self.so.iota[:, :], scalar=self.so.tile[:, self.d, c], in1=self.ps[i % 2][:, 0:T],
                                                op0=ALU.is_equal, op1=ALU.mult, accum_out=self.so.rank[:, c]).then_inc(self.ranked, 1)

    def spots(self, dve):
        nc, so, d = self.nc, self.so, self.d
        ch = Chain(dve, self.order)
        dve.wait_ge(self.ranked, C)
        nc.vector.tensor_copy(so.pay[:, :, 0], so.key[:, 1 - d, :])
        nc.vector.tensor_copy(so.pay[:, :, 1], so.key[:, d, :])
        nc.vector.memset(so.pay[:, :, 2:4], 0.0)
        ch.link(nc.vector.tensor_copy(self.whole[:, :], so.rank[:, :]))
        nc.vector.tensor_scalar(self.part[:, 0, :], self.whole[:, :], 127, None, ALU.bitwise_and)
        ch.link(nc.vector.tensor_scalar(self.part[:, 1, :], self.whole[:, :], 7, None, ALU.logical_shift_right))
        ch.link(nc.vector.tensor_copy(self.part_f[:, :, :], self.part[:, :, :]))
        ch.link(nc.vector.scalar_tensor_tensor(out=self.part_f[:, 1, :], in0=self.part_f[:, 0, :], scalar=float(C), in1=self.part_f[:, 1, :], op0=ALU.mult, op1=ALU.add))
        nc.vector.tensor_copy(so.spot[:, :], self.part_f[:, 1, :])


class Scatter:

    def __init__(self, nc, so, s, d):
        self.nc, self.so, self.d = nc, so, d
        self.w = W_ROW if d == 0 else 4
        self.idx = s.sb("spot_idx", [P, 4, B], I32)
        self.pay = s.sb("spot_pay", [P, 4, B, self.w])
        if d == 0:
            self.attr_staged = s.sem("attr_staged")
        self.staged = s.sem("spot_staged")
        self.seen = s.sem("spot_seen")
        self.scattered = [s.sem(f"scattered{u}") for u in range(4)]

    def stage_attributes(self, act, g, s):
        if past(g, 4):
            act.wait_ge(self.scattered[s], (g - s) * 4 * B)
        self.nc.scalar.copy(self.pay[:, s, :, 0:D], self.so.attr[:, bass.ds(B * g, B), :]).then_inc(self.attr_staged, 1)

    def scatter(self, pool, g, s):
        if past(g, 4):
            pool.wait_ge(self.scattered[s], (g - s) * 4 * B)
        self.nc.gpsimd.tensor_copy(self.idx[:, s, :], self.so.spot[:, bass.ds(B * g, B)])
        self.nc.gpsimd.tensor_copy(self.pay[:, s, :, self.w - 4:self.w], self.so.pay[:, bass.ds(B * g, B), :]).then_inc(self.staged, 1)
        wait_apart(pool, self.staged, g + 1, self.seen)
        if self.d == 0:
            wait_apart(pool, self.attr_staged, g + 1, self.seen)
        for q in range(B):
            self.nc.gpsimd.indirect_dma_start(out=self.so.tables[self.d], out_offset=bass.IndirectOffsetOnAxis(ap=self.idx[:, s, q:q + 1], axis=0), in_=self.pay[:, s, q, :], in_offset=None).then_inc(self.scattered[s], 16)

    def end(self, pool):
        for s in range(4):
            pool.wait_ge(self.scattered[s], ((G - 1 - s) // 4 + 1) * 16 * B)


def rank_first(nc, k, so, src, dst, edge_attr):
    with Scope(nc, "rank") as s:
        t_i = s.sb("t_i", [P, 2, C], I32)
        low_i = s.sb("low_i", [P, 2, C], I32)
        lane_i = s.sb("lane_i", [P, 2, C], I32)
        eq = s.sb("eq", [P, 2])
        iota_i = s.sb("iota_i", [P, T], I32)
        iotap_i = s.sb("iotap_i", [P, 1], I32)
        loaded = s.sem("loaded")
        memset_done = s.sem("memset_done")
        iota_done = s.sem("iota_done")
        v = s.sem("v")
        based = s.sem("base_done")
        attr_cleared = s.sem("attr_cleared")
        attr_here = s.sem("attr_here")
        ct = Count(nc, k, so, s, 0)
        rk = Rank(nc, k, so, s, 0)

        with nc.Block() as block:

            @block.sync
            def _(sp):
                sp.wait_ge(memset_done, 1)
                for d, ends_of in enumerate((dst, src)):
                    sp.dma_start(so.key[0:127, d, :], ends_of[0:127 * C].rearrange("(p c) -> p c", c=C)).then_inc(loaded, 16)
                    sp.dma_start(so.key[127:128, d, 0:E - 127 * C], ends_of[127 * C:E].rearrange("(p c) -> p c", p=1)).then_inc(loaded, 16)
                sp.wait_ge(attr_cleared, 1)
                sp.dma_start(so.attr[0:127, :, :], edge_attr[0:127 * C, :].rearrange("(p c) d -> p c d", c=C)).then_inc(attr_here, 16)
                sp.dma_start(so.attr[127:128, 0:E - 127 * C, :], edge_attr[127 * C:E, :].rearrange("(p c) d -> p c d", p=1)).then_inc(attr_here, 16)
                sp.wait_ge(attr_here, 32)

            @block.gpsimd
            def _(pool):
                nc.gpsimd.iota(iota_i[:, :], [[1, T]], base=0, channel_multiplier=0).then_inc(iota_done, 1)
                nc.gpsimd.iota(iotap_i[:, :], [[1, 1]], base=0, channel_multiplier=1).then_inc(iota_done, 1)
                nc.gpsimd.memset(so.attr[:, :, :], 0.0).then_inc(attr_cleared, 1)

            @block.vector
            def _(dve):
                ch = Chain(dve, v)
                nc.vector.memset(so.key[:, :, :], PAD).then_inc(memset_done, 1)
                ch.link(nc.vector.memset(so.ones[:, :], 1.0))
                dve.wait_ge(iota_done, 2)
                nc.vector.tensor_copy(so.iota[:, :], iota_i[:, :])
                nc.vector.tensor_copy(k.lanes[:, :], iota_i[:, 0:P])
                nc.vector.tensor_copy(so.iota16[:, :], iota_i[:, :])
                ch.link(nc.vector.tensor_copy(k.iotap[:, :], iotap_i[:, :]))
                nc.vector.tensor_scalar(k.ident[:, :], so.iota[:, 0:P], k.iotap[:, 0:1], None, ALU.is_equal)
                nc.vector.tensor_scalar(so.below[:, :], so.iota[:, 0:P], k.iotap[:, 0:1], None, ALU.is_gt)
                nc.vector.tensor_scalar(so.upto[:, :], so.iota[:, 0:P], k.iotap[:, 0:1], None, ALU.is_le)
                nc.vector.tensor_scalar(eq[:, 0:1], k.iotap[:, :], 0.0, None, ALU.is_equal)
                ch.link(nc.vector.tensor_scalar(eq[:, 1:2], k.iotap[:, :], 127.0, None, ALU.is_equal))
                nc.vector.tensor_scalar(so.row0[:, :], so.ones[:, 0:P], eq[:, 0:1], None, ALU.mult)
                nc.vector.tensor_scalar(so.row127[:, :], so.ones[:, 0:P], eq[:, 1:2], None, ALU.mult)
                dve.wait_ge(loaded, 64)
                nc.vector.tensor_scalar(t_i[:, :, :], so.key[:, :, :], 10, 3, ALU.logical_shift_right, ALU.logical_shift_left)
                nc.vector.tensor_scalar(low_i[:, :, :], so.key[:, :, :], 7, None, ALU.bitwise_and)
                ch.link(nc.vector.tensor_scalar(lane_i[:, :, :], so.key[:, :, :], 3, 127, ALU.logical_shift_right, ALU.bitwise_and))
                ch.link(nc.vector.tensor_tensor(t_i[:, :, :], t_i[:, :, :], low_i[:, :, :], ALU.bitwise_or))
                nc.vector.tensor_copy(so.tile[:, :, :], t_i[:, :, :])
                ch.link(nc.vector.tensor_copy(so.lane[:, :, :], lane_i[:, :, :]))
                by_group(dve, lambda g, s: ct.one_hot(dve, g, s))
                ct.read(dve)
                ct.bases(dve, based)
                dve.wait_ge(based, 1)
                rk.second_start(dve)

                def group(g, s):
                    back(rk.one_hot, dve, g, s, 0)
                    back(rk.read, dve, g, s, 1)
                by_group(dve, group, 1)
                rk.spots(dve)

            @block.tensor
            def _(t):
                by_group(t, lambda g, s: ct.add(t, g, s))
                ct.add_lanes(t)
                rk.begin(t)
                by_group(t, lambda g, s: rk.prefix(t, g, s))


def sorted_tables(nc, k, so, d, rows_of):
    with Scope(nc, "tables") as s:
        key = s.sb("key", [P, C], I32)
        t_i = s.sb("t_i", [P, C], I32)
        low_i = s.sb("low_i", [P, C], I32)
        lane_i = s.sb("lane_i", [P, C], I32)
        lane = s.sb("lane", [P, C])
        tsort = s.sb("tsort", [P, C])
        code = s.sb("code", [P, C])
        code_t = s.sb("code_t", [98, 2, P])
        sel = s.sb("sel", [98, 2, T])
        c0_i = s.sb("c0_i", [P, T], I32)
        c0 = s.sb("c0", [P, T])
        cl_i = s.sb("cl_i", [P, T], I32)
        cl = s.sb("cl", [P, T])
        more = s.sb("more", [P, T])
        ends = s.sb("ends", [P, 2, C])
        cont = s.sb("cont", [P, C])
        ps_e = s.ps("ends", [P, 512])
        ps_x = s.ps("x", [P, 512])
        ps_y = s.ps("y", [P, 512])
        fetched = s.sem("fetched")
        v = s.sem("v")
        code_ready = s.sem("code_ready")
        turned = s.sem("turned")
        sel_ready = s.sem("sel_ready")
        tables_ps = s.sem("tables_ps")
        base, total, pb, keep = so.base[:, d, :], so.total[:, d, :], k.pb[:, d, :], k.keep[:, d, :]

        with nc.Block() as block:

            @block.sync
            def _(sp):
                sp.dma_start(rows_of[:, :, :], so.tables[d].rearrange("(p c) w -> p c w", c=C)).then_inc(fetched, 16)

            @block.vector
            def _(dve):
                ch = Chain(dve, v)
                ch.link(nc.vector.tensor_copy(c0_i[:, :], base))
                ch.link(nc.vector.tensor_scalar(c0_i[:, :], c0_i[:, :], 7, None, ALU.logical_shift_right))
                ch.link(nc.vector.tensor_copy(c0[:, :], c0_i[:, :]))
                ch.link(nc.vector.tensor_scalar(c0[:, :], c0[:, :], float(C - 1), None, ALU.min))
                ch.link(nc.vector.tensor_tensor(cl[:, :], base, total, ALU.add))
                ch.link(nc.vector.tensor_scalar(cl[:, :], cl[:, :], 1.0, 0.0, ALU.subtract, ALU.max))
                ch.link(nc.vector.tensor_copy(cl_i[:, :], cl[:, :]))
                ch.link(nc.vector.tensor_scalar(cl_i[:, :], cl_i[:, :], 7, None, ALU.logical_shift_right))
                ch.link(nc.vector.tensor_copy(cl[:, :], cl_i[:, :]))
                ch.link(nc.vector.tensor_tensor(more[:, :], cl[:, :], c0[:, :], ALU.is_gt))
                ch.link(nc.vector.scalar_tensor_tensor(out=cl[:, :], in0=cl[:, :], scalar=1.0, in1=more[:, :], op0=ALU.add, op1=ALU.mult))
                nc.vector.tensor_scalar(k.offs[:, d, 0, :], c0[0:1, :], float(D), None, ALU.mult)
                if d == 0:
                    nc.vector.tensor_scalar(so.offs[:, 0, :], c0[0:1, :], float(W_ROW), None, ALU.mult)
                nc.vector.tensor_scalar(k.offs[:, d, 1, :], cl[0:1, :], float(D), None, ALU.mult)
                for h in range(2):
                    nc.vector.tensor_scalar(sel[:, h, :], c0[0:98, :], k.iotap[0:98, 0:1], float(98 * h), ALU.subtract, ALU.is_equal)
                dve.wait_ge(fetched, 16)
                at = D if d == 0 else 0
                nc.vector.tensor_copy(k.other[:, d, :], rows_of[:, :, at])
                ch.link(nc.vector.tensor_copy(key[:, :], rows_of[:, :, at + 1]))
                nc.vector.tensor_scalar(t_i[:, :], key[:, :], 10, 3, ALU.logical_shift_right, ALU.logical_shift_left)
                nc.vector.tensor_scalar(lane_i[:, :], key[:, :], 3, 127, ALU.logical_shift_right, ALU.bitwise_and)
                ch.link(nc.vector.tensor_scalar(low_i[:, :], key[:, :], 7, None, ALU.bitwise_and))
                ch.link(nc.vector.tensor_tensor(t_i[:, :], t_i[:, :], low_i[:, :], ALU.bitwise_or))
                nc.vector.tensor_copy(lane[:, :], lane_i[:, :])
                ch.link(nc.vector.tensor_copy(tsort[:, :], t_i[:, :]))
                nc.vector.scalar_tensor_tensor(out=code[:, :], in0=tsort[:, :], scalar=128.0, in1=lane[:, :], op0=ALU.mult, op1=ALU.add).then_inc(code_ready, 1)
                dve.wait_ge(turned, 1)
                nc.vector.tensor_copy(ends[:, :, :], ps_e[:, 0:2 * C].rearrange("p (w c) -> p w c", w=2))
                nc.vector.tensor_copy(code_t[:, :, :], ps_y[0:98, 0:2 * P].rearrange("p (w c) -> p w c", w=2)).then_inc(sel_ready, 1)
                dve.wait_ge(sel_ready, 1)
                ch.link(nc.vector.memset(cont[:, 0:1], 0.0))
                ch.link(nc.vector.tensor_tensor(cont[:, 1:C], ends[:, 1, 0:C - 1], ends[:, 0, 1:C], ALU.is_equal))
                ch.link(nc.vector.scalar_tensor_tensor(out=pb, in0=ends[:, 0, :], scalar=-128.0, in1=code[:, :], op0=ALU.mult, op1=ALU.add))
                ch.link(nc.vector.scalar_tensor_tensor(out=pb, in0=pb, scalar=1.0, in1=cont[:, :], op0=ALU.add, op1=ALU.mult))
                ch.link(nc.vector.tensor_scalar(pb, pb, -1.0, None, ALU.add))
                ch.link(nc.vector.memset(keep[:, 0:1], 0.0))
                ch.link(nc.vector.tensor_tensor(keep[:, 1:C], ends[:, 0, 0:C - 1], ends[:, 0, 1:C], ALU.is_equal))
                ch.link(nc.vector.tensor_tensor(keep[:, 1:C], keep[:, 1:C], cont[:, 1:C], ALU.mult))
                dve.wait_ge(tables_ps, 1)
                nc.vector.scalar_tensor_tensor(out=k.pa[:, d, :], in0=so.iota[:, :], scalar=-128.0, in1=ps_x[:, 0:T], op0=ALU.mult, op1=ALU.add)

            @block.tensor
            def _(t):
                t.wait_ge(code_ready, 1)
                for h in range(2):
                    nc.tensor.transpose(ps_y[0:98, h * P:(h + 1) * P], code[:, 98 * h:98 * h + 98], k.ident[:, :])
                nc.tensor.matmul(ps_e[:, 0:C], so.row0[:, :], tsort[:, :], start=True, stop=True)
                nc.tensor.matmul(ps_e[:, C:2 * C], so.row127[:, :], tsort[:, :], start=True, stop=True).then_inc(turned, 1)
                t.wait_ge(sel_ready, 1)
                for h in range(2):
                    last = nc.tensor.matmul(ps_x[:, 0:T], code_t[:, h, :], sel[:, h, :], start=h == 0, stop=h == 1)
                last.then_inc(tables_ps, 1)


def warm_up(nc, k, ps, products=WARM_UP):
    for _ in range(products):
        nc.tensor.matmul(ps[:, 0:P], k.ident[:, :], k.ident[:, :], start=True, stop=True)


class Norm:

    def __init__(self, nc, k, s, stored):
        self.nc, self.k, self.stored = nc, k, stored
        self.cent = s.sb("cent", [P, 4, J, D])
        self.sq = s.sb("sq", [P, 2, J, D])
        self.h = s.sb("h", [P, 2, J, D])
        self.sum = s.sb("sum", [P, 2, J])
        self.mean = s.sb("mean", [P, 2, J])
        self.var = s.sb("var", [P, 2, J])
        self.std = s.sb("std", [P, 2, J])
        self.rstd = s.sb("rstd", [P, 2, J])
        self.sum_done = s.sem("sum_done")
        self.mean_done = s.sem("mean_done")
        self.cent_done = s.sem("cent_done")
        self.sq_done = s.sem("sq_done")
        self.var_done = s.sem("var_done")
        self.std_done = s.sem("std_done")
        self.rstd_done = s.sem("rstd_done")
        self.h_done = s.sem("h_done")

    def add_up(self, dve, g, s, x):
        self.nc.vector.tensor_reduce(self.sum[:, s % 2, :], x, mybir.AxisListType.X, ALU.add).then_inc(self.sum_done, 1)
        dve.wait_ge(self.sum_done, g + 1)
        self.nc.vector.tensor_scalar(self.mean[:, s % 2, :], self.sum[:, s % 2, :], 1.0 / D, None, ALU.mult).then_inc(self.mean_done, 1)

    def center(self, dve, g, s, x):
        dve.wait_ge(self.mean_done, g + 1)
        if past(g, 4):
            dve.wait_ge(self.h_done, g - 3)
        self.nc.vector.tensor_tensor(self.cent[:, s], x, self.mean[:, s % 2, :].unsqueeze(2).to_broadcast([P, J, D]), ALU.subtract).then_inc(self.cent_done, 1)

    def square(self, act, g, s):
        act.wait_ge(self.cent_done, g + 1)
        if past(g, 2):
            act.wait_ge(self.var_done, g - 1)
        self.nc.scalar.activation(self.sq[:, s % 2], self.cent[:, s], ACT.Square).then_inc(self.sq_done, 1)

    def variance(self, dve, g, s):
        dve.wait_ge(self.sq_done, g + 1)
        self.nc.vector.tensor_reduce(self.var[:, s % 2, :], self.sq[:, s % 2], mybir.AxisListType.X, ALU.add).then_inc(self.var_done, 1)

    def deviation(self, act, g, s):
        act.wait_ge(self.var_done, g + 1)
        self.nc.scalar.activation(self.std[:, s % 2, :], self.var[:, s % 2, :], ACT.Sqrt, bias=self.k.eps[:, 0:1], scale=1.0 / D).then_inc(self.std_done, 1)

    def scale(self, dve, g, s):
        dve.wait_ge(self.std_done, g + 1)
        self.nc.vector.reciprocal(self.rstd[:, s % 2, :], self.std[:, s % 2, :]).then_inc(self.rstd_done, 1)
        if past(g, 2):
            dve.wait_ge(self.stored[s % 2], uses(g, s) - 16)
        dve.wait_ge(self.rstd_done, g + 1)
        self.nc.vector.scalar_tensor_tensor(out=self.h[:, s % 2], in0=self.cent[:, s], scalar=0.0, in1=self.rstd[:, s % 2, :].unsqueeze(2).to_broadcast([P, J, D]), op0=ALU.max, op1=ALU.mult).then_inc(self.h_done, 1)


def tiles(ap):
    return ap.rearrange("p (j d) -> p j d", d=D)


def all_stored(eng, stored):
    eng.wait_ge(stored[0], (G + 1) // 2 * 16)
    eng.wait_ge(stored[1], G // 2 * 16)


def normalise_input(nc, k, so, x, table):
    with Scope(nc, "ln") as s:
        xin = s.sb("xin", [P, 2, J * D])
        loaded = [s.sem(f"loaded{i}") for i in range(2)]
        stored = [s.sem(f"stored{i}") for i in range(2)]
        sc = Scatter(nc, so, s, 0)
        ct = Count(nc, k, so, s, 1)
        based = s.sem("base_done")
        nm = Norm(nc, k, s, stored)
        with nc.Block() as block:

            @block.sync
            def _(sp):
                def load(sp, g, s):
                    if past(g, 2):
                        sp.wait_ge(nm.cent_done, g - 1)
                    sp.dma_start(xin[0:lanes(g), s % 2, :], outer_rows(nc, x, g)).then_inc(loaded[s % 2], 16)

                def store(sp, g, s):
                    sp.wait_ge(nm.h_done, g + 1)
                    sp.dma_start(rows(table, g), nm.h[:, s % 2].rearrange("p j d -> p (j d)")).then_inc(stored[s % 2], 16)

                def group(g, s):
                    back(load, sp, g, s, 0)
                    back(store, sp, g, s, 2)
                by_group(sp, group, 2)
                all_stored(sp, stored)

            @block.vector
            def _(dve):
                def add_up(dve, g, s):
                    dve.wait_ge(loaded[s % 2], uses(g, s))
                    nm.add_up(dve, g, s, tiles(xin[:, s % 2, :]))

                def group(g, s):
                    back(nm.scale, dve, g, s, 2)
                    back(add_up, dve, g, s, 0)
                    back(nm.variance, dve, g, s, 1)
                    back(lambda dve, g, s: nm.center(dve, g, s, tiles(xin[:, s % 2, :])), dve, g, s, 0)
                    back(ct.one_hot, dve, g, s, 0)
                by_group(dve, group, 2)
                ct.read(dve)
                ct.bases(dve, based)

            @block.scalar
            def _(act):
                def group(g, s):
                    back(nm.deviation, act, g, s, 1)
                    back(nm.square, act, g, s, 0)
                    back(sc.stage_attributes, act, g, s, 0)
                by_group(act, group, 1)

            @block.tensor
            def _(t):
                by_group(t, lambda g, s: ct.add(t, g, s))
                ct.add_lanes(t)

            @block.gpsimd
            def _(pool):
                by_group(pool, lambda g, s: sc.scatter(pool, g, s))
                sc.end(pool)


class Chunks:

    def __init__(self, nc, k, s, d, table, weights=None, own=None, spill=None):
        self.spill = spill
        self.nc, self.k, self.d, self.table, self.weights, self.own = nc, k, d, table, weights, own
        self.land = s.sb("land", [P, 4, B * D])
        self.idx = s.sb("idx", [P, 4, B], I32)
        self.msg = s.sb("msg", [P, 2, B * D])
        self.oh = s.sb("oh_b", [P, 2, B, P])
        self.ps_r = s.ps("r", [P, 512])
        self.indexed = s.sem("indexed")
        self.indices_seen = s.sem("indices_seen")
        self.landed = [s.sem(f"landed{u}") for u in range(4)]
        self.taken = s.sem("taken")
        self.made = s.sem("made")
        self.staged = s.sem("staged")
        self.kept = s.sem("kept")
        self.hot = s.sem("chunk_hot")
        self.summed = s.sem("summed")
        self.sums_kept = s.sem("sums_kept")
        if spill is not None:
            self.sums = s.sb("sums", [P, 2, B * D])
            self.spilled = [s.sem(f"spilled{i}") for i in range(2)]
        if own is None:
            self.rows_t = s.sb("rows_t", [P, B // 2 * P])
            self.ps_t = s.ps("t", [P, 512])
            self.ps_m = s.ps("m", [P, 512])
            self.rows_kept = s.sem("rows_kept")
            self.rows_seen = s.sem("rows_seen")

    def gather(self, pool, g, s):
        nc, k = self.nc, self.k
        if past(g, 4):
            pool.wait_ge(self.taken, g - 3)
        nc.gpsimd.tensor_copy(self.idx[:, s, :], k.other[:, self.d, bass.ds(B * g, B)]).then_inc(self.indexed, 1)
        wait_apart(pool, self.indexed, g + 1, self.indices_seen)
        for q in range(B):
            nc.gpsimd.indirect_dma_start(out=self.land[:, s, q * D:(q + 1) * D], out_offset=None, in_=self.table, in_offset=bass.IndirectOffsetOnAxis(ap=self.idx[:, s, q:q + 1], axis=0)).then_inc(self.landed[s], 16)

    def turn(self, t, g, s):
        if past(g, 1):
            t.wait_ge(self.rows_kept, g)
        wait_apart(t, self.landed[s], (g - s) * 4 * B + 16 * B, self.rows_seen)
        for q in range(B // 2):
            last = self.nc.tensor.transpose(self.ps_t[:, q * P:(q + 1) * P], self.land[:, s, 2 * q * D:2 * (q + 1) * D], self.k.ident[:, :])
        last.then_inc(self.taken, 1)

    def keep_rows(self, act, g, s):
        act.wait_ge(self.taken, g + 1)
        if past(g, 1):
            act.wait_ge(self.made, g)
        self.nc.scalar.copy(self.rows_t[:, :], self.ps_t[:, 0:B // 2 * P]).then_inc(self.rows_kept, 1)

    def transform(self, t, g, s):
        t.wait_ge(self.rows_kept, g + 1)
        if past(g, 1):
            t.wait_ge(self.kept, g)
        for q in range(B):
            last = self.nc.tensor.matmul(self.ps_m[:, q * D:(q + 1) * D], self.rows_t[:, q // 2 * P:(q // 2 + 1) * P], self.weights[:, q % 2 * D:(q % 2 + 1) * D], start=True, stop=True)
        last.then_inc(self.made, 1)

    def keep(self, act, g, s):
        act.wait_ge(self.made, g + 1)
        if past(g, 2):
            act.wait_ge(self.summed, g - 1)
        self.nc.scalar.copy(self.msg[:, s % 2, :], self.ps_m[:, 0:B * D]).then_inc(self.staged, 1)
        self.nc.scalar.copy(self.k.msg[self.d][:, bass.ds(g * (B * D), B * D)], self.ps_m[:, 0:B * D]).then_inc(self.kept, 1)

    def add_own(self, dve, g, s):
        dve.wait_ge(self.landed[s], (g - s) * 4 * B + 16 * B)
        if past(g, 2):
            dve.wait_ge(self.kept, g - 1)
            dve.wait_ge(self.summed, g - 1)
        self.nc.vector.tensor_tensor(tiles(self.msg[:, s % 2, :]), tiles(self.land[:, s, :]), self.own[:, bass.ds(g * B, B), 0:D], ALU.add).then_inc(self.taken, 1)

    def keep_added(self, act, g, s):
        act.wait_ge(self.taken, g + 1)
        self.nc.scalar.copy(self.own[:, bass.ds(g * B, B), 0:D], tiles(self.msg[:, s % 2, :])).then_inc(self.kept, 1)

    def one_hot(self, dve, g, s):
        if past(g, 2):
            dve.wait_ge(self.summed, g - 1)
        self.nc.vector.tensor_tensor(self.oh[:, s % 2], self.k.lanes[:, :].unsqueeze(1).to_broadcast([P, B, P]),
                                     self.k.pb[:, self.d, bass.ds(g * B, B)].unsqueeze(2).to_broadcast([P, B, P]), ALU.is_equal).then_inc(self.hot, 1)

    def sum_up(self, t, g, s):
        t.wait_ge(self.staged if self.own is None else self.taken, g + 1)
        t.wait_ge(self.hot, g + 1)
        if past(g, 1):
            t.wait_ge(self.sums_kept, g)
        for q in range(B):
            last = self.nc.tensor.matmul(self.ps_r[:, q * D:(q + 1) * D], self.oh[:, s % 2, q, :], self.msg[:, s % 2, q * D:(q + 1) * D], start=True, stop=True)
        last.then_inc(self.summed, 1)

    def keep_sums(self, act, g, s):
        act.wait_ge(self.summed, g + 1)
        if self.spill is not None:
            if past(g, 2):
                act.wait_ge(self.spilled[s % 2], uses(g, s) - 16)
            to = self.sums[:, s % 2, :]
        else:
            to = self.k.carry[:, bass.ds(g * (B * D) + D, B * D)]
        self.nc.scalar.copy(to, self.ps_r[:, 0:B * D]).then_inc(self.sums_kept, 1)

    def spill_sums(self, sp, g, s):
        sp.wait_ge(self.sums_kept, g + 1)
        sp.dma_start(self.spill[:, bass.ds(g * (B * D), B * D)], self.sums[:, s % 2, :]).then_inc(self.spilled[s % 2], 16)


def carry_over(nc, k, d):
    nc.vector.memset(k.carry[:, 0:D], 0.0)
    sums = k.carry[:, D:(C + 1) * D].rearrange("p (c f) -> p f c", f=D)
    for f in range(D):
        last = nc.vector.tensor_tensor_scan(sums[:, f, :], k.keep[:, d, :], sums[:, f, :], 0.0, ALU.mult, ALU.add)
    return last


class Tiles:

    def __init__(self, nc, k, s, d, used, direct, msg=None, offs=None):
        self.nc, self.k, self.d, self.used, self.direct = nc, k, d, used, direct
        self.msg = k.msg[d] if msg is None else msg
        self.offs = k.offs[:, d, :, :] if offs is None else offs
        self.halves = [h for h in range(2) if h not in direct]
        self.oh = s.sb("oh", [P, 2, J, P])
        if self.halves:
            self.first = s.sb("first", [P, 2, len(self.halves), H, D])
            self.first_here = s.sem("first_here")
        self.mean = s.sb("mean", [P, 2, J * D])
        self.ps = [s.ps(f"agg{i}", [P, 512]) for i in range(2)]
        self.hot = s.sem("hot")
        self.tiles_done = s.sem("tiles_done")
        self.carried_here = s.sem("carried_here")
        self.summed = s.sem("tile_summed")
        self.mean_done = s.sem("tile_mean_done")

    def offsets(self, engine, which, tile, count):
        _, offs = self.nc.values_load_multi_w_load_instructions(
            (self.offs if which == 0 else self.k.offs[:, self.d, :, :])[0:1, which, bass.ds(tile, count)], engines=[engine], min_val=0,
            max_val=C * D if which == 1 else self.msg.shape[1] - self.msg.shape[1] // C,
            skip_runtime_bounds_check_because="offsets come from ranks clamped to the tables")
        return offs

    def fetch_first(self, eng, copy, g, s):
        for i, h in enumerate(self.halves):
            offs = self.offsets(eng.engine, 0, g * J + h * H, H)
            if past(g, 2):
                eng.wait_ge(self.tiles_done, 2 * g + h - 3)
            for q in range(H):
                last = copy(self.first[:, s % 2, i, q, :], self.msg[:, bass.ds(offs[q], D)])
            last.then_inc(self.first_here, 1)

    def fetch_carried(self, act, g, s):
        offs = self.offsets(act.engine, 1, g * J, J)
        if past(g, 2):
            act.wait_ge(self.used, g - 1)
        for j in range(J):
            last = self.nc.scalar.copy(self.mean[:, s % 2, j * D:(j + 1) * D], self.k.carry[:, bass.ds(offs[j], D)])
        last.then_inc(self.carried_here, 1)

    def one_hot(self, dve, g, s):
        for h in range(2):
            if past(g, 2):
                dve.wait_ge(self.tiles_done, 2 * g + h - 3)
            self.nc.vector.tensor_tensor(self.oh[:, s % 2, h * H:(h + 1) * H, :], self.k.lanes[:, :].unsqueeze(1).to_broadcast([P, H, P]),
                                         self.k.pa[:, self.d, bass.ds(g * J + h * H, H)].unsqueeze(2).to_broadcast([P, H, P]), ALU.is_equal).then_inc(self.hot, 1)

    def sum_tiles(self, t, g, s):
        if past(g, 2):
            t.wait_ge(self.summed, g - 1)
        for h in range(2):
            if h in self.direct:
                offs = self.offsets(t.engine, 0, g * J + h * H, H)
            else:
                i = self.halves.index(h)
                t.wait_ge(self.first_here, len(self.halves) * g + i + 1)
            t.wait_ge(self.hot, 2 * g + h + 1)
            for q in range(H):
                j = h * H + q
                of = self.msg[:, bass.ds(offs[q], D)] if h in self.direct else self.first[:, s % 2, i, q, :]
                last = self.nc.tensor.matmul(self.ps[s % 2][:, j * D:(j + 1) * D], self.oh[:, s % 2, j, :], of, start=True, stop=True)
            last.then_inc(self.tiles_done, 1)

    def take_mean(self, dve, g, s):
        dve.wait_ge(self.tiles_done, 2 * g + 2)
        dve.wait_ge(self.carried_here, g + 1)
        m = self.mean[:, s % 2, :]
        self.nc.vector.tensor_tensor(m, self.ps[s % 2][:, :], m, ALU.add).then_inc(self.summed, 1)
        dve.wait_ge(self.summed, g + 1)
        self.nc.vector.tensor_tensor(tiles(m), tiles(m), self.k.inv[:, self.d, bass.ds(g * J, J)].unsqueeze(2).to_broadcast([P, J, D]), ALU.mult).then_inc(self.mean_done, 1)


class Combine:

    def __init__(self, nc, k, s, d, z, target, relu, direct):
        self.nc, self.z, self.target, self.relu = nc, z, target, relu
        self.added = s.sem("added")
        self.tl = Tiles(nc, k, s, d, self.added, direct)
        self.zin = s.sb("zin", [P, 4, J * D])
        self.loaded = [s.sem(f"z_loaded{i}") for i in range(4)]
        if target is not None:
            self.stored = [s.sem(f"res_stored{i}") for i in range(4)]
        self.relued = s.sem("relued")

    def load(self, sp, g, s):
        if past(g, 4):
            if self.target is None:
                sp.wait_ge(self.turned, g - 3)
            else:
                sp.wait_ge(self.stored[s], (g - s) * 4)
        sp.dma_start(self.zin[:, s, :], rows(self.z, g)).then_inc(self.loaded[s], 16)

    def add(self, dve, g, s):
        dve.wait_ge(self.loaded[s], (g - s) * 4 + 16)
        dve.wait_ge(self.tl.mean_done, g + 1)
        self.nc.vector.tensor_tensor(self.zin[:, s, :], self.tl.mean[:, s % 2, :], self.zin[:, s, :], ALU.add).then_inc(self.added, 1)

    def clip(self, act, g, s):
        act.wait_ge(self.added, g + 1)
        self.nc.scalar.activation(self.zin[:, s, :], self.zin[:, s, :], ACT.Relu).then_inc(self.relued, 1)

    def store(self, act, g, s):
        if self.relu:
            self.clip(act, g, s)
            act.wait_ge(self.relued, g + 1)
        else:
            act.wait_ge(self.added, g + 1)
        act.dma_start(rows(self.target, g), self.zin[:, s, :]).then_inc(self.stored[s], 16)

    def end(self, act):
        for s in range(4):
            act.wait_ge(self.stored[s], ((G - 1 - s) // 4 + 1) * 16)


def gather_edges_and_attributes(nc, k, so, table, own):
    with Scope(nc, "edges") as s:
        ck = Chunks(nc, k, s, 0, table, own=own)
        rk = Rank(nc, k, so, s, 1)
        with nc.Block() as block:

            @block.gpsimd
            def _(pool):
                by_group(pool, lambda g, s: ck.gather(pool, g, s))

            @block.tensor
            def _(t):
                def group(g, s):
                    back(rk.prefix, t, g, s, 0)
                    back(ck.sum_up, t, g, s, 1)
                rk.begin(t)
                by_group(t, group, 1)

            @block.scalar
            def _(act):
                def group(g, s):
                    ck.keep_added(act, g, s)
                    ck.keep_sums(act, g, s)
                by_group(act, group)

            @block.vector
            def _(dve):
                def group(g, s):
                    back(rk.one_hot, dve, g, s, 0)
                    back(rk.read, dve, g, s, 1)
                    back(ck.one_hot, dve, g, s, 1)
                    back(ck.add_own, dve, g, s, 1)
                rk.second_start(dve)
                by_group(dve, group, 1)
                rk.spots(dve)
                dve.wait_ge(ck.sums_kept, G)
                carry_over(nc, k, ck.d)


def gather_first(nc, k, layer, h_tab, z_tab, y_tab):
    with Scope(nc, "edges") as s:
        ck = Chunks(nc, k, s, 0, h_tab, weights=k.lin(0, layer))
        rt = Root(nc, k, s, layer, h_tab, z_tab, y_tab)
        with nc.Block() as block:

            @block.gpsimd
            def _(pool):
                by_group(pool, lambda g, s: ck.gather(pool, g, s))

            @block.tensor
            def _(t):
                def group(g, s):
                    back(ck.transform, t, g, s, 1)
                    back(ck.turn, t, g, s, 0)
                    back(rt.turn, t, g, s, 0)
                    back(ck.sum_up, t, g, s, 2)
                    back(rt.product, t, g, s, 0)
                by_group(t, group, 2)

            @block.scalar
            def _(act):
                def group(g, s):
                    back(ck.keep, act, g, s, 1)
                    back(ck.keep_rows, act, g, s, 0)
                    back(rt.keep, act, g, s, 0)
                    back(ck.keep_sums, act, g, s, 2)
                by_group(act, group, 2)

            @block.vector
            def _(dve):
                def group(g, s):
                    back(ck.one_hot, dve, g, s, 0)
                    back(rt.add, dve, g, s, 0)
                by_group(dve, group)

            @block.sync
            def _(sp):
                def group(g, s):
                    back(rt.load, sp, g, s, 0)
                    back(rt.store, sp, g, s, 2)
                by_group(sp, group, 2)
                rt.end(sp)


def gather_second(nc, k, layer, h_tab, z_tab, spill):
    with Scope(nc, "both") as s:
        ck = Chunks(nc, k, s, 1, h_tab, weights=k.lin(1, layer), spill=spill)
        cb = Combine(nc, k, s, 0, z_tab, z_tab, relu=False, direct=(0,))
        ps_warm = s.ps("warm", [P, 512])
        carried = s.sem("carried")
        with nc.Block() as block:

            @block.gpsimd
            def _(pool):
                by_group(pool, lambda g, s: ck.gather(pool, g, s))

            @block.tensor
            def _(t):
                def group(g, s):
                    if s == 0:
                        warm_up(nc, k, ps_warm, KEEP_WARM)
                    back(ck.sum_up, t, g, s, 2)
                    back(ck.transform, t, g, s, 1)
                    back(ck.turn, t, g, s, 0)
                    back(cb.tl.sum_tiles, t, g, s, 0)
                t.wait_ge(ck.landed[2], 16 * B)
                warm_up(nc, k, ps_warm)
                by_group(t, group, 2)

            @block.scalar
            def _(act):
                def group(g, s):
                    back(ck.keep_sums, act, g, s, 2)
                    back(ck.keep, act, g, s, 1)
                    back(ck.keep_rows, act, g, s, 0)
                    back(cb.tl.fetch_carried, act, g, s, 0)
                act.wait_ge(carried, 1)
                by_group(act, group, 2)

            @block.vector
            def _(dve):
                def group(g, s):
                    back(ck.one_hot, dve, g, s, 0)
                    back(cb.tl.one_hot, dve, g, s, 0)
                    back(lambda dve, g, s: cb.tl.fetch_first(dve, nc.vector.tensor_copy, g, s), dve, g, s, 0)
                    back(cb.tl.take_mean, dve, g, s, 1)
                    back(cb.add, dve, g, s, 1)
                carry_over(nc, k, 0).then_inc(carried, 1)
                by_group(dve, group, 1)

            @block.sync
            def _(sp):
                def group(g, s):
                    back(cb.load, sp, g, s, 0)
                    back(cb.store, sp, g, s, 2)
                    back(ck.spill_sums, sp, g, s, 3)
                by_group(sp, group, 3)
                cb.end(sp)
                all_stored(sp, ck.spilled)


def finish_layer(nc, k, z_tab, target, spill):
    with Scope(nc, "comb") as s:
        cb = Combine(nc, k, s, 1, z_tab, target, relu=True, direct=(0, 1))
        fetched = s.sem("fetched")
        carried = s.sem("carried")
        with nc.Block() as block:

            @block.sync
            def _(sp):
                sp.dma_start(k.carry[:, D:(C + 1) * D], spill[:, :]).then_inc(fetched, 16)
                by_group(sp, lambda g, s: cb.load(sp, g, s))

            @block.tensor
            def _(t):
                by_group(t, lambda g, s: cb.tl.sum_tiles(t, g, s))

            @block.vector
            def _(dve):
                def group(g, s):
                    back(cb.tl.one_hot, dve, g, s, 0)
                    back(cb.tl.take_mean, dve, g, s, 1)
                    back(cb.add, dve, g, s, 1)
                dve.wait_ge(fetched, 16)
                carry_over(nc, k, 1).then_inc(carried, 1)
                by_group(dve, group, 1)

            @block.scalar
            def _(act):
                def group(g, s):
                    back(cb.tl.fetch_carried, act, g, s, 0)
                    back(cb.store, act, g, s, 2)
                act.wait_ge(carried, 1)
                by_group(act, group, 2)
                cb.end(act)


class Turn:

    def __init__(self, nc, k, s, slots=2, name="turn"):
        self.nc, self.k, self.slots = nc, k, slots
        self.ps = [s.ps(f"{name}{i}", [P, 512]) for i in range(2)]
        self.sb = s.sb(f"{name}_sb", [D, slots, J * P])
        self.turned = s.sem(f"{name}_turned")
        self.kept = s.sem(f"{name}_kept")
        self.passed = s.sem(f"{name}_passed")

    def turn(self, t, g, s, x):
        if past(g, 1):
            wait_apart(t, self.kept, 2 * g, self.passed)
        for j in range(J):
            last = self.nc.tensor.transpose(self.ps[j // 4][0:D, (j % 4) * P:(j % 4 + 1) * P], x[:, j * D:(j + 1) * D], self.k.ident[:, :])
            if j % 4 == 3:
                last.then_inc(self.turned, 1)

    def keep(self, act, g, s):
        for h in range(2):
            act.wait_ge(self.turned, 2 * g + h + 1)
            self.nc.scalar.copy(self.sb[:, s % self.slots, h * 512:(h + 1) * 512], self.ps[h][0:D, :]).then_inc(self.kept, 1)


class PairTurn:

    def __init__(self, nc, k, s, slots):
        self.nc, self.k, self.slots = nc, k, slots
        self.ps = s.ps("pairs", [P, 512])
        self.sb = s.sb("pairs_sb", [P, slots, H * P])
        self.turned = s.sem("pairs_turned")
        self.kept = s.sem("pairs_kept")
        self.passed = s.sem("pairs_passed")

    def turn(self, t, g, s, x):
        if past(g, 1):
            wait_apart(t, self.kept, g, self.passed)
        for q in range(H):
            last = self.nc.tensor.transpose(self.ps[:, q * P:(q + 1) * P], x[:, 2 * q * D:2 * (q + 1) * D], self.k.ident[:, :])
        last.then_inc(self.turned, 1)

    def keep(self, act, g, s):
        act.wait_ge(self.turned, g + 1)
        self.nc.scalar.copy(self.sb[:, s % self.slots, :], self.ps[:, :]).then_inc(self.kept, 1)


class Root:

    def __init__(self, nc, k, s, layer, h_tab, z_tab, y_tab, out=None):
        self.nc, self.k, self.layer, self.h_tab, self.z_tab, self.y_tab, self.out = nc, k, layer, h_tab, z_tab, y_tab, out
        self.ends = layer == LAYERS
        self.W = D if self.ends else 2 * D
        self.tn = PairTurn(nc, k, s, slots=2 if self.ends else 1)
        self.y = s.sb("y", [P, 4, J * D])
        self.ps = [s.ps(f"w{i}", [P, 512]) for i in range(2)]
        if not self.ends:
            self.hin = s.sb("hin", [P, 2, J * D])
            self.h_loaded = [s.sem(f"h_loaded{i}") for i in range(2)]
            self.z = s.sb("z", [P, 2, J * D])
            self.z_stored = [s.sem(f"z_stored{i}") for i in range(2)]
        self.y_loaded = [s.sem(f"y_loaded{i}") for i in range(4)]
        self.y_stored = [s.sem(f"y_stored{i}") for i in range(4)]
        self.product_done = s.sem("product_done")
        self.half_added = s.sem("half_added")
        self.seen = s.sem("root_seen")

    def load(self, sp, g, s):
        if past(g, 2):
            sp.wait_ge(self.tn.turned, g - 1)
        sp.dma_start(self.hin[:, s % 2, :], rows(self.h_tab, g)).then_inc(self.h_loaded[s % 2], 16)
        self.load_y(sp, g, s)

    def load_y(self, sp, g, s):
        if past(g, 4):
            sp.wait_ge(self.y_stored[s], (g - s) * 4)
        sp.dma_start(self.y[:, s, :], rows(self.y_tab, g)).then_inc(self.y_loaded[s], 16)

    def turn(self, t, g, s):
        wait_apart(t, self.h_loaded[s % 2], uses(g, s), self.seen)
        self.tn.turn(t, g, s, self.hin[:, s % 2, :])

    def keep(self, act, g, s):
        if past(g, self.tn.slots):
            act.wait_ge(self.product_done, 2 * (g - self.tn.slots) + 2)
        self.tn.keep(act, g, s)

    def product(self, t, g, s):
        t.wait_ge(self.tn.kept, g + 1)
        for h in range(2):
            if past(g, 1):
                t.wait_ge(self.half_added, 2 * g + h - 1)
            for q in range(2):
                last = self.nc.tensor.matmul(self.ps[h][:, 2 * q * self.W:2 * (q + 1) * self.W], self.tn.sb[:, s % self.tn.slots, (2 * h + q) * P:(2 * h + q + 1) * P], self.k.root(self.layer), start=True, stop=True)
            last.then_inc(self.product_done, 1)

    def add(self, dve, g, s):
        dve.wait_ge(self.y_loaded[s], (g - s) * 4 + 16)
        if past(g, 2) and not self.ends:
            dve.wait_ge(self.z_stored[s % 2], uses(g, s) - 16)
        for h in range(2):
            dve.wait_ge(self.product_done, 2 * g + h + 1)
            v = self.ps[h][:, 0:4 * self.W].rearrange("p (j w) -> p j w", j=4)
            c = slice(h * 4 * D, (h + 1) * 4 * D)
            if not self.ends:
                self.nc.vector.tensor_tensor(tiles(self.z[:, s % 2, c]), v[:, :, D:2 * D], self.k.root_b[:, self.layer, :].unsqueeze(1).to_broadcast([P, 4, D]), ALU.add)
            self.nc.vector.tensor_tensor(tiles(self.y[:, s, c]), v[:, :, 0:D], tiles(self.y[:, s, c]), ALU.add).then_inc(self.half_added, 1)

    def store(self, sp, g, s):
        sp.wait_ge(self.half_added, 2 * g + 2)
        if self.ends:
            sp.dma_start(outer_rows(self.nc, self.out, g), self.y[0:lanes(g), s, :]).then_inc(self.y_stored[s], 16)
        else:
            sp.dma_start(rows(self.y_tab, g), self.y[:, s, :]).then_inc(self.y_stored[s], 16)
            sp.dma_start(rows(self.z_tab, g), self.z[:, s % 2, :]).then_inc(self.z_stored[s % 2], 16)

    def end(self, sp):
        for s in range(4):
            sp.wait_ge(self.y_stored[s], ((G - 1 - s) // 4 + 1) * 16)
        if not self.ends:
            all_stored(sp, self.z_stored)


def finish_last(nc, k, z_tab, y_tab, out, spill):
    with Scope(nc, "last") as s:
        cb = Combine(nc, k, s, 1, z_tab, None, relu=True, direct=(0, 1))
        rt = Root(nc, k, s, LAYERS, None, None, y_tab, out)
        cb.turned = rt.tn.turned
        ps_warm = s.ps("warm", [P, 512])
        seen = s.sem("relued_seen")
        fetched = s.sem("fetched")
        carried = s.sem("carried")
        with nc.Block() as block:

            @block.sync
            def _(sp):
                def group(g, s):
                    back(cb.load, sp, g, s, 0)
                    back(rt.load_y, sp, g, s, 4)
                    back(rt.store, sp, g, s, 7)
                sp.dma_start(k.carry[:, D:(C + 1) * D], spill[:, :]).then_inc(fetched, 16)
                by_group(sp, group, 7)
                rt.end(sp)

            @block.tensor
            def _(t):
                def turn(t, g, s):
                    wait_apart(t, cb.relued, g + 1, seen)
                    rt.tn.turn(t, g, s, cb.zin[:, s, :])

                def group(g, s):
                    if not past(g, 8) and past(g, 7):
                        warm_up(nc, k, ps_warm)
                    back(cb.tl.sum_tiles, t, g, s, 0)
                    back(rt.product, t, g, s, 5)
                    back(turn, t, g, s, 3)
                by_group(t, group, 5)

            @block.vector
            def _(dve):
                def group(g, s):
                    back(rt.add, dve, g, s, 6)
                    back(cb.tl.one_hot, dve, g, s, 0)
                    back(cb.tl.take_mean, dve, g, s, 1)
                    back(cb.add, dve, g, s, 1)
                dve.wait_ge(fetched, 16)
                carry_over(nc, k, 1).then_inc(carried, 1)
                by_group(dve, group, 6)

            @block.scalar
            def _(act):
                def group(g, s):
                    back(rt.keep, act, g, s, 4)
                    back(cb.tl.fetch_carried, act, g, s, 0)
                    back(cb.clip, act, g, s, 2)
                act.wait_ge(carried, 1)
                by_group(act, group, 4)


def mix_nodes(nc, k, so, own, z_t):
    with Scope(nc, "mix") as s:
        mixed = s.sem("mixed")
        tl = Tiles(nc, k, s, 0, used=mixed, direct=(0,), msg=own.rearrange("p c w -> p (c w)"), offs=so.offs)
        tn = Turn(nc, k, s)
        hin = s.sb("hin", [P, 2, J * D])
        hp = s.sb("hp", [P, 2, J * D])
        stats = s.sb("stats", [P, 2 * (G - 1) + 8, 6])
        moments = s.sb("moments", [P, 4])
        ps_z = [s.ps(f"z{i}", [P, 512]) for i in range(2)]
        loaded = [s.sem(f"loaded{i}") for i in range(2)]
        stored = [s.sem(f"stored{i}") for i in range(2)]
        made = s.sem("made")
        counted = s.sem("counted")
        stats_done = s.sem("stats_done")
        rooted = s.sem("rooted")
        with nc.Block() as block:

            @block.sync
            def _(sp):
                def load(g, s):
                    if past(g, 2):
                        sp.wait_ge(mixed, g - 1)
                    sp.dma_start(hin[:, s % 2, :], rows(k.tab[0], g)).then_inc(loaded[s % 2], 16)
                by_group(sp, load)

            @block.tensor
            def _(t):
                def turn(t, g, s):
                    t.wait_ge(mixed, g + 1)
                    tn.turn(t, g, s, hp[:, s % 2, :])

                def product(t, g, s):
                    for h in range(2):
                        t.wait_ge(tn.kept, 2 * g + h + 1)
                        if past(g, 1):
                            t.wait_ge(counted, 2 * g + h - 1)
                        nc.tensor.matmul(ps_z[h][:, :], k.w1[:, :], tn.sb[:, s % 2, h * 512:(h + 1) * 512], start=True, stop=True).then_inc(made, 1)

                def group(g, s):
                    back(tl.sum_tiles, t, g, s, 0)
                    back(product, t, g, s, 2)
                    back(turn, t, g, s, 1)
                by_group(t, group, 2)

            @block.scalar
            def _(act):
                def store(act, g, s):
                    if past(g, 2):
                        act.wait_ge(stored[s % 2], uses(g, s) - 16)
                        act.wait_ge(made, 2 * g - 2)
                    tn.keep(act, g, s)
                    act.wait_ge(tn.kept, 2 * g + 2)
                    act.dma_start(z_t[bass.ds(g, 1), :, :].rearrange("a f n -> (a f) n"), tn.sb[:, s % 2, :]).then_inc(stored[s % 2], 16)

                def group(g, s):
                    back(tl.fetch_carried, act, g, s, 0)
                    back(store, act, g, s, 2)
                by_group(act, group, 2)
                root_of_variance(nc, act, k, moments, stats_done, rooted, P)
                all_stored(act, stored)

            @block.gpsimd
            def _(pool):
                by_group(pool, lambda g, s: tl.fetch_first(pool, nc.gpsimd.tensor_copy, g, s))

            @block.vector
            def _(dve):
                def mix(dve, g, s):
                    dve.wait_ge(loaded[s % 2], uses(g, s))
                    dve.wait_ge(tl.mean_done, g + 1)
                    if past(g, 2):
                        dve.wait_ge(tn.turned, 2 * g - 2)
                    nc.vector.scalar_tensor_tensor(out=hp[:, s % 2, :], in0=hin[:, s % 2, :], scalar=k.one_eps[:, 0:1], in1=tl.mean[:, s % 2, :], op0=ALU.mult, op1=ALU.add).then_inc(mixed, 1)

                def group(g, s):
                    back(tl.one_hot, dve, g, s, 0)
                    back(tl.take_mean, dve, g, s, 1)
                    back(lambda dve, g, s: statistics(nc, dve, g, ps_z, made, counted, stats, P), dve, g, s, 3)
                    back(mix, dve, g, s, 1)
                by_group(dve, group, 3)
                aggregate(nc, dve, k, stats, moments, counted, stats_done, rooted, P, k.b1, k.gamma1, k.beta1, k.scale1, k.shift1)


def statistics(nc, dve, g, ps, made, counted, stats, parts):
    last_group = isinstance(g, int) and g == G - 1
    for h in range(2):
        dve.wait_ge(made, 2 * g + h + 1)
        if last_group:
            for j in range(4):
                last = nc.vector.bn_stats(stats[0:parts, 2 * (G - 1) + h * 4 + j, :], ps[h][0:parts, j * P:j * P + LAST])
        else:
            last = nc.vector.bn_stats(stats[0:parts, bass.ds(2 * g + h, 1), :].rearrange("p a b -> p (a b)"), ps[h][0:parts, :])
        last.then_inc(counted, 1)


def aggregate(nc, dve, k, stats, moments, counted, done, rooted, parts, bias, gamma, beta, scale, shift):
    m = moments[0:parts, :]
    ch = Chain(dve, done)
    dve.wait_ge(counted, 2 * G)
    ch.link(nc.vector.bn_aggr(m[:, 0:2], stats[0:parts, :, :].rearrange("p a b -> p (a b)")))
    dve.wait_ge(rooted, 1)
    ch.link(nc.vector.reciprocal(m[:, 2:3], m[:, 2:3]))
    ch.link(nc.vector.tensor_tensor(scale[:, :], m[:, 2:3], gamma[:, :], ALU.mult))
    ch.link(nc.vector.tensor_tensor(m[:, 3:4], m[:, 0:1], bias[:, :], ALU.add))
    ch.link(nc.vector.tensor_tensor(m[:, 3:4], bias[:, :], m[:, 3:4], ALU.subtract))
    nc.vector.scalar_tensor_tensor(out=shift[:, :], in0=m[:, 3:4], scalar=scale[:, 0:1], in1=beta[:, :], op0=ALU.mult, op1=ALU.add).then_inc(done, 1)


def root_of_variance(nc, act, k, moments, done, rooted, parts):
    act.wait_ge(done, 1)
    nc.scalar.activation(moments[0:parts, 2:3], moments[0:parts, 1:2], ACT.Sqrt, bias=k.eps[0:parts, 0:1]).then_inc(rooted, 1)


def second_product(nc, k, z_t):
    with Scope(nc, "prod") as s:
        hp = s.sb("hp", [D, 4, J * P])
        a1 = s.sb("a1", [P, 2, J * P])
        z2 = s.sb("z2", [D, 2, J * P])
        ps_a = [s.ps(f"a{i}", [P, 512]) for i in range(4)]
        stats = s.sb("stats", [P, 2 * (G - 1) + 8, 6])
        moments = s.sb("moments", [P, 4])
        ps_z = [s.ps(f"z{i}", [P, 512]) for i in range(4)]
        loaded = [s.sem(f"loaded{i}") for i in range(4)]
        stored = [s.sem(f"stored{i}") for i in range(2)]
        first_done = s.sem("first_done")
        relued = s.sem("relued")
        made = s.sem("made")
        copied = s.sem("copied")
        counted = s.sem("counted")
        done = s.sem("done")
        rooted = s.sem("rooted")

        def at(g):
            return z_t[bass.ds(g, 1), :, :].rearrange("a f n -> (a f) n")
        with nc.Block() as block:

            @block.sync
            def _(sp):
                def load(sp, g, s):
                    if past(g, 4):
                        sp.wait_ge(first_done, 2 * g - 6)
                    sp.dma_start(hp[:, s, :], at(g)).then_inc(loaded[s], 16)

                def store(sp, g, s):
                    sp.wait_ge(copied, 2 * g + 2)
                    sp.dma_start(at(g), z2[:, s % 2, :]).then_inc(stored[s % 2], 16)

                def group(g, s):
                    back(load, sp, g, s, 0)
                    back(store, sp, g, s, 4)
                by_group(sp, group, 4)
                all_stored(sp, stored)

            @block.tensor
            def _(t):
                def early(t, g, s):
                    t.wait_ge(loaded[s], (g - s) * 4 + 16)
                    for h in range(2):
                        if past(g, 2):
                            t.wait_ge(relued, 2 * g + h - 3)
                        nc.tensor.matmul(ps_a[2 * (s % 2) + h][:, :], k.w1[:, :], hp[:, s, h * 512:(h + 1) * 512], start=True, stop=True).then_inc(first_done, 1)

                def late(t, g, s):
                    for h in range(2):
                        t.wait_ge(relued, 2 * g + h + 1)
                        if past(g, 2):
                            t.wait_ge(copied, 2 * g + h - 3)
                        nc.tensor.matmul(ps_z[2 * (s % 2) + h][0:D, :], k.w2[:, :], a1[:, s % 2, h * 512:(h + 1) * 512], start=True, stop=True).then_inc(made, 1)

                def group(g, s):
                    back(early, t, g, s, 0)
                    back(late, t, g, s, 1)
                t.wait_ge(loaded[2], 16)
                warm_up(nc, k, ps_z[1])
                by_group(t, group, 1)

            @block.scalar
            def _(act):
                def group(g, s):
                    for h in range(2):
                        act.wait_ge(first_done, 2 * g + h + 1)
                        if past(g, 2):
                            act.wait_ge(made, 2 * g + h - 3)
                        nc.scalar.activation(a1[:, s % 2, h * 512:(h + 1) * 512], ps_a[2 * (s % 2) + h][:, :], ACT.Relu, bias=k.shift1[:, 0:1], scale=k.scale1[:, 0:1]).then_inc(relued, 1)
                by_group(act, group)
                root_of_variance(nc, act, k, moments, done, rooted, D)

            @block.vector
            def _(dve):
                def group(g, s):
                    if past(g, 2):
                        dve.wait_ge(stored[s % 2], uses(g, s) - 16)
                    statistics(nc, dve, g, ps_z[2 * (s % 2):2 * (s % 2) + 2], made, counted, stats, D)
                    for h in range(2):
                        nc.vector.tensor_copy(z2[:, s % 2, h * 512:(h + 1) * 512], ps_z[2 * (s % 2) + h][0:D, :]).then_inc(copied, 1)
                by_group(dve, group)
                aggregate(nc, dve, k, stats, moments, counted, done, rooted, D, k.b2, k.gamma2, k.beta2, k.scale2, k.shift2)


def finish_first(nc, k, so, x, z_t, y_tab, h_tab):
    with Scope(nc, "fin") as s:
        z = s.sb("z", [D, 4, J * P])
        r = s.sb("r", [D, 2, J * P])
        xin = s.sb("xin", [P, 4, J * D])
        x1 = s.sb("x1", [P, 2, J * D])
        y = s.sb("y", [P, 2, J * D])
        ps_b = [s.ps(f"b{i}", [P, 512]) for i in range(2)]
        z_loaded = [s.sem(f"z_loaded{i}") for i in range(4)]
        x_loaded = [s.sem(f"x_loaded{i}") for i in range(4)]
        h_stored = [s.sem(f"h_stored{i}") for i in range(2)]
        y_stored = [s.sem(f"y_stored{i}") for i in range(2)]
        relued = s.sem("relued")
        back_done = s.sem("back_done")
        passed = s.sem("passed")
        added = s.sem("added")
        y_done = s.sem("y_done")
        nm = Norm(nc, k, s, h_stored)
        sc = Scatter(nc, so, s, 1)
        with nc.Block() as block:

            @block.sync
            def _(sp):
                def load(sp, g, s):
                    if past(g, 4):
                        sp.wait_ge(relued, g - 3)
                    sp.dma_start(z[:, s, :], z_t[bass.ds(g, 1), :, :].rearrange("a f n -> (a f) n")).then_inc(z_loaded[s], 16)
                    if past(g, 4):
                        sp.wait_ge(added, g - 3)
                    sp.dma_start(xin[0:lanes(g), s, :], outer_rows(nc, x, g)).then_inc(x_loaded[s], 16)

                def store(sp, g, s):
                    sp.wait_ge(y_done, g + 1)
                    sp.dma_start(rows(y_tab, g), y[:, s % 2, :]).then_inc(y_stored[s % 2], 16)

                def store_h(sp, g, s):
                    sp.wait_ge(nm.h_done, g + 1)
                    sp.dma_start(rows(h_tab, g), nm.h[:, s % 2].rearrange("p j d -> p (j d)")).then_inc(h_stored[s % 2], 16)

                def group(g, s):
                    back(load, sp, g, s, 0)
                    back(store, sp, g, s, 3)
                    back(store_h, sp, g, s, 6)
                by_group(sp, group, 6)
                all_stored(sp, h_stored)
                all_stored(sp, y_stored)

            @block.scalar
            def _(act):
                def relu(act, g, s):
                    act.wait_ge(z_loaded[s], (g - s) * 4 + 16)
                    if past(g, 2):
                        act.wait_ge(back_done, g - 1)
                    nc.scalar.activation(r[:, s % 2, :], z[:, s, :], ACT.Relu, bias=k.shift2[:, 0:1], scale=k.scale2[:, 0:1]).then_inc(relued, 1)

                def group(g, s):
                    back(relu, act, g, s, 0)
                    back(nm.square, act, g, s, 2)
                    back(nm.deviation, act, g, s, 4)
                by_group(act, group, 4)

            @block.tensor
            def _(t):
                def group(g, s):
                    if past(g, 2):
                        t.wait_ge(added, g - 1)
                    wait_apart(t, relued, g + 1, passed)
                    for j in range(J):
                        last = nc.tensor.transpose(ps_b[s % 2][:, j * D:(j + 1) * D], r[:, s % 2, j * P:(j + 1) * P], k.ident[0:D, 0:D])
                    last.then_inc(back_done, 1)
                by_group(t, group)

            @block.vector
            def _(dve):
                def add(dve, g, s):
                    dve.wait_ge(back_done, g + 1)
                    dve.wait_ge(x_loaded[s], (g - s) * 4 + 16)
                    if past(g, 2):
                        dve.wait_ge(y_done, g - 1)
                        dve.wait_ge(nm.cent_done, g - 1)
                    nc.vector.tensor_tensor(x1[:, s % 2, :], xin[:, s, :], ps_b[s % 2][:, :], ALU.add).then_inc(added, 1)

                def normal(dve, g, s):
                    dve.wait_ge(added, g + 1)
                    nm.add_up(dve, g, s, tiles(x1[:, s % 2, :]))
                    if past(g, 2):
                        dve.wait_ge(y_stored[s % 2], uses(g, s) - 16)
                    nc.vector.tensor_tensor(tiles(y[:, s % 2, :]), tiles(x1[:, s % 2, :]), k.final_b[:, :].unsqueeze(1).to_broadcast([P, J, D]), ALU.add).then_inc(y_done, 1)
                    nm.center(dve, g, s, tiles(x1[:, s % 2, :]))

                def group(g, s):
                    back(nm.scale, dve, g, s, 5)
                    back(add, dve, g, s, 0)
                    back(nm.variance, dve, g, s, 3)
                    back(normal, dve, g, s, 1)
                by_group(dve, group, 5)

            @block.gpsimd
            def _(pool):
                by_group(pool, lambda g, s: sc.scatter(pool, g, s))
                sc.end(pool)


def load_parameters(nc, k, a):
    with Scope(nc, "par") as s:
        wn = s.sb("wn", [D, 13, 2, D])
        ps = [s.ps(f"turned{i}", [P, 512]) for i in range(2)]
        loaded = s.sem("loaded")
        turned = s.sem("turned")
        zeroed = s.sem("zeroed")
        n = [0]
        col = lambda v: v.rearrange("(p o) -> p o", o=1)
        row = lambda v, cnt: v.rearrange("(o n) -> o n", o=1).to_broadcast([P, cnt])
        with nc.Block() as block:

            @block.sync
            def _(sp):
                def load(to, of):
                    n[0] += 1
                    sp.dma_start(to, of).then_inc(loaded, 16)
                for twice in range(2):
                    for i, w in enumerate(("root_w", "lin1_w", "lin2_w")):
                        load(wn[:, 3 * i:3 * i + 3, twice, :], a["L1_gnn_" + w].rearrange("l o i -> o l i"))
                    load(wn[:, 9:13, twice, :], a["L1_gnn_final_w"].rearrange("o (l i) -> o l i", l=4))
                load(k.w1[:, :], a["L0_gnn_W1"])
                load(k.w2[:, :], a["L0_gnn_W2"])
                for to, of in ((k.b1, "b1"), (k.gamma1, "gamma1"), (k.beta1, "beta1"), (k.b2, "b2"), (k.gamma2, "gamma2"), (k.beta2, "beta2")):
                    load(to[:, :], col(a["L0_gnn_" + of]))
                load(k.one_eps[:, :], row(a["L0_gnn_eps"], 1))
                load(k.final_b[:, :], row(a["L1_gnn_final_b"], D))
                for l in range(LAYERS):
                    load(k.root_b[:, l, :], a["L1_gnn_root_b"][l:l + 1, :].to_broadcast([P, D]))
                assert n[0] == PARAMETER_LOADS
                sp.wait_ge(loaded, 16 * PARAMETER_LOADS)

            @block.tensor
            def _(t):
                t.wait_ge(loaded, 16 * PARAMETER_LOADS)
                for i in range(13):
                    last = nc.tensor.transpose(ps[i // 8][:, (i % 8) * D:(i % 8 + 1) * D], wn[:, i, :, :].rearrange("p a d -> p (a d)"), k.ident[0:D, 0:D])
                last.then_inc(turned, 1)

            @block.vector
            def _(dve):
                nc.vector.memset(k.wt[:, :], 0.0).then_inc(zeroed, 1)
                dve.wait_ge(zeroed, 1)
                dve.wait_ge(turned, 1)

                def put(to, i, pair):
                    lanes_of = slice(pair * D, (pair + 1) * D)
                    nc.vector.tensor_copy(to[lanes_of, :], ps[i // 8][lanes_of, (i % 8) * D:(i % 8 + 1) * D])
                for pair in range(2):
                    for l in range(LAYERS):
                        put(k.root(l)[:, 2 * pair * D:(2 * pair + 1) * D], 9 + l, pair)
                        put(k.root(l)[:, (2 * pair + 1) * D:(2 * pair + 2) * D], l, pair)
                        for d in range(2):
                            put(k.lin(d, l)[:, pair * D:(pair + 1) * D], 3 + 3 * d + l, pair)
                    put(k.root(LAYERS)[:, pair * D:(pair + 1) * D], 9 + LAYERS, pair)
                nc.vector.memset(k.eps[:, :], EPS)
                nc.vector.tensor_scalar(k.one_eps[:, :], k.one_eps[:, :], 1.0, None, ALU.add)


class Kept:

    def __init__(self, s):
        self.lanes = s.sb("lanes", [P, P])
        self.iotap = s.sb("iotap", [P, 1])
        self.ident = s.sb("ident", [P, P])
        self.inv = s.sb("inv", [P, 2, T])
        self.other = s.sb("other", [P, 2, C], I32)
        self.pa = s.sb("pa", [P, 2, T])
        self.pb = s.sb("pb", [P, 2, C])
        self.keep = s.sb("keep", [P, 2, C])
        self.offs = s.sb("offs", [1, 2, 2, T], I32)
        self.wt = s.sb("wt", [P, LAYERS * 4 * D + 2 * D + 2 * LAYERS * 2 * D])
        self.final_b = s.sb("final_b", [P, D])
        self.root_b = s.sb("root_b", [P, LAYERS, D])
        self.eps = s.sb("eps", [P, 1])

    def keep_first(self, s):
        self.w1 = s.sb("w1", [D, 2 * D])
        self.w2 = s.sb("w2", [2 * D, D])
        self.b1, self.gamma1, self.beta1, self.scale1, self.shift1 = (
            s.sb(name, [2 * D, 1]) for name in ("b1", "gamma1", "beta1", "scale1", "shift1"))
        self.b2, self.gamma2, self.beta2, self.scale2, self.shift2 = (
            s.sb(name, [D, 1]) for name in ("b2", "gamma2", "beta2", "scale2", "shift2"))
        self.one_eps = s.sb("one_eps", [P, 1])

    def root(self, layer):
        at = layer * 4 * D
        return self.wt[:, at:at + (2 * D if layer == LAYERS else 4 * D)]

    def lin(self, d, layer):
        at = LAYERS * 4 * D + 2 * D + (LAYERS * d + layer) * 2 * D
        return self.wt[:, at:at + 2 * D]


def build(nc, a, out):
    with Scope(nc, "kept") as s:
        k = Kept(s)
        k.tab = [nc.dram_tensor(f"tab{i}", (NP, D), F32, kind="Internal").ap() for i in range(2)]
        z_tab = nc.dram_tensor("z_tab", (NP, D), F32, kind="Internal").ap()
        y_tab = nc.dram_tensor("y_tab", (NP, D), F32, kind="Internal").ap()
        spill = nc.dram_tensor("spill", (P, C * D), F32, kind="Internal").ap()
        z_t = nc.dram_tensor("z_t", (G, D, J * P), F32, kind="Internal").ap()
        with Scope(nc, "early") as e:
            so = Sorting(nc, e)
            k.keep_first(e)
            with Scope(nc, "attr") as m:
                so.attr = m.sb("attr", [P, C, D])
                rank_first(nc, k, so, a["src"], a["dst"], a["edge_attr_64"])
                load_parameters(nc, k, a)
                normalise_input(nc, k, so, a["x"], k.tab[0])
            with Scope(nc, "msg") as m:
                own = m.sb("own", [P, C, W_ROW])
                k.carry = m.sb("carry", [P, (C + 1) * D])
                sorted_tables(nc, k, so, 0, own)
                gather_edges_and_attributes(nc, k, so, k.tab[0], own)
                mix_nodes(nc, k, so, own, z_t)
            second_product(nc, k, z_t)
            finish_first(nc, k, so, a["x"], z_t, y_tab, k.tab[1])
            with Scope(nc, "rows") as m:
                sorted_tables(nc, k, so, 1, m.sb("rows_of", [P, C, 4]))
        with Scope(nc, "msgs") as m:
            k.msg = [m.sb(f"of{d}", [P, C * D]) for d in range(2)]
            k.carry = m.sb("carry", [P, (C + 1) * D])
            for l in range(LAYERS):
                h_in, h_out = k.tab[(l + 1) % 2], k.tab[l % 2]
                gather_first(nc, k, l, h_in, z_tab, y_tab)
                gather_second(nc, k, l, h_in, z_tab, spill)
                if l < LAYERS - 1:
                    finish_layer(nc, k, z_tab, h_out, spill)
                else:
                    finish_last(nc, k, z_tab, y_tab, out, spill)


_INS = ["x", "src", "dst", "edge_attr_64", "L0_gnn_eps", "L0_gnn_W1", "L0_gnn_b1", "L0_gnn_gamma1", "L0_gnn_beta1",
        "L0_gnn_W2", "L0_gnn_b2", "L0_gnn_gamma2", "L0_gnn_beta2", "L1_gnn_lin1_w", "L1_gnn_lin2_w", "L1_gnn_root_w",
        "L1_gnn_root_b", "L1_gnn_final_w", "L1_gnn_final_b"]


def kernel(**inputs):
    import numpy as np
    import concourse.bacc as bacc
    from concourse.bass_utils import run_bass_kernel_spmd

    nc = bacc.Bacc("TRN2", target_bir_lowering=False, num_devices=1)
    arrays, args = {}, {}
    for name in _INS:
        v = np.ascontiguousarray(inputs[name])
        arrays[f"in_{name}"] = v
        args[name] = nc.dram_tensor(f"in_{name}", v.shape, mybir.dt.from_np(v.dtype), kind="ExternalInput").ap()
    out = nc.dram_tensor("out", (N, D), F32, kind="ExternalOutput").ap()
    build(nc, args, out)
    return run_bass_kernel_spmd(nc, [arrays], core_ids=[0]).results[0]["out"]
```
